# Optimizing a Trainium2 kernel written in Bass

```python
import numpy as np
import jax
import jax.numpy as jnp

def _softmax(x, axis=-1):
    return jax.nn.softmax(x, axis=axis)

def _gelu(x):
    return jax.nn.gelu(x, approximate=True)

def _silu(x):
    return jax.nn.silu(x)

def _sigmoid(x):
    return jax.nn.sigmoid(x)

def _layernorm(x, axis=-1, eps=1e-05):
    m = jnp.mean(x, axis=axis, keepdims=True)
    v = jnp.var(x, axis=axis, keepdims=True)
    return (x - m) / jnp.sqrt(v + eps)

def _scatter_add(tgt, idx, src, axis=0):
    return tgt.at[idx].add(src)

def _segment_sum(src, seg, n):
    return jax.ops.segment_sum(src, seg, n)
kernel_name = 'mk_gnn_ffn_d1_gnn_r32_b3fc09'

def setup_inputs(seed: int=0):
    np.random.seed(seed)
    _w = jnp.asarray

    def _rec_inputs():
        import jax
        import jax.numpy as jnp
        _gk = jax.random.key(seed)
        x = -0.0001394 + 0.9999 * jax.random.normal(jax.random.fold_in(_gk, 1), (10000, 768), jnp.float32)
        src = jax.random.randint(jax.random.fold_in(_gk, 2), (10000,), 0, 10000, jnp.int32)
        dst = jnp.minimum((10000 * jax.random.uniform(jax.random.fold_in(_gk, 3), (10000,)) ** 2.0).astype(jnp.int32), 9999)
        _o = jnp.argsort(dst, stable=True)
        src = src[_o]
        dst = dst[_o]
        return (x, src, dst)
    x, src, dst = _rec_inputs()

    def _L0_gnn_setup():
        import jax, jax.numpy as jnp
        import numpy as np
        N = 50000
        E = 250000
        H = 12
        D = 64
        NEG_SLOPE = 0.2
        key = jax.random.key(seed)
        k1, k2, k3, k4, k5, k6, k7 = jax.random.split(key, 7)
        h = jax.random.normal(k1, (N, H * D), dtype=jnp.float32)
        src = jnp.concatenate([jnp.arange(N, dtype=jnp.int32), jax.random.randint(k2, (E - N,), 0, N, dtype=jnp.int32)])
        dst = jnp.concatenate([jnp.arange(N, dtype=jnp.int32), jax.random.randint(k3, (E - N,), 0, N, dtype=jnp.int32)])
        xav = 1.414 / np.sqrt(D)
        W_fc = jax.random.normal(k4, (D, D), dtype=jnp.float32) * xav
        attn_l = jax.random.normal(k5, (H, D), dtype=jnp.float32) * 0.15
        attn_r = jax.random.normal(k6, (H, D), dtype=jnp.float32) * 0.15
        W_res = jax.random.normal(k7, (D, D), dtype=jnp.float32) * xav
        return {'h': h, 'W_fc': W_fc, 'attn_l': attn_l, 'attn_r': attn_r, 'W_res': W_res, 'src': src, 'dst': dst}
    _L0_gnn_all = _L0_gnn_setup()
    _L0_gnn_in = {k: v for k, v in _L0_gnn_all.items() if k in ('W_fc', 'attn_l', 'attn_r', 'W_res')}
    del _L0_gnn_all

    def _L0_ffn_setup():
        import jax, jax.numpy as jnp
        import numpy as np
        EPS_NORM = 1e-05
        RMS_EPS = 1e-05

        def _l2_normalize(v):
            n = jnp.sqrt(jnp.sum(v * v, axis=-1, keepdims=True))
            return v / jnp.maximum(n, EPS_NORM)

        def _rms_norm(x, weight, eps):
            ms = jnp.mean(x * x, axis=-1, keepdims=True)
            return x * jax.lax.rsqrt(ms + eps) * weight
        key = jax.random.key(seed)
        ks = jax.random.split(key, 6)
        B, T, D = (8, 128, 768)
        S, F = (64, 96)
        x = jax.random.normal(ks[0], (B, T, D), dtype=jnp.float32)
        slots = 0.02 * jax.random.normal(ks[1], (S, D), dtype=jnp.float32)
        scale = jnp.ones((S,), dtype=jnp.float32)
        fc1_weight = 0.02 * jax.random.normal(ks[2], (S, D, F), dtype=jnp.float32)
        fc1_bias = jnp.zeros((S, F), dtype=jnp.float32)
        fc2_weight = 0.02 * jax.random.normal(ks[3], (S, F, D), dtype=jnp.float32)
        fc2_bias = jnp.zeros((S, D), dtype=jnp.float32)
        norm_weight = jnp.ones((D,), dtype=jnp.float32)
        return {'x': x, 'slots': slots, 'scale': scale, 'fc1_weight': fc1_weight, 'fc1_bias': fc1_bias, 'fc2_weight': fc2_weight, 'fc2_bias': fc2_bias, 'norm_weight': norm_weight}
    _L0_ffn_all = _L0_ffn_setup()
    _L0_ffn_in = {k: v for k, v in _L0_ffn_all.items() if k in ('slots', 'scale', 'fc1_weight', 'fc1_bias', 'fc2_weight', 'fc2_bias', 'norm_weight')}
    del _L0_ffn_all
    return {'x': x, 'src': src, 'dst': dst, 'L0_gnn_W_fc': _L0_gnn_in['W_fc'], 'L0_gnn_attn_l': _L0_gnn_in['attn_l'], 'L0_gnn_attn_r': _L0_gnn_in['attn_r'], 'L0_gnn_W_res': _L0_gnn_in['W_res'], 'L0_ffn_slots': _L0_ffn_in['slots'], 'L0_ffn_scale': _L0_ffn_in['scale'], 'L0_ffn_fc1_weight': _L0_ffn_in['fc1_weight'], 'L0_ffn_fc1_bias': _L0_ffn_in['fc1_bias'], 'L0_ffn_fc2_weight': _L0_ffn_in['fc2_weight'], 'L0_ffn_fc2_bias': _L0_ffn_in['fc2_bias'], 'L0_ffn_norm_weight': _L0_ffn_in['norm_weight']}

def reference(x, src, dst, L0_gnn_W_fc, L0_gnn_attn_l, L0_gnn_attn_r, L0_gnn_W_res, L0_ffn_slots, L0_ffn_scale, L0_ffn_fc1_weight, L0_ffn_fc1_bias, L0_ffn_fc2_weight, L0_ffn_fc2_bias, L0_ffn_norm_weight):
    import jax
    import jax.numpy as jnp

    def _L0_gnn_ref(h, W_fc, attn_l, attn_r, W_res, src, dst):
        import jax, jax.numpy as jnp
        import numpy as np
        N = 50000
        E = 250000
        H = 12
        D = 64
        NEG_SLOPE = 0.2
        n = h.shape[0]
        hh = h.reshape(n, H, D)
        ft = jnp.einsum('nhd,ed->nhe', hh, W_fc)
        a1 = jnp.einsum('nhd,hd->nh', ft, attn_l)
        a2 = jnp.einsum('nhd,hd->nh', ft, attn_r)
        e = jax.nn.leaky_relu(a1[src] + a2[dst], negative_slope=NEG_SLOPE)
        m = jax.ops.segment_max(e, dst, num_segments=n)
        ee = jnp.exp(e - m[dst])
        denom = jax.ops.segment_sum(ee, dst, num_segments=n)
        alpha = ee / denom[dst]
        agg = jax.ops.segment_sum(alpha[:, :, None] * ft[src], dst, num_segments=n)
        res = jnp.einsum('nhd,ed->nhe', hh, W_res)
        return jax.nn.relu((res + agg).reshape(n, H * D))

    def _L0_ffn_ref(x, slots, scale, fc1_weight, fc1_bias, fc2_weight, fc2_bias, norm_weight):
        import jax, jax.numpy as jnp
        import numpy as np
        EPS_NORM = 1e-05
        RMS_EPS = 1e-05

        def _l2_normalize(v):
            n = jnp.sqrt(jnp.sum(v * v, axis=-1, keepdims=True))
            return v / jnp.maximum(n, EPS_NORM)

        def _rms_norm(x, weight, eps):
            ms = jnp.mean(x * x, axis=-1, keepdims=True)
            return x * jax.lax.rsqrt(ms + eps) * weight
        xn = _rms_norm(x, norm_weight, RMS_EPS)
        tok = _l2_normalize(xn)
        sl = _l2_normalize(slots) * scale[:, None]
        logits = jnp.einsum('sd,btd->bst', sl, tok)
        dispatch_w = jax.nn.softmax(logits, axis=-1)
        combine_w = jax.nn.softmax(logits, axis=-2)
        y = jnp.einsum('btd,bst->bsd', xn, dispatch_w)
        y = jnp.einsum('sio,bsi->bso', fc1_weight, y) + fc1_bias
        y = jax.nn.gelu(y, approximate=False)
        y = jnp.einsum('sio,bsi->bso', fc2_weight, y) + fc2_bias
        out = jnp.einsum('bsd,bst->btd', y, combine_w)
        return out
    x = x + _L0_gnn_ref(_layernorm(x, axis=-1), L0_gnn_W_fc, L0_gnn_attn_l, L0_gnn_attn_r, L0_gnn_W_res, src, dst)
    x = x + _L0_ffn_ref(_layernorm(x, axis=-1)[None], L0_ffn_slots, L0_ffn_scale, L0_ffn_fc1_weight, L0_ffn_fc1_bias, L0_ffn_fc2_weight, L0_ffn_fc2_bias, L0_ffn_norm_weight)[0]
    return x

_drawn_inputs = setup_inputs


def setup_inputs(seed=0):
    import zlib

    import numpy as np

    out = dict(_drawn_inputs(seed))
    spreads = {'L0_ffn_scale': (1.0, 0.6),
     'L0_ffn_fc1_bias': (0.0, 0.8),
     'L0_ffn_fc2_bias': (0.0, 0.8),
     'L0_ffn_norm_weight': (1.0, 0.6)}
    factors = {'L0_ffn_slots': 64.0, 'L0_ffn_fc1_weight': 29.404, 'L0_ffn_fc2_weight': 8.0}
    for name, (base, spread) in spreads.items():
        noise = np.random.default_rng([zlib.crc32(name.encode()), seed]).standard_normal(out[name].shape)
        drawn = base * np.exp(spread * noise) if base else spread * noise
        out[name] = jnp.asarray(drawn.astype(out[name].dtype))
    for name, factor in factors.items():
        out[name] = (out[name] * factor).astype(out[name].dtype)
    return out
```

```python
import concourse.bass as bass
from concourse import mybir
from concourse.alu_op_type import AluOpType as ALU
from contextlib import ExitStack

F32 = mybir.dt.float32
BF16 = mybir.dt.bfloat16
I32 = mybir.dt.int32
ACT = mybir.ActivationFunctionType
AX = mybir.AxisListType

P = 128
LAP = 6
BIG = 1.0e38
EPS = 1e-5
SLOPE = 0.2
TAB = 32
A2, MEAN, RSTD = 12, 24, 25


class Step:

    def __init__(self, t, lap, slot, rows):
        self.t, self.lap, self.slot, self.rows = t, lap, slot, rows

    def ring(self, depth):
        return self.slot % depth

    def div(self, depth):
        return self.lap * (LAP // depth) + self.slot // depth

    def after(self, depth):
        return not isinstance(self.t, int) or self.t >= depth

    def shift(self, by):
        over = (self.slot + by) // LAP
        return Step(self.t + by, self.lap + over, (self.slot + by) % LAP, P)


def ring_uses(tiles, depth, slot):
    return (tiles - slot + depth - 1) // depth


def walk(eng, full, unroll, tail_rows, body):
    for t in range(unroll):
        body(Step(t, 0, t, P))
    with eng.Fori(1, full // unroll) as lap:
        for k in range(unroll):
            body(Step(lap * unroll + k, lap, k, P))
    if tail_rows:
        body(Step(full, full // unroll, 0, tail_rows))


def build(nc, x, src, dst, w_cat, w_fc, attn, slots, scale, w1, b1t, w2, b2, norm_w, out):
    N, D = x.shape
    H, DH = attn.shape[1] // 2, w_fc.shape[0]
    S, _, F = w1.shape
    FULL, TAIL = N // P, N % P
    NT = FULL + 1
    C = D // P
    ET = 80
    EG = 4
    GROUPS = ET // EG
    PAD_NODE = ET * P - 1
    ROW = D + 2 * H
    NU = LAP
    POOL_SET = 10
    NG = 3
    LAPS_E = ET // (2 * EG)
    E_FULL, E_TAIL = src.shape[0] // P, src.shape[0] % P

    node_table = nc.dram_tensor("node_table", (N, TAB), F32).ap()
    seg_rows = nc.dram_tensor("seg_rows", (ET * P, ROW), F32).ap()
    dst_padded = nc.dram_tensor("dst_padded", (ET, P), I32).ap()
    x1_dram = nc.dram_tensor("x1_dram", (N, D), F32).ap()

    ctx = ExitStack()
    with ctx:
        def sb(name, shape, dt=F32):
            return ctx.enter_context(nc.sbuf_tensor(name, shape, dt))

        def sem(name):
            return ctx.enter_context(nc.semaphore(name))

        ident = sb("ident", [P, P])
        wcat = sb("wcat", [P, DH])
        avec = sb("avec", [P, C * 2 * H])
        slT = sb("slT", [P, C, S])
        wn = sb("wn", [P, D])
        table = sb("table", [P, NT + 1, TAB])
        logits = sb("logits", [P, NT, S])
        src_i = sb("src_i", [P, ET], I32)
        dst_i = sb("dst_i", [P, ET], I32)
        dst_f = sb("dst_f", [P, ET])
        hi_f = sb("hi_f", [P, ET])
        lo_f = sb("lo_f", [P, ET])
        iota_f = sb("iota_f", [P, P])
        flag_t = sb("flag_t", [P, ET])
        pos_i = sb("pos_i", [P, ET], I32)
        first_end = sb("first_end", [ET, 1], I32)
        chain = sb("chain", [ET, ET])
        tri = sb("tri", [ET, ET])
        kc = sb("kc", [P, 4])
        ones = sb("ones", [P, P])

        ph = ExitStack()

        def scratch(name, shape, dt=F32):
            return ph.enter_context(nc.sbuf_tensor(name, shape, dt))

        e_src = scratch("e_src", [ET, P], I32)
        e_dst = scratch("e_dst", [ET, P], I32)
        e_srcf = scratch("e_srcf", [ET, P])
        e_dstf = scratch("e_dstf", [ET, P])
        e_flag = scratch("e_flag", [ET, P])
        e_eq = scratch("e_eq", [ET, P])
        e_cnt = scratch("e_cnt", [ET, 1])
        e_base = scratch("e_base", [ET, 1], I32)
        e_basef = scratch("e_basef", [ET, 1])
        sel_last = scratch("sel_last", [P, ET])
        dst_ti = scratch("dst_ti", [P, ET], I32)
        hi_i = scratch("hi_i", [P, ET], I32)
        lo_i = scratch("lo_i", [P, ET], I32)
        iota_i = scratch("iota_i", [P, P], I32)
        wfc2 = scratch("wfc2", [DH, 2 * DH])
        attn_sb = scratch("attn_sb", [DH, 2 * H])
        slots_sb = scratch("slots_sb", [S, D])
        slots_sq = scratch("slots_sq", [S, D])
        scale_sb = scratch("scale_sb", [S, 1])
        s_norm = scratch("s_norm", [S, 4])
        xa = scratch("xa", [P, 6, D])
        ha = scratch("ha", [P, 2, D])
        haT = scratch("haT", [P, 2, D])
        bna = scratch("bna", [P, 2, 12])
        mva = scratch("mva", [P, 2, 4])
        ph.close()

        ph = ExitStack()
        XR = 2 * EG
        dst_row = scratch("dst_row", [P, 2, EG * P], I32)
        ix_s = scratch("ix_s", [P, 2, EG], I32)
        ix_d = scratch("ix_d", [P, 2, EG], I32)
        tg_s = scratch("tg_s", [P, 2, EG, TAB])
        tg_d = scratch("tg_d", [P, 2, EG, TAB])
        dsc = scratch("dsc", [P, 2, EG])
        sc = scratch("sc", [P, EG, H])
        lk = scratch("lk", [P, EG, H])
        fb = scratch("fb", [P, EG, H])
        flagT = scratch("flagT", [EG * H, P + 1])
        pmax = scratch("pmax", [EG * H, P])
        smax = scratch("smax", [EG * H, P])
        dif = scratch("dif", [EG * H, P])
        eeT = scratch("eeT", [EG * H, P])
        eem = scratch("eem", [P, 2, 2, EG, H])
        wt = scratch("wt", [P, 2, EG, H])
        hot_hi = scratch("hot_hi", [P, 2, EG, ET], BF16)
        hot_lo = scratch("hot_lo", [P, 2, EG, P], BF16)
        deg = scratch("deg", [ET, P])
        xg = scratch("xg", [P, XR, D])
        vv = scratch("vv", [P, 2, D])
        same = scratch("same", [P, 2, P])
        rl = scratch("rl", [P, 2, H])
        zo = scratch("zo", [P, 4, ROW])
        cum = scratch("cum", [ET, P])
        none = scratch("none", [ET, P])
        off_sb = scratch("off_sb", [ET, 1])
        pos_f = scratch("pos_f", [ET, P])
        rr = scratch("rr", [ET, ROW])
        ff = scratch("ff", [ET, ROW])
        bd = scratch("bd", [ET, H, ET])
        bm = scratch("bm", [ET, H, ET])
        be = scratch("be", [ET, H, ET])
        bwT = scratch("bwT", [ET, H, ET])
        bmax = scratch("bmax", [ET, H])
        bdf = scratch("bdf", [ET, H])
        bcf = scratch("bcf", [ET, H])
        btot = scratch("btot", [ET, H])
        bz = scratch("bz", [ET, D])
        ph.close()

        ph = ExitStack()
        xn = scratch("xn", [P, 3, D])
        ixn = scratch("ixn", [P, 3, 1], I32)
        mr = scratch("mr", [P, 3, 2])
        cat = scratch("cat", [P, 3, D + ROW])
        catT = scratch("catT", [P, H * P])
        x1 = scratch("x1", [P, 3, D])
        uu = scratch("uu", [P, NU, D])
        usq = scratch("usq", [P, D])
        uT = scratch("uT", [P, D])
        bnn = scratch("bnn", [P, 12])
        mvn = scratch("mvn", [P, 3, 2])
        usum = scratch("usum", [P, 3, 1])
        gam = scratch("gam", [P, NU, 1])
        pw = scratch("pw", [P, 6])
        tok = scratch("tok", [P, 3, 1])
        lg = scratch("lg", [P, 3, S])
        mrun = scratch("mrun", [S, 2, 1])
        nneg = scratch("nneg", [S, 1])
        gmax = scratch("gmax", [S, 1])
        cc = scratch("cc", [S, 1])
        cdiag = scratch("cdiag", [S, S])
        dT = scratch("dT", [S, NG * P])
        dsum = scratch("dsum", [S, 1])
        lrun = scratch("lrun", [S, 1])
        pg = scratch("pg", [P, NG, S])
        ytmp = scratch("ytmp", [P, C, S])
        yT = scratch("yT", [P, C, S])
        w1b = scratch("w1b", [P, 4, 2, C * F])
        w2b = scratch("w2b", [F, 4, 2, D])
        b1_sb = scratch("b1_sb", [F, S])
        hpre = scratch("hpre", [F, S])
        hT = scratch("hT", [F, S])
        rlr = scratch("rlr", [S, 1])
        y2T = scratch("y2T", [P, C * S])
        b2_sb = scratch("b2_sb", [S, D])
        y2 = scratch("y2", [S, D])
        xo = scratch("xo", [P, 6, D])
        oo = scratch("oo", [P, 3, D])
        tmax = scratch("tmax", [P, NT])
        tsum = scratch("tsum", [P, NT])
        ex = scratch("ex", [P, 2, S])
        exT = scratch("exT", [S, 2, P])
        ph.close()

        ps = ctx.enter_context(nc.psum_tensor("ps", [P, 8 * 512], F32))

        def bank(b, n=512, at=0):
            return ps[:, b * 512 + at:b * 512 + at + n]

        def sems(names):
            return [sem(n) for n in names.split()]

        s_in, s_edge_in, s_edge_pad, s_dstp, s_ident, s_pool = sems("s_in s_edge_in s_edge_pad s_dstp s_ident s_pool")
        s_dve, s_pe, s_gp = sems("s_dve s_pe s_gp")
        s_copies, s_sq, s_slots = sems("s_copies s_sq s_slots")

        xa_in = [sem(f"xa_in_{i}") for i in range(6)]
        a_bn, a_mv, a_ve, a_rstd, a_hh, a_mr, a_tr, a_ev, a_att, a_tab, a_out = sems(
            "a_bn a_mv a_ve a_rstd a_hh a_mr a_tr a_ev a_att a_tab a_out")

        e_row = [sem(f"e_row_{i}") for i in range(2)]
        e_tab = [sem(f"e_tab_{i}") for i in range(2)]
        e_x = [sem(f"e_x_{i}") for i in range(XR)]
        e_out = [sem(f"e_out_{i}") for i in range(4)]
        e_ix, e_sc, e_lk, e_fb, e_dsc, e_tr, e_flag_ev, e_pm, e_sm, e_dif = sems(
            "e_ix e_sc e_lk e_fb e_dsc e_tr e_flag_ev e_pm e_sm e_dif")
        e_exp, e_back, e_em, e_wt, e_hot, e_hist, e_deg, e_init = sems(
            "e_exp e_back e_em e_wt e_hot e_hist e_deg e_init")
        e_vv, e_same, e_mm, e_rl, e_z, e_lcp, e_mcp, e_go = sems("e_vv e_same e_mm e_rl e_z e_lcp e_mcp e_go")
        b_in, b_ff, b_fix, b_dve, b_pe, b_act = sems("b_in b_ff b_fix b_dve b_pe b_act")

        n_x = [sem(f"n_x_{i}") for i in range(3)]
        n_ag = [sem(f"n_ag_{i}") for i in range(3)]
        n_st = [sem(f"n_st_{i}") for i in range(3)]
        n_ix, n_mr, n_hh, n_t1, n_ev01, n_ev2, n_mm, n_x1, n_bn, n_mv, n_u, n_sq = sems(
            "n_ix n_mr n_hh n_t1 n_ev01 n_ev2 n_mm n_x1 n_bn n_mv n_u n_sq")
        n_t3, n_ev3, n_lg, n_pw, n_gam, n_tok, n_L, n_keep, n_go = sems(
            "n_t3 n_ev3 n_lg n_pw n_gam n_tok n_L n_keep n_go")
        g_init, g_lt, g_max, g_new, g_neg, g_exp, g_c, g_cd, g_back, g_pg, g_y, g_l, g_ym, g_ya = sems(
            "g_init g_lt g_max g_new g_neg g_exp g_c g_cd g_back g_pg g_y g_l g_ym g_ya")
        f_in, f_d, f_p, f_a, f_h, f_y = sems("f_in f_d f_p f_a f_h f_y")
        f_w1 = [sem(f"f_w1_{i}") for i in range(4)]
        f_w2 = [sem(f"f_w2_{i}") for i in range(4)]
        o_x = [sem(f"o_x_{i}") for i in range(6)]
        o_out = [sem(f"o_out_{i}") for i in range(3)]
        o_cw, o_cexp, o_ex, o_t, o_ev, o_mm, o_o = sems("o_cw o_cexp o_ex o_t o_ev o_mm o_o")

        def tile_rows(st):
            return bass.ds(st.t * P, st.rows)

        def chain_of(eng, s, start=0):
            n = [start]

            def link(ins):
                n[0] += 1
                ins.then_inc(s, 1)
                eng.wait_ge(s, n[0])
            return link

        block = ctx.enter_context(nc.Block())


        @block.sync
        def _(sp):
            sp.wait_ge(s_edge_pad, 2)
            for buf, lst in ((e_src, src), (e_dst, dst)):
                sp.dma_start(buf[0:E_FULL, :], lst[0:E_FULL * P].rearrange("(k p) -> k p", p=P)).then_inc(s_edge_in, 16)
                sp.dma_start(buf[E_FULL:E_FULL + 1, 0:E_TAIL],
                             lst[E_FULL * P:].rearrange("(a p) -> a p", a=1)).then_inc(s_edge_in, 16)
            sp.dma_start(wfc2[:, 0:DH], w_fc[:, :]).then_inc(s_in, 16)
            sp.dma_start(wfc2[:, DH:2 * DH], w_fc[:, :]).then_inc(s_in, 16)
            sp.dma_start(attn_sb[:, :], attn[:, :]).then_inc(s_in, 16)
            sp.dma_start(wcat[:, :], w_cat[:, :]).then_inc(s_in, 16)
            sp.dma_start(slots_sb[:, :], slots[:, :]).then_inc(s_in, 16)
            sp.dma_start(scale_sb[:, :], scale.rearrange("(s a) -> s a", a=1)).then_inc(s_in, 16)
            sp.dma_start(wn[:, :], norm_w.partition_broadcast(P)).then_inc(s_in, 16)
            sp.wait_ge(s_edge_in, 64)
            sp.dma_start(dst_padded[:, :], e_dst[:, :]).then_inc(s_dstp, 16)

            def load_x(st):
                if st.after(6):
                    sp.wait_ge(a_hh, st.t - 5)
                sp.dma_start(xa[0:st.rows, st.slot, :], x[tile_rows(st), :]).then_inc(xa_in[st.slot], 16)
            walk(sp, FULL, NU, TAIL, load_x)

            sp.wait_ge(s_dstp, 16)
            sp.wait_ge(a_tab, NT)

            def row_in(lap, gb):
                sp.dma_start(dst_row[:, gb, :],
                             dst_padded[bass.ds(lap * 2 * EG + gb * EG, EG), :]
                             .rearrange("k p -> (k p)").partition_broadcast(P)).then_inc(e_row[gb], 16)

            def rows_out(lap, k):
                t = lap * XR + k
                sp.wait_ge(e_z, t + 1)
                sp.wait_ge(e_lcp, t + 1)
                sp.wait_ge(e_mcp, t + 1)
                sp.dma_start(seg_rows[bass.ds(t * P, P), :], zo[:, k % 4, :]).then_inc(e_out[k % 4], 16)

            row_in(0, 0)
            row_in(0, 1)
            for k in range(XR):
                rows_out(0, k)
            with sp.Fori(1, LAPS_E) as lap:
                for k in range(XR):
                    if k % EG == 0:
                        sp.wait_ge(e_same, (lap - 1) * XR + k + EG)
                        row_in(lap, k // EG)
                    rows_out(lap, k)
            for j in range(4):
                sp.wait_ge(e_out[j], 16 * (ET // 4))
            sp.dma_start(rr[:, :], seg_rows.rearrange("(k p) r -> k p r", p=P)[:, P - 1, :]).then_inc(b_in, 16)

            sp.wait_ge(b_fix, 16)

            def store_x1(st):
                sp.wait_ge(n_x1, st.t + 1)
                sp.dma_start(x1_dram[tile_rows(st), :], x1[0:st.rows, st.ring(3), :]).then_inc(n_st[st.ring(3)], 16)

            def nodes_io(st):
                if st.after(3):
                    store_x1(st.shift(-3))
                sp.dma_start(xn[0:st.rows, st.ring(3), :], x[tile_rows(st), :]).then_inc(n_x[st.ring(3)], 16)

            sp.dma_start(b1_sb[:, :], b1t[:, :]).then_inc(f_in, 16)
            sp.dma_start(b2_sb[:, :], b2[:, :]).then_inc(f_in, 16)

            def load_w1(lap, q):
                sp.dma_start(w1b[:, q, :, :], w1[bass.ds(lap * 8 + 2 * q, 2)]
                             .rearrange("s (p c) f -> p s (c f)", p=P)).then_inc(f_w1[q], 16)

            def load_w2(lap, q):
                sp.dma_start(w2b[:, q, :, :], w2[bass.ds(lap * 8 + 2 * q, 2)]
                             .rearrange("s f d -> f s d")).then_inc(f_w2[q], 16)

            walk(sp, FULL, NU, TAIL, nodes_io)
            for t in range(NT - 3, NT):
                store_x1(Step(t, t // NU, t % NU, P if t < FULL else TAIL))
            for q in range(4):
                load_w1(0, q)
            for q in range(4):
                load_w2(0, q)
            with sp.Fori(1, S // 8) as lap:
                for q in range(4):
                    sp.wait_ge(f_h, lap * 4 + q - 3)
                    load_w1(lap, q)
            with sp.Fori(1, S // 8) as lap:
                for q in range(4):
                    sp.wait_ge(f_y, lap * 4 + q - 3)
                    load_w2(lap, q)

            def store_out(st):
                sp.wait_ge(o_o, st.t + 1)
                sp.dma_start(out[tile_rows(st), :], oo[0:st.rows, st.ring(3), :]).then_inc(o_out[st.ring(3)], 16)
            walk(sp, FULL, NU, TAIL, store_out)
            for i in range(3):
                sp.wait_ge(o_out[i], 16 * ring_uses(NT, 3, i))

        @block.gpsimd
        def _(g):
            g.memset(e_src[:, :], 0).then_inc(s_edge_pad, 1)
            g.memset(e_dst[:, :], PAD_NODE).then_inc(s_edge_pad, 1)
            g.memset(ident[:, :], 0.0).then_inc(s_ident, 1)
            for i, v in enumerate((-0.5, EPS, 1.0 + EPS, EPS * EPS)):
                g.memset(kc[:, i:i + 1], v).then_inc(s_pool, 1)
            g.memset(ones[:, :], 1.0).then_inc(s_pool, 1)
            g.iota(iota_i[:, :], pattern=[[1, P]], base=0, channel_multiplier=0).then_inc(s_pool, 1)
            g.iota(e_base[:, :], pattern=[[0, 1]], base=-1, channel_multiplier=P).then_inc(s_pool, 1)
            g.memset(tri[:, :], 1.0).then_inc(s_pool, 1)
            g.memset(table[:, :, :], 0.0).then_inc(s_pool, 1)
            g.wait_ge(s_ident, 1)
            g.affine_select(out=ident[:, :], in_=ident[:, :], compare_op=ALU.not_equal, fill=1.0, base=0,
                            pattern=[[-1, P]], channel_multiplier=1).then_inc(s_ident, 1)
            g.wait_ge(s_pool, POOL_SET - 1)
            g.affine_select(out=tri[:, :], in_=tri[:, :], compare_op=ALU.is_gt, fill=0.0, base=0,
                            pattern=[[1, ET]], channel_multiplier=-1).then_inc(s_pool, 1)
            g.wait_ge(s_sq, 1)
            g.tensor_scalar(s_norm[:, 1:2], s_norm[:, 0:1], EPS * EPS, None, ALU.max).then_inc(s_gp, 1)
            g.wait_ge(s_gp, 1)
            g.tensor_tensor(s_norm[:, 2:3], s_norm[:, 1:2], kc[0:S, 0:1], ALU.pow).then_inc(s_gp, 1)

            def rstd(st):
                b = st.ring(2)
                g.wait_ge(a_mv, st.t + 1)
                g.tensor_tensor(mva[:, b, 2:3], mva[:, b, 1:2], kc[:, 1:2], ALU.add).then_inc(a_ve, 1)
                g.wait_ge(a_ve, st.t + 1)
                g.tensor_tensor(mva[:, b, 3:4], mva[:, b, 2:3], kc[:, 0:1], ALU.pow).then_inc(a_rstd, 1)
            walk(g, FULL, NU, TAIL, rstd)

            g.wait_ge(a_tab, NT)
            g.wait_ge(a_out, 16 * (FULL // NU + 1))

            def table_rows(lap, gb, first):
                if not first:
                    for j in range(EG):
                        g.wait_ge(e_x[gb * EG + j], lap * 16)
                    g.wait_ge(e_tab[gb], lap * 32 * EG)
                    g.sem_inc(e_go, 1)
                base = lap * XR + gb * EG
                g.tensor_copy(ix_s[:, gb, :], src_i[:, bass.ds(base, EG)]).then_inc(e_ix, 1)
                g.tensor_copy(ix_d[:, gb, :], dst_i[:, bass.ds(base, EG)]).then_inc(e_ix, 1)
                g.wait_ge(e_ix, (lap * 2 + gb) * 2 + 2)
                if not first:
                    g.wait_ge(e_wt, lap * 2 + gb - 1)
                    g.wait_ge(e_vv, (lap * 2 + gb - 1) * EG)
                g.sem_inc(e_go, 1)
                for j in range(EG):
                    for ix, tg in ((ix_s, tg_s), (ix_d, tg_d)):
                        g.indirect_dma_start(
                            out=tg[:, gb, j, :], out_offset=None, in_=node_table[:, :],
                            in_offset=bass.IndirectOffsetOnAxis(ap=ix[:, gb, j:j + 1], axis=0))\
                            .then_inc(e_tab[gb], 16)

            def x_rows(lap, gb, first):
                for j in range(EG):
                    slot = gb * EG + j
                    if not first:
                        g.wait_ge(e_vv, (lap - 1) * XR + slot + 1)
                        g.sem_inc(e_go, 1)
                    g.indirect_dma_start(
                        out=xg[:, slot, :], out_offset=None, in_=x[:, :],
                        in_offset=bass.IndirectOffsetOnAxis(ap=ix_s[:, gb, j:j + 1], axis=0))\
                        .then_inc(e_x[slot], 16)

            g.wait_ge(s_dve, 16)
            for gb in range(2):
                table_rows(0, gb, True)
                x_rows(0, gb, True)
            with g.Fori(1, LAPS_E) as lap:
                for gb in range(2):
                    table_rows(lap, gb, False)
                    x_rows(lap, gb, False)

            for j in range(4):
                g.wait_ge(e_out[j], 16 * (ET // 4))
            g.indirect_dma_start(out=ff[:, :], out_offset=None, in_=seg_rows[:, :],
                                 in_offset=bass.IndirectOffsetOnAxis(ap=first_end[:, 0:1], axis=0)).then_inc(b_ff, 16)
            g.wait_ge(b_dve, 22)
            g.wait_ge(b_in, 16)
            g.indirect_dma_start(out=seg_rows[:, :], in_=ff[:, :], in_offset=None,
                                 out_offset=bass.IndirectOffsetOnAxis(ap=first_end[:, 0:1], axis=0)).then_inc(b_fix, 16)

            g.wait_ge(b_fix, 16)

            def gather(st, first):
                r, u = st.ring(3), st.t
                if not first:
                    g.wait_ge(n_t1, u - 2)
                    g.wait_ge(n_hh, u - 2)
                    g.wait_ge(n_ag[r], 16 * st.div(3))
                    g.sem_inc(n_go, 1)
                g.tensor_copy(ixn[:, r, :], pos_i[:, bass.ds(u, 1)]).then_inc(n_ix, 1)
                g.tensor_copy(mr[:, r, :], table[:, bass.ds(u, 1), MEAN:RSTD + 1]).then_inc(n_mr, 1)
                g.memset(cat[:, r, D:D + ROW], 0.0).then_inc(n_ix, 1)
                g.wait_ge(n_ix, u * 2 + 2)
                g.sem_inc(n_go, 1)
                g.indirect_dma_start(out=cat[:, r, D:D + ROW], out_offset=None, in_=seg_rows[:, :],
                                     in_offset=bass.IndirectOffsetOnAxis(ap=ixn[:, r, :], axis=0),
                                     bounds_check=ET * P - 1, oob_is_err=False).then_inc(n_ag[r], 16)

            def norms(st):
                u, r, s6 = st.t, st.ring(3), st.slot
                base = u * 6
                g.wait_ge(n_mv, u + 1)
                g.tensor_tensor(pw[:, 0:1], mvn[:, r, 1:2], kc[:, 2:3], ALU.mult).then_inc(n_pw, 1)
                g.wait_ge(n_pw, base + 1)
                g.tensor_tensor(pw[:, 1:2], pw[:, 0:1], kc[:, 3:4], ALU.add).then_inc(n_pw, 1)
                g.wait_ge(n_pw, base + 2)
                if st.after(6):
                    g.wait_ge(g_pg, st.div(3) - 1)
                g.tensor_tensor(gam[:, s6, :], pw[:, 1:2], kc[:, 0:1], ALU.pow).then_inc(n_gam, 1)
                g.wait_ge(n_gam, u + 1)
                g.tensor_tensor(pw[:, 2:3], gam[:, s6, :], gam[:, s6, :], ALU.mult).then_inc(n_pw, 1)
                g.wait_ge(n_pw, base + 3)
                g.wait_ge(n_sq, u + 1)
                g.tensor_tensor(pw[:, 3:4], pw[:, 2:3], usum[:, r, :], ALU.mult).then_inc(n_pw, 1)
                g.wait_ge(n_pw, base + 4)
                g.sem_inc(n_go, 1)
                g.tensor_scalar(pw[:, 4:5], pw[:, 3:4], EPS * EPS, None, ALU.max).then_inc(n_pw, 1)
                g.wait_ge(n_pw, base + 5)
                g.tensor_tensor(pw[:, 5:6], pw[:, 4:5], kc[:, 0:1], ALU.pow).then_inc(n_pw, 1)
                g.wait_ge(n_pw, base + 6)
                if st.after(3):
                    g.wait_ge(n_L, u - 2)
                g.tensor_tensor(tok[:, r, :], gam[:, s6, :], pw[:, 5:6], ALU.mult).then_inc(n_tok, 1)

            def node_step(st):
                if not (isinstance(st.t, int) and st.t == FULL):
                    gather(st.shift(2), isinstance(st.t, int) and st.t == 0)
                if st.after(1):
                    norms(st.shift(-1))
            g.wait_ge(b_dve, 6)
            gather(Step(0, 0, 0, P), True)
            gather(Step(1, 0, 1, P), True)
            walk(g, FULL, NU, TAIL, node_step)
            norms(Step(FULL, FULL // NU, 0, P))

            for i in range(3):
                g.wait_ge(n_st[i], 16 * ring_uses(NT, 3, i))

            def load_x1(st):
                if st.after(6):
                    g.wait_ge(o_o, st.t - 5)
                    g.sem_inc(n_go, 1)
                g.dma_start(xo[0:st.rows, st.slot, :], x1_dram[tile_rows(st), :]).then_inc(o_x[st.slot], 16)
            walk(g, FULL, NU, TAIL, load_x1)

        @block.tensor
        def _(pe):
            mm, tr = nc.tensor.matmul, nc.tensor.transpose

            pe.wait_ge(s_in, 16 * 7)
            mm(bank(6, 2 * H), wfc2[:, :], attn_sb[:, :], start=True, stop=True).then_inc(s_pe, 1)
            pe.wait_ge(s_ident, 2)
            pe.wait_ge(s_dve, 4)
            for i, m in enumerate((e_srcf, e_dstf, e_flag)):
                last = tr(bank(7, ET, i * ET), m[:, :], ident[0:ET, 0:ET])
            last.then_inc(s_pe, 1)
            pe.wait_ge(s_dve, 6)
            mm(ps[0:ET, 7 * 512 + 256:7 * 512 + 256 + ET], sel_last[:, :], dst_f[:, :], start=True, stop=True)\
                .then_inc(s_pe, 1)
            pe.wait_ge(s_slots, 1)
            pe.wait_ge(s_dve, 16)
            for c in range(C):
                last = tr(bank(7, S, c * S), slots_sq[:, c * P:(c + 1) * P], ident[0:S, 0:S])
            last.then_inc(s_pe, 1)

            pe.wait_ge(s_dve, 21)

            def attention(st):
                b = st.ring(2)
                pe.wait_ge(a_ev, st.t + 1)
                if st.after(2):
                    pe.wait_ge(a_tab, st.t - 1)
                for c in range(C):
                    last = mm(bank(4 + b, 2 * H), haT[:, b, c * P:(c + 1) * P], avec[:, c * 2 * H:(c + 1) * 2 * H],
                              start=(c == 0), stop=(c == C - 1))
                last.then_inc(a_att, 1)

            def stats_step(st):
                b = st.ring(2)
                pe.wait_ge(a_hh, st.t + 1)
                if st.after(2):
                    pe.wait_ge(a_ev, st.t - 1)
                for c in range(C):
                    last = tr(bank(2 * b, P, c * P), ha[:, b, c * P:(c + 1) * P], ident[:, :])
                last.then_inc(a_tr, 1)
                if st.after(1):
                    attention(st.shift(-1))
            walk(pe, FULL, NU, TAIL, stats_step)
            attention(Step(FULL, FULL // NU, 0, P))

            pe.wait_ge(a_tab, NT)

            def group(lap, gb, first):
                n = lap * 2 + gb
                pe.wait_ge(e_lk, n + 1)
                pe.wait_ge(e_fb, n + 1)
                if not first:
                    pe.wait_ge(e_dif, n)
                    pe.wait_ge(e_flag_ev, n)
                pe.sem_inc(e_go, 1)
                tr(ps[0:EG * H, 4 * 512:4 * 512 + P], lk[:, :, :].rearrange("p k h -> p (k h)"), ident[:, :])
                tr(ps[0:EG * H, 4 * 512 + P:4 * 512 + 2 * P], fb[:, :, :].rearrange("p k h -> p (k h)"), ident[:, :])\
                    .then_inc(e_tr, 1)
                pe.wait_ge(e_hot, n + 1)
                if not first:
                    pe.wait_ge(e_deg, n)
                for j in range(EG):
                    last = mm(ps[0:ET, 6 * 512:6 * 512 + P], hot_hi[:, gb, j, :], hot_lo[:, gb, j, :],
                              start=(j == 0), stop=(j == EG - 1))
                last.then_inc(e_hist, 1)
                pe.wait_ge(e_exp, n + 1)
                pe.wait_ge(e_sm, n + 1)
                if not first:
                    pe.wait_ge(e_em, n)
                pe.sem_inc(e_go, 1)
                tr(bank(5, EG * H), eeT[:, :], ident[0:EG * H, 0:EG * H])
                tr(bank(5, EG * H, EG * H), smax[:, :], ident[0:EG * H, 0:EG * H]).then_inc(e_back, 1)
                for j in range(EG):
                    t = lap * XR + gb * EG + j
                    b = j % 2
                    pe.wait_ge(e_em, n + 1)
                    pe.wait_ge(e_same, t + 1)
                    pe.wait_ge(e_vv, t + 1)
                    if not first or j >= 2:
                        pe.wait_ge(e_z, t - 1)
                        pe.wait_ge(e_lcp, t - 1)
                    mm(bank(2 * b), same[:, b, :], vv[:, b, 0:512], start=True, stop=True)
                    mm(bank(2 * b + 1, D - 512), same[:, b, :], vv[:, b, 512:D], start=True, stop=True)
                    mm(bank(2 * b + 1, H, D - 512), same[:, b, :], eem[:, gb, 0, j, :], start=True, stop=True)\
                        .then_inc(e_mm, 1)
            group(0, 0, True)
            group(0, 1, False)
            with pe.Fori(1, LAPS_E) as lap:
                for gb in range(2):
                    group(lap, gb, False)

            pe.wait_ge(b_dve, 1)
            mm(ps[0:ET, 7 * 512:7 * 512 + 1], tri[:, :], cum[:, P - 1:P], start=True, stop=True).then_inc(b_pe, 1)
            pe.wait_ge(b_dve, 5)
            tr(bank(7, ET, 256), pos_f[:, :], ident[0:ET, 0:ET]).then_inc(b_pe, 1)
            pe.wait_ge(b_dve, 7)
            HH = H // 2
            for i in range(2):
                last = mm(ps[0:ET, i * 512:i * 512 + HH * ET], ones[0:ET, 0:ET],
                          bd[:, i * HH:(i + 1) * HH, :].rearrange("j h k -> j (h k)"), start=True, stop=True)
            last.then_inc(b_pe, 1)
            pe.wait_ge(b_act, 1)
            for h in range(H):
                at = (2 + h // HH) * 512 + (h % HH) * ET
                last = tr(ps[0:ET, at:at + ET], be[:, h, :], ident[0:ET, 0:ET])
            last.then_inc(b_pe, 1)
            pe.wait_ge(b_dve, 15)
            for h in range(H):
                mm(ps[0:ET, 4 * 512 + h * DH:4 * 512 + (h + 1) * DH], bwT[:, h, :], rr[:, h:D:H],
                   start=True, stop=True)
                last = mm(ps[0:ET, 6 * 512 + h:6 * 512 + h + 1], bwT[:, h, :], ones[0:ET, 0:1], start=True, stop=True)
            last.then_inc(b_pe, 1)

            def cat_transposes(st):
                r = st.ring(3)
                pe.wait_ge(n_ag[r], 16 * st.div(3) + 16)
                pe.wait_ge(n_hh, st.t + 1)
                for h in range(H):
                    last = tr(bank(0, P, h * P), cat[:, r, h:2 * D:H], ident[:, :])
                last.then_inc(n_t1, 1)

            def slot_logits(st):
                pe.wait_ge(n_ev3, st.t + 1)
                if st.after(1):
                    pe.wait_ge(n_L, st.t)
                for c in range(C):
                    last = mm(bank(5, S), uT[:, c * P:(c + 1) * P], slT[:, c, :], start=(c == 0), stop=(c == C - 1))
                last.then_inc(n_lg, 1)

            def group_transpose(q, tiles, rows, first):
                pe.wait_ge(n_L, q * NG + tiles)
                if not first:
                    pe.wait_ge(g_ym, q)
                    pe.wait_ge(g_pg, q)
                pe.sem_inc(n_go, 1)
                for j in range(tiles):
                    last = tr(ps[0:S, 6 * 512 + j * P:6 * 512 + j * P + rows], lg[0:rows, j, :],
                              ident[0:rows, 0:rows])
                last.then_inc(g_lt, 1)

            def group_back(q, tiles, rows):
                pe.wait_ge(g_exp, q + 1)
                pe.wait_ge(g_cd, q + 1)
                pe.sem_inc(n_go, 1)
                for j in range(tiles):
                    tr(ps[0:rows, 6 * 512 + j * S:6 * 512 + (j + 1) * S], dT[:, j * P:j * P + rows],
                       ident[0:S, 0:S])
                mm(bank(6, S, NG * S), ones[0:S, :], cdiag[:, :], start=True, stop=True).then_inc(g_back, 1)

            def group_inputs(q, tiles, rows, s0, first):
                pe.wait_ge(g_pg, q + 1)
                if not first:
                    pe.wait_ge(g_ya, q)
                for c in range(C):
                    for j in range(tiles):
                        last = mm(bank(7, S, c * S), uu[0:rows, s0 + j, c:D:C], pg[0:rows, j, :],
                                  start=(j == 0), stop=(j == tiles - 1))
                last.then_inc(g_y, 1)

            def node_mm(st):
                k = st.slot % NG
                tail = isinstance(st.t, int) and st.t == FULL
                pe.wait_ge(n_ev01, st.t + 1)
                pe.wait_ge(n_ev2, st.t + 1)
                if st.after(1):
                    pe.wait_ge(n_x1, st.t)
                for h in range(H):
                    last = mm(bank(3, DH, h * DH), catT[:, h * P:(h + 1) * P], wcat[:, :], start=True, stop=True)
                last.then_inc(n_mm, 1)
                if st.after(1):
                    slot_logits(st.shift(-1))
                if not tail:
                    if st.after(1):
                        pe.wait_ge(n_ev3, st.t)
                    cat_transposes(st.shift(1))
                if k == 2 and st.after(5):
                    q = st.div(3) - 1
                    group_back(q, NG, P)
                if not tail:
                    pe.wait_ge(n_ev01, st.t + 2)
                pe.wait_ge(n_u, st.t + 1)
                for c in range(C):
                    last = tr(bank(0, P, c * P), uu[:, st.slot, c * P:(c + 1) * P], ident[:, :])
                last.then_inc(n_t3, 1)
                if k == 0 and st.after(3):
                    group_transpose(st.div(3) - 1, NG, P, isinstance(st.t, int) and st.t < 6)
                if k == 2 and st.after(5):
                    group_inputs(st.div(3) - 1, NG, P, (st.slot + 1) % NU, isinstance(st.t, int) and st.t < 6)

            pe.wait_ge(b_fix, 16)
            cat_transposes(Step(0, 0, 0, P))
            walk(pe, FULL, NU, TAIL, node_mm)
            slot_logits(Step(FULL, FULL // NU, 0, P))
            QL = FULL // NG
            group_back(QL - 1, NG, P)
            group_inputs(QL - 1, NG, P, NG, False)
            group_transpose(QL, 1, TAIL, False)
            group_back(QL, 1, TAIL)
            group_inputs(QL, 1, TAIL, 0, False)

            pe.wait_ge(f_d, 2)
            mm(bank(5, S), ones[0:S, :], cdiag[:, :], start=True, stop=True).then_inc(f_p, 1)
            pe.wait_ge(f_d, 3)

            def first_products(lap):
                for q in range(4):
                    pe.wait_ge(f_w1[q], 16 * (lap + 1))
                    for e in range(2):
                        s = lap * 8 + 2 * q + e
                        for c in range(C):
                            last = mm(ps[0:F, bass.ds(s, 1)], w1b[:, q, e, c * F:(c + 1) * F],
                                      yT[:, c, bass.ds(s, 1)], start=(c == 0), stop=(c == C - 1))
                    last.then_inc(f_h, 1)

            def second_products(lap):
                for q in range(4):
                    pe.wait_ge(f_w2[q], 16 * (lap + 1))
                    for e in range(2):
                        s = lap * 8 + 2 * q + e
                        for c in range(C):
                            last = mm(ps[:, bass.ds(512 + c * S + s, 1)], w2b[:, q, e, c * P:(c + 1) * P],
                                      hT[:, bass.ds(s, 1)], start=True, stop=True)
                    last.then_inc(f_y, 1)

            first_products(0)
            with pe.Fori(1, S // 8) as lap:
                first_products(lap)
            pe.wait_ge(f_a, 1)
            second_products(0)
            with pe.Fori(1, S // 8) as lap:
                second_products(lap)
            pe.wait_ge(f_d, 5)
            for c in range(C):
                last = tr(ps[0:S, 2 * 512 + c * P:2 * 512 + (c + 1) * P], y2T[:, c * S:(c + 1) * S], ident[:, :])
            last.then_inc(f_p, 1)

            def mix(st):
                b = st.ring(2)
                pe.wait_ge(o_ev, st.t + 1)
                if st.after(2):
                    pe.wait_ge(o_o, st.t - 1)
                mm(bank(2 * b), exT[:, b, :], y2[:, 0:512], start=True, stop=True)
                mm(bank(2 * b + 1, D - 512), exT[:, b, :], y2[:, 512:D], start=True, stop=True).then_inc(o_mm, 1)

            def out_step(st):
                b = st.ring(2)
                pe.wait_ge(o_ex, st.t + 1)
                if st.after(2):
                    pe.wait_ge(o_ev, st.t - 1)
                pe.sem_inc(n_go, 1)
                tr(ps[0:S, (4 + b) * 512:(4 + b) * 512 + P], ex[:, b, :], ident[:, :]).then_inc(o_t, 1)
                if st.after(1):
                    mix(st.shift(-1))
            pe.wait_ge(f_d, 6)
            walk(pe, FULL, NU, TAIL, out_step)
            mix(Step(FULL, FULL // NU, 0, P))

        @block.scalar
        def _(act):
            def copy(o, i):
                return nc.scalar.activation(o, i, ACT.Copy)

            act.wait_ge(s_in, 16 * 7)
            nc.scalar.activation(slots_sq[:, :], slots_sb[:, :], ACT.Square, accum_out=s_norm[:, 0:1]).then_inc(s_sq, 1)

            def table_out(t0, k, rows):
                act.dma_start(node_table[bass.ds(t0 * P, (k - 1) * P + rows), :]
                              .rearrange("(k p) c -> p k c", k=k),
                              table[0:rows, bass.ds(t0, k), :]).then_inc(a_out, 16)

            def stats_step(st):
                b = st.ring(2)
                act.wait_ge(a_tr, st.t + 1)
                if st.after(2):
                    act.wait_ge(a_att, st.t - 1)
                copy(haT[:, b, :], bank(2 * b, D)).then_inc(a_ev, 1)
                if st.after(2):
                    copy(table[:, bass.ds(st.t - 2, 1), 0:2 * H], bank(4 + b, 2 * H)).then_inc(a_tab, 1)
                if st.slot == 1 and st.after(NU):
                    act.wait_ge(a_tab, st.t - 1)
                    act.wait_ge(a_mr, st.t - 1)
                    table_out(st.t - 1 - NU, NU, P)
            act.wait_ge(s_pool, POOL_SET)
            walk(act, FULL, NU, TAIL, stats_step)
            for t in (FULL - 1, FULL):
                act.wait_ge(a_att, t + 1)
                copy(table[:, t, 0:2 * H], bank(4 + t % 2, 2 * H)).then_inc(a_tab, 1)
            act.wait_ge(a_tab, NT)
            act.wait_ge(a_mr, NT)
            table_out(FULL - NU, NU, P)
            table_out(FULL, 1, TAIL)

            def group(lap, gb, first):
                n = lap * 2 + gb
                act.wait_ge(e_tr, n + 1)
                if not first:
                    act.wait_ge(e_sm, n)
                copy(flagT[:, 0:P], ps[0:EG * H, 4 * 512 + P:4 * 512 + 2 * P]).then_inc(e_flag_ev, 1)
                act.wait_ge(e_dif, n + 1)
                if not first:
                    act.wait_ge(e_back, n)
                nc.scalar.activation(eeT[:, :], dif[:, :], ACT.Exp).then_inc(e_exp, 1)
                act.wait_ge(e_em, n + 1)
                for j in range(EG):
                    t = lap * XR + gb * EG + j
                    if not first:
                        act.wait_ge(e_out[j], 16 * n)
                    copy(zo[:, j, D + H:ROW], eem[:, gb, 1, j, :]).then_inc(e_mcp, 1)
            group(0, 0, True)
            group(0, 1, False)
            with act.Fori(1, LAPS_E) as lap:
                for gb in range(2):
                    group(lap, gb, False)

            act.wait_ge(b_dve, 12)
            nc.scalar.activation(be[:, :, :], bm[:, :, :], ACT.Exp).then_inc(b_act, 1)
            act.wait_ge(b_dve, 13)
            nc.scalar.activation(bcf[:, :], bdf[:, :], ACT.Exp).then_inc(b_act, 1)

            def ev01(st):
                act.wait_ge(n_t1, st.t + 1)
                if st.after(1):
                    act.wait_ge(n_mm, st.t)
                copy(catT[:, 0:1024], bank(0, 1024)).then_inc(n_ev01, 1)

            def keep(st):
                copy(logits[:, bass.ds(st.t, 1), :], lg[:, st.ring(3), :]).then_inc(n_keep, 1)

            def group_exp(q, par, cols, first):
                act.wait_ge(g_neg, q + 1)
                if not first:
                    act.wait_ge(g_back, q)
                    act.wait_ge(g_l, q)
                    act.wait_ge(g_cd, q)
                nc.scalar.activation(dT[:, 0:cols], ps[0:S, 6 * 512:6 * 512 + cols], ACT.Exp, bias=nneg[:, :],
                                     accum_out=dsum[:, :]).then_inc(g_exp, 1)
                nc.scalar.activation(cc[:, :], mrun[:, 1 - par, :], ACT.Exp, bias=nneg[:, :]).then_inc(g_c, 1)

            def node_step(st):
                r = st.ring(3)
                if not (isinstance(st.t, int) and st.t == FULL):
                    ev01(st.shift(1))
                act.wait_ge(n_u, st.t + 1)
                if st.after(3):
                    act.wait_ge(n_tok, st.t - 2)
                nc.scalar.activation(usq[:, :], uu[:, st.slot, :], ACT.Square, accum_out=usum[:, r, :]).then_inc(n_sq, 1)
                act.wait_ge(n_t3, st.t + 1)
                if st.after(1):
                    act.wait_ge(n_lg, st.t)
                    act.wait_ge(n_L, st.t)
                copy(uT[:, :], bank(0, D)).then_inc(n_ev3, 1)
                if st.after(1):
                    keep(st.shift(-1))
                if st.slot % NG == 1 and st.after(4):
                    group_exp(st.div(3) - 1, (st.slot // NG + 1) % 2, NG * P, isinstance(st.t, int) and st.t < 6)
            act.wait_ge(b_fix, 16)
            ev01(Step(0, 0, 0, P))
            walk(act, FULL, NU, TAIL, node_step)
            act.wait_ge(n_L, NT)
            keep(Step(FULL, FULL // NU, 0, P))
            QL = FULL // NG
            group_exp(QL - 1, (QL - 1) % 2, NG * P, False)
            group_exp(QL, QL % 2, TAIL, False)

            act.wait_ge(o_cw, 2)
            nc.scalar.activation(logits[:, :, :], logits[:, :, :], ACT.Exp).then_inc(o_cexp, 1)
            act.wait_ge(f_d, 4)
            nc.scalar.activation(hT[:, :], hpre[:, :], ACT.Gelu).then_inc(f_a, 1)

            def weights_of(t, b):
                return copy(ex[:, b, :], logits[:, bass.ds(t, 1), :]).then_inc(o_ex, 1)

            def weights_T(st):
                b = st.ring(2)
                act.wait_ge(o_t, st.t + 1)
                if st.after(2):
                    act.wait_ge(o_mm, st.t - 1)
                copy(exT[:, b, :], ps[0:S, (4 + b) * 512:(4 + b) * 512 + P]).then_inc(o_ev, 1)

            def out_step(st):
                if st.after(1):
                    weights_T(st.shift(-1))
                    if not (isinstance(st.t, int) and st.t == FULL):
                        weights_of(st.t + 1, (st.slot + 1) % 2)
            act.wait_ge(o_cw, 5)
            weights_of(0, 0)
            weights_of(1, 1)
            walk(act, FULL, NU, TAIL, out_step)
            weights_T(Step(FULL, FULL // NU, 0, P))

        @block.vector
        def _(dve):
            v = nc.vector
            link = chain_of(dve, s_dve)
            dve.wait_ge(s_edge_in, 64)
            v.memset(e_flag[:, 0:1], 0.0).then_inc(s_copies, 1)
            v.memset(avec[:, :], 0.0).then_inc(s_copies, 1)
            link(v.tensor_copy(e_srcf[:, :], e_src[:, :]))
            link(v.tensor_copy(e_dstf[:, :], e_dst[:, :]))
            link(v.tensor_tensor(e_eq[:, 1:P], e_dstf[:, 1:P], e_dstf[:, 0:P - 1], ALU.not_equal))
            dve.wait_ge(s_copies, 2)
            link(v.tensor_scalar(e_flag[:, 1:P], e_eq[:, 1:P], -BIG, None, ALU.mult))
            dve.wait_ge(s_ident, 2)
            dve.wait_ge(s_pe, 2)
            v.tensor_copy(src_i[:, :], bank(7, ET)).then_inc(s_copies, 1)
            v.tensor_copy(flag_t[:, :], bank(7, ET, 2 * ET)).then_inc(s_copies, 1)
            v.tensor_scalar(dst_i[:, :], bank(7, ET, ET), float(N - 1), None, ALU.min).then_inc(s_copies, 1)
            v.tensor_copy(dst_ti[:, :], bank(7, ET, ET)).then_inc(s_copies, 1)
            link(v.tensor_copy(sel_last[:, :], ident[:, P - 1:P].broadcast_to([P, ET])))
            link(v.tensor_copy(dst_f[:, :], bank(7, ET, ET)))
            dve.wait_ge(s_copies, 6)
            link(v.tensor_scalar(hi_i[:, :], dst_ti[:, :], P.bit_length() - 1, None, ALU.arith_shift_right))
            link(v.tensor_scalar(lo_i[:, :], dst_ti[:, :], P - 1, None, ALU.bitwise_and))
            v.tensor_copy(hi_f[:, :], hi_i[:, :]).then_inc(s_copies, 1)
            v.tensor_copy(lo_f[:, :], lo_i[:, :]).then_inc(s_copies, 1)
            dve.wait_ge(s_pool, POOL_SET)
            v.tensor_copy(iota_f[:, :], iota_i[:, :]).then_inc(s_copies, 1)
            v.tensor_copy(e_basef[:, :], e_base[:, :]).then_inc(s_copies, 1)
            link(v.tensor_scalar(e_eq[:, :], e_dstf[:, :], e_dstf[:, 0:1], None, ALU.is_equal))
            link(v.tensor_reduce(e_cnt[:, :], e_eq[:, :], AX.X, ALU.add))
            dve.wait_ge(s_copies, 10)
            link(v.tensor_tensor(first_end[:, :], e_cnt[:, :], e_basef[:, :], ALU.add))
            dve.wait_ge(s_pe, 3)
            link(v.tensor_scalar(chain[:, :], ps[0:ET, 7 * 512 + 256:7 * 512 + 256 + ET], e_dstf[:, 0:1], None,
                                 ALU.is_equal))
            link(v.tensor_tensor(e_eq[:, 0:ET], tri[:, :], ident[0:ET, 0:ET], ALU.add))
            link(v.tensor_scalar(e_eq[:, 0:ET], e_eq[:, 0:ET], -1.0, 1.0, ALU.mult, ALU.add))
            link(v.tensor_tensor(chain[:, :], chain[:, :], e_eq[:, 0:ET], ALU.mult))
            link(v.tensor_scalar(chain[:, :], chain[:, :], -1.0, BIG, ALU.add, ALU.mult))
            for half in range(2):
                for part in range(2):
                    at = half + part * H
                    link(v.tensor_copy(
                        avec[half * DH:(half + 1) * DH, at:at + (2 * H + 2) * (C - 1) + 1:2 * H + 2],
                        ps[half * DH:(half + 1) * DH, 6 * 512 + at:6 * 512 + part * H + H:2]))
            dve.wait_ge(s_gp, 2)
            dve.wait_ge(s_in, 16 * 7)
            v.tensor_scalar(slots_sq[:, :], slots_sb[:, :], s_norm[:, 2:3], scale_sb[:, :], ALU.mult, ALU.mult)\
                .then_inc(s_slots, 1)
            dve.wait_ge(s_pe, 4)
            link(v.tensor_copy(slT[:, :, :].rearrange("p c s -> p (c s)"), bank(7, C * S)))

            def normalise(st):
                b = st.ring(2)
                dve.wait_ge(a_rstd, st.t + 1)
                if st.after(2):
                    dve.wait_ge(a_tr, st.t - 1)
                v.tensor_scalar(ha[:, b, :], xa[:, st.slot, :], mva[:, b, 0:1], mva[:, b, 3:4], ALU.subtract, ALU.mult)\
                    .then_inc(a_hh, 1)
                v.tensor_copy(table[:, bass.ds(st.t, 1), MEAN:RSTD + 1], mva[:, b, 0:4:3]).then_inc(a_mr, 1)

            def stats_step(st):
                b = st.ring(2)
                dve.wait_ge(xa_in[st.slot], 16 * (st.lap + 1))
                v.bn_stats(bna[:, b, 0:6], xa[:, st.slot, 0:512])
                v.bn_stats(bna[:, b, 6:12], xa[:, st.slot, 512:D]).then_inc(a_bn, 1)
                dve.wait_ge(a_bn, st.t + 1)
                if st.after(2):
                    dve.wait_ge(a_mr, st.t - 1)
                if st.after(1):
                    normalise(st.shift(-1))
                v.bn_aggr(mva[:, b, 0:2], bna[:, b, :]).then_inc(a_mv, 1)
            walk(dve, FULL, NU, TAIL, stats_step)
            normalise(Step(FULL, FULL // NU, 0, P))

            dve.wait_ge(a_tab, NT)
            v.memset(flagT[:, P:P + 1], 0.0).then_inc(e_init, 1)
            v.memset(deg[:, :], 0.0).then_inc(e_init, 1)
            dve.wait_ge(e_init, 2)

            def group(lap, gb, first, early):
                n = lap * 2 + gb
                t0 = lap * XR + gb * EG
                dve.wait_ge(e_tab[gb], 32 * EG * (lap + 1))
                v.tensor_tensor(sc[:, :, :], tg_s[:, gb, :, 0:H], tg_d[:, gb, :, A2:A2 + H], ALU.add).then_inc(e_sc, 1)
                if not early:
                    dve.wait_ge(e_hist, n - 1)
                v.tensor_tensor(hot_lo[:, gb, :, :], lo_f[:, bass.ds(t0, EG)].unsqueeze(2).broadcast_to([P, EG, P]),
                                iota_f[:, :].unsqueeze(1).broadcast_to([P, EG, P]), ALU.is_equal)
                v.tensor_tensor(hot_hi[:, gb, :, :], hi_f[:, bass.ds(t0, EG)].unsqueeze(2).broadcast_to([P, EG, ET]),
                                iota_f[:, 0:ET].unsqueeze(1).broadcast_to([P, EG, ET]), ALU.is_equal).then_inc(e_hot, 1)
                dve.wait_ge(e_sc, n + 1)
                v.scalar_tensor_tensor(lk[:, :, :], sc[:, :, :], SLOPE, sc[:, :, :], ALU.mult, ALU.max).then_inc(e_lk, 1)
                v.tensor_copy(fb[:, :, :], flag_t[:, bass.ds(t0, EG)].unsqueeze(2).broadcast_to([P, EG, H]))\
                    .then_inc(e_fb, 1)
                v.tensor_copy(dsc[:, gb, :], dst_f[:, bass.ds(t0, EG)]).then_inc(e_dsc, 1)
                dve.wait_ge(e_tr, n + 1)
                dve.wait_ge(e_flag_ev, n + 1)
                v.tensor_tensor_scan(pmax[:, :], flagT[:, 0:P], ps[0:EG * H, 4 * 512:4 * 512 + P], -BIG,
                                     ALU.add, ALU.max).then_inc(e_pm, 1)
                dve.wait_ge(e_pm, n + 1)
                v.tensor_tensor_scan(smax[:, ::-1], flagT[:, P:0:-1], pmax[:, ::-1], -BIG,
                                     ALU.add, ALU.max).then_inc(e_sm, 1)
                dve.wait_ge(e_hist, n + 1)
                v.tensor_tensor(deg[:, :], deg[:, :], ps[0:ET, 6 * 512:6 * 512 + P], ALU.add).then_inc(e_deg, 1)
                dve.wait_ge(e_sm, n + 1)
                v.tensor_tensor(dif[:, :], ps[0:EG * H, 4 * 512:4 * 512 + P], smax[:, :], ALU.subtract).then_inc(e_dif, 1)
                if not early:
                    dve.wait_ge(e_mcp, (n - 1) * EG)
                dve.wait_ge(e_back, n + 1)
                v.tensor_copy(eem[:, gb, :, :, :].rearrange("p a k h -> p (a k h)"), bank(5, 2 * EG * H)).then_inc(e_em, 1)
                dve.wait_ge(e_em, n + 1)
                v.tensor_tensor(wt[:, gb, :, :], eem[:, gb, 0, :, :],
                                tg_s[:, gb, :, RSTD:RSTD + 1].broadcast_to([P, EG, H]), ALU.mult).then_inc(e_wt, 1)
                dve.wait_ge(e_row[gb], 16 * (lap + 1))
                dve.wait_ge(e_dsc, n + 1)
                dve.wait_ge(e_wt, n + 1)

                def rows(j):
                    t, b = t0 + j, j % 2
                    if not first or j >= 2:
                        dve.wait_ge(e_mm, t - 1)
                    v.tensor_scalar(same[:, b, :], dst_row[:, gb, j * P:(j + 1) * P], dsc[:, gb, j:j + 1], None,
                                    ALU.is_equal).then_inc(e_same, 1)
                    dve.wait_ge(e_x[gb * EG + j], 16 * (lap + 1))
                    v.scalar_tensor_tensor(
                        vv[:, b, :].rearrange("p (h d) -> p h d", d=DH),
                        xg[:, gb * EG + j, :].rearrange("p (h d) -> p h d", d=DH), tg_s[:, gb, j, MEAN:MEAN + 1],
                        wt[:, gb, j, :].unsqueeze(2).broadcast_to([P, H, DH]), ALU.subtract, ALU.mult)\
                        .then_inc(e_vv, 1)

                def sums(j):
                    t, b = t0 + j, j % 2
                    dve.wait_ge(e_mm, t + 1)
                    v.reciprocal(rl[:, b, :], bank(2 * b + 1, H, D - 512)).then_inc(e_rl, 1)
                    if not first:
                        dve.wait_ge(e_out[j], 16 * n)
                    v.tensor_copy(zo[:, j, D:D + H], bank(2 * b + 1, H, D - 512)).then_inc(e_lcp, 1)
                    dve.wait_ge(e_rl, t + 1)
                    v.tensor_tensor(zo[:, j, 0:D].rearrange("p (d h) -> p h d", h=H),
                                    bank(2 * b, D).rearrange("p (h d) -> p h d", d=DH),
                                    rl[:, b, :].unsqueeze(2).broadcast_to([P, H, DH]), ALU.mult).then_inc(e_z, 1)
                rows(0)
                rows(1)
                sums(0)
                rows(2)
                sums(1)
                rows(3)
                sums(2)
                sums(3)
            group(0, 0, True, True)
            group(0, 1, False, True)
            with dve.Fori(1, LAPS_E) as lap:
                for gb in range(2):
                    group(lap, gb, False, False)

            link = chain_of(dve, b_dve)
            dve.wait_ge(e_deg, GROUPS)
            link(v.tensor_tensor_scan(cum[:, :], ones[0:ET, :], deg[:, :], 0.0, ALU.mult, ALU.add))
            dve.wait_ge(b_pe, 1)
            link(v.tensor_copy(off_sb[:, :], ps[0:ET, 7 * 512:7 * 512 + 1]))
            link(v.tensor_scalar(none[:, :], deg[:, :], 0.0, float(1 << 20), ALU.is_equal, ALU.mult))
            link(v.scalar_tensor_tensor(pos_f[:, :], cum[:, :], off_sb[:, :], none[:, :], ALU.add, ALU.add))
            link(v.tensor_scalar(pos_f[:, :], pos_f[:, :], -1.0, None, ALU.add))
            dve.wait_ge(b_pe, 2)
            link(v.tensor_copy(pos_i[:, :], bank(7, ET, 256)))
            dve.wait_ge(b_in, 16)
            LC, MC = D, D + H
            link(v.tensor_tensor(bd[:, :, :], rr[:, MC:MC + H].unsqueeze(2).broadcast_to([ET, H, ET]),
                                 ident[0:ET, 0:ET].unsqueeze(1).broadcast_to([ET, H, ET]), ALU.mult))
            dve.wait_ge(b_pe, 3)
            HH = H // 2
            for i in range(2):
                link(v.tensor_tensor(bm[:, i * HH:(i + 1) * HH, :],
                                     ps[0:ET, i * 512:i * 512 + HH * ET].rearrange("k (h j) -> k h j", j=ET),
                                     chain[:, :].unsqueeze(1).broadcast_to([ET, HH, ET]), ALU.add))
            link(v.tensor_reduce(bmax[:, :], bm[:, :, :], AX.X, ALU.max))
            dve.wait_ge(b_ff, 16)
            link(v.tensor_tensor(bmax[:, :], bmax[:, :], ff[:, MC:MC + H], ALU.max))
            link(v.tensor_tensor(bm[:, :, :], bm[:, :, :], bmax[:, :].unsqueeze(2).broadcast_to([ET, H, ET]),
                                 ALU.subtract))
            link(v.tensor_tensor(bdf[:, :], ff[:, MC:MC + H], bmax[:, :], ALU.subtract))
            dve.wait_ge(b_pe, 4)
            for i in range(2):
                link(v.tensor_tensor(bwT[:, i * HH:(i + 1) * HH, :],
                                     ps[0:ET, (2 + i) * 512:(2 + i) * 512 + HH * ET]
                                     .rearrange("j (h k) -> j h k", k=ET),
                                     rr[:, LC + i * HH:LC + (i + 1) * HH].unsqueeze(2).broadcast_to([ET, HH, ET]),
                                     ALU.mult))
            dve.wait_ge(b_act, 2)
            link(v.tensor_tensor(bcf[:, :], bcf[:, :], ff[:, LC:LC + H], ALU.mult))
            dve.wait_ge(b_pe, 5)
            link(v.tensor_tensor(btot[:, :], bcf[:, :], ps[0:ET, 6 * 512:6 * 512 + H], ALU.add))
            link(v.reciprocal(btot[:, :], btot[:, :]))
            link(v.tensor_tensor(bcf[:, :], bcf[:, :], btot[:, :], ALU.mult))
            fz = ff[:, 0:D].rearrange("k (d h) -> k h d", h=H)
            bzv = bz[:, :].rearrange("k (h d) -> k h d", d=DH)
            link(v.tensor_tensor(fz, fz, bcf[:, :].unsqueeze(2).broadcast_to([ET, H, DH]), ALU.mult))
            link(v.tensor_tensor(bzv, ps[0:ET, 4 * 512:4 * 512 + D].rearrange("k (h d) -> k h d", d=DH),
                                 btot[:, :].unsqueeze(2).broadcast_to([ET, H, DH]), ALU.mult))
            link(v.tensor_tensor(fz, fz, bzv, ALU.add))

            dve.wait_ge(b_fix, 16)
            v.memset(yT[:, :, :], 0.0).then_inc(g_init, 1)
            v.memset(mrun[:, 1, :], -BIG).then_inc(g_init, 1)
            v.memset(lrun[:, :], 0.0).then_inc(g_init, 1)
            dve.wait_ge(g_init, 3)

            def hh(st):
                r = st.ring(3)
                dve.wait_ge(n_x[r], 16 * st.div(3) + 16)
                dve.wait_ge(n_mr, st.t + 1)
                if st.after(3):
                    dve.wait_ge(n_t1, st.t - 2)
                v.tensor_scalar(cat[:, r, 0:D].rearrange("p (d h) -> p h d", h=H),
                                xn[:, r, :].rearrange("p (h d) -> p h d", d=DH), mr[:, r, 0:1], mr[:, r, 1:2],
                                ALU.subtract, ALU.mult).then_inc(n_hh, 1)

            def ev2(st):
                dve.wait_ge(n_t1, st.t + 1)
                if st.after(1):
                    dve.wait_ge(n_mm, st.t)
                v.tensor_copy(catT[:, 1024:H * P], bank(2)).then_inc(n_ev2, 1)

            def logits_of(st):
                r = st.ring(3)
                dve.wait_ge(n_lg, st.t + 1)
                dve.wait_ge(n_tok, st.t + 1)
                if st.after(3):
                    dve.wait_ge(g_lt, st.div(3))
                    dve.wait_ge(n_keep, st.t - 2)
                v.tensor_scalar(lg[:, r, :], bank(5, S), tok[:, r, :], None, ALU.mult).then_inc(n_L, 1)

            def group_max(q, par, cols):
                dve.wait_ge(g_lt, q + 1)
                v.tensor_reduce(gmax[:, :], ps[0:S, 6 * 512:6 * 512 + cols], AX.X, ALU.max).then_inc(g_max, 1)
                dve.wait_ge(g_max, q + 1)
                v.tensor_tensor(mrun[:, par, :], mrun[:, 1 - par, :], gmax[:, :], ALU.max).then_inc(g_new, 1)
                dve.wait_ge(g_new, q + 1)
                v.tensor_scalar(nneg[:, :], mrun[:, par, :], -1.0, None, ALU.mult).then_inc(g_neg, 1)

            def group_scale(q, first):
                dve.wait_ge(g_exp, q + 1)
                dve.wait_ge(g_c, q + 1)
                if not first:
                    dve.wait_ge(g_l, q)
                v.scalar_tensor_tensor(lrun[:, :], lrun[:, :], cc[:, :], dsum[:, :], ALU.mult, ALU.add).then_inc(g_l, 1)
                v.tensor_scalar(cdiag[:, :], ident[0:S, 0:S], cc[:, :], None, ALU.mult).then_inc(g_cd, 1)

            def group_weights(q, tiles, rows, s0):
                dve.wait_ge(g_back, q + 1)
                dve.wait_ge(n_gam, q * NG + tiles)
                v.tensor_tensor(pg[0:rows, 0:tiles, :],
                                ps[0:rows, 6 * 512:6 * 512 + tiles * S].rearrange("p (k s) -> p k s", s=S),
                                gam[0:rows, s0:s0 + tiles, :].broadcast_to([rows, tiles, S]), ALU.mult).then_inc(g_pg, 1)

            def group_sum(q):
                dve.wait_ge(g_y, q + 1)
                v.tensor_tensor(ytmp[:, :, :], yT[:, :, :],
                                bank(6, S, NG * S).unsqueeze(1).broadcast_to([P, C, S]), ALU.mult).then_inc(g_ym, 1)
                dve.wait_ge(g_ym, q + 1)
                v.tensor_tensor(yT[:, :, :].rearrange("p c s -> p (c s)"), ytmp[:, :, :].rearrange("p c s -> p (c s)"),
                                bank(7, C * S), ALU.add).then_inc(g_ya, 1)

            def node_step(st):
                r, k = st.ring(3), st.slot % NG
                tail = isinstance(st.t, int) and st.t == FULL
                if not tail:
                    hh(st.shift(1))
                dve.wait_ge(n_mm, st.t + 1)
                if st.after(3):
                    dve.wait_ge(n_st[r], 16 * st.div(3))
                v.scalar_tensor_tensor(x1[:, r, :], bank(3, D), 0.0, xn[:, r, :], ALU.max, ALU.add).then_inc(n_x1, 1)
                dve.wait_ge(n_x1, st.t + 1)
                v.bn_stats(bnn[:, 0:6], x1[:, r, 0:512])
                v.bn_stats(bnn[:, 6:12], x1[:, r, 512:D]).then_inc(n_bn, 1)
                dve.wait_ge(n_bn, st.t + 1)
                if st.after(1):
                    logits_of(st.shift(-1))
                v.bn_aggr(mvn[:, r, :], bnn[:, :]).then_inc(n_mv, 1)
                if k == 2 and st.after(5):
                    group_scale(st.div(3) - 1, isinstance(st.t, int) and st.t < 6)
                if st.after(6):
                    dve.wait_ge(g_y, st.div(3) - 1)
                dve.wait_ge(n_mv, st.t + 1)
                v.scalar_tensor_tensor(uu[:, st.slot, :], x1[:, r, :], mvn[:, r, 0:1], wn[:, :],
                                       ALU.subtract, ALU.mult).then_inc(n_u, 1)
                if not tail:
                    ev2(st.shift(1))
                if k == 0 and st.after(6):
                    group_sum(st.div(3) - 2)
                if k == 1 and st.after(4):
                    group_max(st.div(3) - 1, (st.slot // NG + 1) % 2, NG * P)
                if k == 2 and st.after(5):
                    group_weights(st.div(3) - 1, NG, P, (st.slot + 1) % NU)

            hh(Step(0, 0, 0, P))
            ev2(Step(0, 0, 0, P))
            walk(dve, FULL, NU, TAIL, node_step)
            logits_of(Step(FULL, FULL // NU, 0, P))
            QL = FULL // NG
            group_max(QL - 1, (QL - 1) % 2, NG * P)
            group_scale(QL - 1, False)
            group_weights(QL - 1, NG, P, NG)
            group_sum(QL - 1)
            group_max(QL, QL % 2, TAIL)
            group_scale(QL, False)
            group_weights(QL, 1, TAIL, 0)
            group_sum(QL)

            link = chain_of(dve, f_d)
            dve.wait_ge(g_l, QL + 1)
            dve.wait_ge(g_ya, QL + 1)
            link(v.reciprocal(rlr[:, :], lrun[:, :]))
            link(v.tensor_scalar(cdiag[:, :], ident[0:S, 0:S], rlr[:, :], None, ALU.mult))
            dve.wait_ge(f_p, 1)
            link(v.tensor_tensor(yT[:, :, :], yT[:, :, :], bank(5, S).unsqueeze(1).broadcast_to([P, C, S]),
                                 ALU.mult))
            cw = chain_of(dve, o_cw)
            dve.wait_ge(n_keep, NT)
            cw(v.tensor_reduce(tmax[:, :], logits[:, :, :], AX.X, ALU.max))
            cw(v.tensor_tensor(logits[:, :, :], logits[:, :, :], tmax[:, :].unsqueeze(2).broadcast_to([P, NT, S]),
                               ALU.subtract))
            dve.wait_ge(o_cexp, 1)
            cw(v.tensor_reduce(tsum[:, :], logits[:, :, :], AX.X, ALU.add))
            cw(v.reciprocal(tsum[:, :], tsum[:, :]))
            cw(v.tensor_tensor(logits[:, :, :], logits[:, :, :], tsum[:, :].unsqueeze(2).broadcast_to([P, NT, S]),
                               ALU.mult))
            dve.wait_ge(f_in, 32)
            dve.wait_ge(f_h, S // 2)
            link(v.tensor_tensor(hpre[:, :], ps[0:F, 0:S], b1_sb[:, :], ALU.add))
            dve.wait_ge(f_y, S // 2)
            link(v.tensor_copy(y2T[:, :], bank(1, C * S)))
            dve.wait_ge(f_p, 2)
            link(v.tensor_tensor(y2[:, :], ps[0:S, 2 * 512:2 * 512 + D], b2_sb[:, :], ALU.add))

            def out_step(st):
                b = st.ring(2)
                dve.wait_ge(o_x[st.slot], 16 * (st.lap + 1))
                if st.after(3):
                    dve.wait_ge(o_out[st.ring(3)], 16 * st.div(3))
                dve.wait_ge(o_mm, st.t + 1)
                v.tensor_tensor(oo[:, st.ring(3), :], bank(2 * b, D), xo[:, st.slot, :], ALU.add).then_inc(o_o, 1)
            walk(dve, FULL, NU, TAIL, out_step)


def kernel(**inputs):
    import numpy as _np
    import concourse.bacc as _bacc
    from concourse import mybir as _mybir
    from concourse.bass_utils import run_bass_kernel_spmd as _run

    a = {k: _np.asarray(v) for k, v in inputs.items()}
    arrays = {
        "x": a["x"], "src": a["src"], "dst": a["dst"],
        "w_cat": _np.concatenate([a["L0_gnn_W_res"].T, a["L0_gnn_W_fc"].T], axis=0),
        "w_fc": a["L0_gnn_W_fc"],
        "attn": _np.concatenate([a["L0_gnn_attn_l"].T, a["L0_gnn_attn_r"].T], axis=1),
        "slots": a["L0_ffn_slots"], "scale": a["L0_ffn_scale"],
        "w1": a["L0_ffn_fc1_weight"], "b1t": a["L0_ffn_fc1_bias"].T,
        "w2": a["L0_ffn_fc2_weight"], "b2": a["L0_ffn_fc2_bias"], "norm_w": a["L0_ffn_norm_weight"],
    }
    arrays = {k: _np.ascontiguousarray(v) for k, v in arrays.items()}
    nc = _bacc.Bacc("TRN2", target_bir_lowering=False, num_devices=1)
    args = [nc.dram_tensor(k, v.shape, _mybir.dt.from_np(v.dtype), kind="ExternalInput").ap()
            for k, v in arrays.items()]
    out = nc.dram_tensor("out", a["x"].shape, F32, kind="ExternalOutput").ap()
    build(nc, *args, out)
    r = _run(nc, [arrays], core_ids=[0])
    return r.results[0]["out"]
```

```python
import concourse.bass as bass
from concourse import mybir
from concourse.alu_op_type import AluOpType as ALU
from contextlib import ExitStack

F32 = mybir.dt.float32
BF16 = mybir.dt.bfloat16
I32 = mybir.dt.int32
ACT = mybir.ActivationFunctionType
AX = mybir.AxisListType

P = 128
LAP = 6
BIG = 1.0e38
EPS = 1e-5
SLOPE = 0.2
TAB = 16
SHIFT, RSTD = 12, 13


class Step:

    def __init__(self, t, lap, slot, rows):
        self.t, self.lap, self.slot, self.rows = t, lap, slot, rows

    def ring(self, depth):
        return self.slot % depth

    def div(self, depth):
        return self.lap * (LAP // depth) + self.slot // depth

    def after(self, depth):
        return not isinstance(self.t, int) or self.t >= depth

    def shift(self, by):
        over = (self.slot + by) // LAP
        return Step(self.t + by, self.lap + over, (self.slot + by) % LAP, P)


def ring_uses(tiles, depth, slot):
    return (tiles - slot + depth - 1) // depth


def walk(eng, full, unroll, tail_rows, body):
    for t in range(unroll):
        body(Step(t, 0, t, P))
    with eng.Fori(1, full // unroll) as lap:
        for k in range(unroll):
            body(Step(lap * unroll + k, lap, k, P))
    if tail_rows:
        body(Step(full, full // unroll, 0, tail_rows))


def build(nc, x, src, dst, w_cat, w_fc, attn, slots, scale, w1, b1, w2, b2, norm_w, out):
    N, D = x.shape
    H, DH = attn.shape[1] // 2, w_fc.shape[0]
    S, _, F = w1.shape
    FULL, TAIL = N // P, N % P
    NT = FULL + 1
    C = D // P
    ET = 80
    EG = 4
    GROUPS = ET // EG
    PAD_NODE = ET * P - 1
    ROW = D + 2 * H
    NU = LAP
    HD = D // 2
    G = 4
    GR = P // G
    QUADS = S // G
    FC = 2 * DH + 4
    A1C, A2C = 2 * DH, 2 * DH + 2
    WIDE = C * FC
    POOL_SET = 10
    NG = 3
    LAPS_E = ET // (2 * EG)
    E_FULL, E_TAIL = src.shape[0] // P, src.shape[0] % P

    node_rows = nc.dram_tensor("node_rows", (N, WIDE), F32).ap()
    node_table = nc.dram_tensor("node_table", (N, TAB), F32).ap()
    seg_rows = nc.dram_tensor("seg_rows", (ET * P, ROW), F32).ap()
    dst_padded = nc.dram_tensor("dst_padded", (ET, P), I32).ap()
    x1_dram = nc.dram_tensor("x1_dram", (N, D), F32).ap()

    ctx = ExitStack()
    with ctx:
        def sb(name, shape, dt=F32):
            return ctx.enter_context(nc.sbuf_tensor(name, shape, dt))

        def sem(name):
            return ctx.enter_context(nc.semaphore(name))

        ident = sb("ident", [P, P])
        wres = sb("wres", [P, P])
        wfc = sb("wfc", [P, C, FC])
        slT = sb("slT", [P, C, S])
        wn = sb("wn", [P, D])
        table = sb("table", [P, NT + 1, TAB])
        logits = sb("logits", [P, NT, S])
        src_i = sb("src_i", [P, ET], I32)
        dst_i = sb("dst_i", [P, ET], I32)
        dst_f = sb("dst_f", [P, ET])
        hi_f = sb("hi_f", [P, ET])
        lo_f = sb("lo_f", [P, ET])
        iota_f = sb("iota_f", [P, P])
        flag_t = sb("flag_t", [P, ET])
        pos_i = sb("pos_i", [P, ET], I32)
        first_end = sb("first_end", [ET, 1], I32)
        chain = sb("chain", [ET, ET])
        tri = sb("tri", [ET, ET])
        kc = sb("kc", [P, 4])
        ones = sb("ones", [P, P])
        ident_b = sb("ident_b", [P, P], BF16)
        yT = sb("yT", [P, C, S])
        rlr = sb("rlr", [P, 1])
        zeros = sb("zeros", [P, G, C])
        w1b = sb("w1b", [P, 2, G, C * F])
        w2b = sb("w2b", [F, 2, G, D])
        yw = sb("yw", [P, 2, G, C, GR])
        hw = sb("hw", [F, 2, G, GR])
        tmax = sb("tmax", [P, NT])
        tsum = sb("tsum", [P, NT])

        ph = ExitStack()

        def scratch(name, shape, dt=F32):
            return ph.enter_context(nc.sbuf_tensor(name, shape, dt))

        e_src = scratch("e_src", [ET, P], I32)
        e_dst = scratch("e_dst", [ET, P], I32)
        e_srcf = scratch("e_srcf", [ET, P])
        e_dstf = scratch("e_dstf", [ET, P])
        e_flag = scratch("e_flag", [ET, P])
        e_eq = scratch("e_eq", [ET, P])
        e_cnt = scratch("e_cnt", [ET, 1])
        e_base = scratch("e_base", [ET, 1], I32)
        e_basef = scratch("e_basef", [ET, 1])
        sel_last = scratch("sel_last", [P, ET])
        dst_ti = scratch("dst_ti", [P, ET], I32)
        hi_i = scratch("hi_i", [P, ET], I32)
        lo_i = scratch("lo_i", [P, ET], I32)
        iota_i = scratch("iota_i", [P, P], I32)
        wfc2 = scratch("wfc2", [DH, 2 * DH])
        wfcT = scratch("wfcT", [P, DH])
        frow = scratch("frow", [P, NU, WIDE])
        attn_sb = scratch("attn_sb", [DH, 2 * H])
        slots_sb = scratch("slots_sb", [S, D])
        slots_sq = scratch("slots_sq", [S, D])
        scale_sb = scratch("scale_sb", [S, 1])
        s_norm = scratch("s_norm", [S, 4])
        xa = scratch("xa", [P, 6, D])
        ha = scratch("ha", [P, 2, D])
        haT = scratch("haT", [P, 2, D])
        bna = scratch("bna", [P, 2, 12])
        mva = scratch("mva", [P, 2, 4])
        ph.close()

        ph = ExitStack()
        XR = 2 * EG
        dst_row = scratch("dst_row", [P, 2, EG * P], I32)
        ix_s = scratch("ix_s", [P, 2, EG], I32)
        ix_d = scratch("ix_d", [P, 2, EG], I32)
        tg_d = scratch("tg_d", [P, 2, EG, TAB])
        dsc = scratch("dsc", [P, 2, EG])
        sc = scratch("sc", [P, EG, H])
        lk = scratch("lk", [P, EG, H])
        fb = scratch("fb", [P, EG, H])
        flagT = scratch("flagT", [EG * H, P + 1])
        pmax = scratch("pmax", [EG * H, P])
        smax = scratch("smax", [EG * H, P])
        dif = scratch("dif", [EG * H, P])
        eeT = scratch("eeT", [EG * H, P])
        eem = scratch("eem", [P, 2, 2, EG, H])
        hot_hi = scratch("hot_hi", [P, 2, EG, ET], BF16)
        hot_lo = scratch("hot_lo", [P, 2, EG, P], BF16)
        deg = scratch("deg", [ET, P])
        xg = scratch("xg", [P, XR, WIDE])
        vv = scratch("vv", [P, 2, D])
        same = scratch("same", [P, 2, P])
        rl = scratch("rl", [P, 2, H])
        zo = scratch("zo", [P, 4, ROW])
        cum = scratch("cum", [ET, P])
        none = scratch("none", [ET, P])
        off_sb = scratch("off_sb", [ET, 1])
        pos_f = scratch("pos_f", [ET, P])
        rr = scratch("rr", [ET, ROW])
        ff = scratch("ff", [ET, ROW])
        bd = scratch("bd", [ET, H, ET])
        bm = scratch("bm", [ET, H, ET])
        be = scratch("be", [ET, H, ET])
        bwT = scratch("bwT", [ET, H, ET])
        bmax = scratch("bmax", [ET, H])
        bdf = scratch("bdf", [ET, H])
        bcf = scratch("bcf", [ET, H])
        btot = scratch("btot", [ET, H])
        bz = scratch("bz", [ET, D])
        ph.close()

        ph = ExitStack()
        xn = scratch("xn", [P, 3, D])
        ixn = scratch("ixn", [P, 3, 1], I32)
        mr = scratch("mr", [P, 3, 2])
        hn = scratch("hn", [P, 3, D])
        hnT = scratch("hnT", [P, D])
        agg = scratch("agg", [P, 3, ROW])
        gat = scratch("gat", [P, D])
        x1 = scratch("x1", [P, 3, D])
        uu = scratch("uu", [P, NU, D])
        usq = scratch("usq", [P, D])
        uT = scratch("uT", [P, D])
        bnn = scratch("bnn", [P, 12])
        mvn = scratch("mvn", [P, 3, 2])
        usum = scratch("usum", [P, 3, 1])
        gam = scratch("gam", [P, NU, 1])
        pw = scratch("pw", [P, 6])
        tok = scratch("tok", [P, 3, 1])
        lg = scratch("lg", [P, 3, S])
        mrun = scratch("mrun", [S, 2, 1])
        nneg = scratch("nneg", [S, 1])
        gmax = scratch("gmax", [S, 1])
        cc = scratch("cc", [P, 1])
        dT = scratch("dT", [S, NG * P])
        dsum = scratch("dsum", [S, 1])
        lrun = scratch("lrun", [S, 1])
        pg = scratch("pg", [P, NG, S])
        ysum = scratch("ysum", [P, HD])
        ph.close()

        ph = ExitStack()
        e12 = scratch("e12", [P, NT, P], BF16)
        e13 = scratch("e13", [P, NT, P], BF16)
        b1_sb = scratch("b1_sb", [P, F])
        hpre = scratch("hpre", [P, F])
        hact = scratch("hact", [P, F])
        hT = scratch("hT", [F, P])
        b2_sb = scratch("b2_sb", [P, D])
        y2 = scratch("y2", [P, D])
        yf = scratch("yf", [P, D])
        y_a = scratch("y_a", [P, D], BF16)
        y_b = scratch("y_b", [P, D], BF16)
        y_c = scratch("y_c", [P, D], BF16)
        xo = scratch("xo", [P, 6, D])
        oo = scratch("oo", [P, 3, D])
        exT = scratch("exT", [P, 2, 2 * P], BF16)
        ph.close()

        ps = ctx.enter_context(nc.psum_tensor("ps", [P, 8 * 512], F32))

        def bank(b, n=512, at=0):
            return ps[:, b * 512 + at:b * 512 + at + n]

        def sems(names):
            return [sem(n) for n in names.split()]

        s_in, s_edge_in, s_edge_pad, s_dstp, s_ident, s_pool = sems("s_in s_edge_in s_edge_pad s_dstp s_ident s_pool")
        s_dve, s_pe, s_gp = sems("s_dve s_pe s_gp")
        s_copies, s_sq, s_slots = sems("s_copies s_sq s_slots")

        xa_in = [sem(f"xa_in_{i}") for i in range(6)]
        a_bn, a_mv, a_ve, a_rstd, a_hh, a_mr, a_tr, a_ev, a_att, a_row, a_tab, a_out = sems(
            "a_bn a_mv a_ve a_rstd a_hh a_mr a_tr a_ev a_att a_row a_tab a_out")
        a_st = [sem(f"a_st_{i}") for i in range(NU)]

        e_row = [sem(f"e_row_{i}") for i in range(2)]
        e_tab = [sem(f"e_tab_{i}") for i in range(2)]
        e_x = [sem(f"e_x_{i}") for i in range(XR)]
        e_out = [sem(f"e_out_{i}") for i in range(4)]
        e_ix, e_sc, e_lk, e_fb, e_dsc, e_tr, e_flag_ev, e_pm, e_sm, e_dif = sems(
            "e_ix e_sc e_lk e_fb e_dsc e_tr e_flag_ev e_pm e_sm e_dif")
        e_exp, e_back, e_em, e_hot, e_hist, e_deg, e_init = sems(
            "e_exp e_back e_em e_hot e_hist e_deg e_init")
        e_vv, e_same, e_mm, e_rl, e_z, e_lcp, e_mcp, e_go = sems("e_vv e_same e_mm e_rl e_z e_lcp e_mcp e_go")
        b_in, b_ff, b_fix, b_dve, b_pe, b_act = sems("b_in b_ff b_fix b_dve b_pe b_act")

        n_x = [sem(f"n_x_{i}") for i in range(3)]
        n_ag = [sem(f"n_ag_{i}") for i in range(3)]
        n_st = [sem(f"n_st_{i}") for i in range(3)]
        n_ix, n_mr, n_hh, n_t1, n_ev1, n_mm, n_sum, n_x1, n_bn, n_mv, n_u, n_sq = sems(
            "n_ix n_mr n_hh n_t1 n_ev1 n_mm n_sum n_x1 n_bn n_mv n_u n_sq")
        n_t3, n_ev3, n_lg, n_pw, n_gam, n_tok, n_L, n_keep, n_go = sems(
            "n_t3 n_ev3 n_lg n_pw n_gam n_tok n_L n_keep n_go")
        g_init, g_lt, g_max, g_new, g_neg, g_exp, g_c, g_cd, g_back, g_pg, g_y, g_l, g_ya = sems(
            "g_init g_lt g_max g_new g_neg g_exp g_c g_cd g_back g_pg g_y g_l g_ya")
        f_in, f_d, f_p, f_a, f_h, f_y, f_win, f_hwin, f_zero, f_yf = sems("f_in f_d f_p f_a f_h f_y f_win f_hwin f_zero f_yf")
        f_w1 = [sem(f"f_w1_{i}") for i in range(2)]
        f_w2 = [sem(f"f_w2_{i}") for i in range(2)]
        o_x = [sem(f"o_x_{i}") for i in range(6)]
        o_out = [sem(f"o_out_{i}") for i in range(3)]
        o_cw, o_cexp, o_ex, o_t, o_ev, o_mm, o_o = sems("o_cw o_cexp o_ex o_t o_ev o_mm o_o")

        IN_DMAS = 16 * 10

        def tile_rows(st):
            return bass.ds(st.t * P, st.rows)

        CW = 10
        F_OUT = 14

        def chain_of(eng, s, start=0):
            n = [start]

            def link(ins):
                n[0] += 1
                ins.then_inc(s, 1)
                eng.wait_ge(s, n[0])
            return link

        block = ctx.enter_context(nc.Block())


        @block.sync
        def _(sp):
            sp.wait_ge(s_edge_pad, 2)
            for buf, lst in ((e_src, src), (e_dst, dst)):
                sp.dma_start(buf[0:E_FULL, :], lst[0:E_FULL * P].rearrange("(k p) -> k p", p=P)).then_inc(s_edge_in, 16)
                sp.dma_start(buf[E_FULL:E_FULL + 1, 0:E_TAIL],
                             lst[E_FULL * P:].rearrange("(a p) -> a p", a=1)).then_inc(s_edge_in, 16)
            sp.dma_start(wfc2[:, 0:DH], w_fc[:, :]).then_inc(s_in, 16)
            sp.dma_start(wfc2[:, DH:2 * DH], w_fc[:, :]).then_inc(s_in, 16)
            sp.dma_start(attn_sb[:, :], attn[:, :]).then_inc(s_in, 16)
            for half in range(2):
                rows = slice(half * DH, (half + 1) * DH)
                sp.dma_start(wfcT[rows, :], w_cat[DH:2 * DH, :]).then_inc(s_in, 16)
            sp.wait_ge(s_edge_pad, 3)
            for half in range(2):
                rows = slice(half * DH, (half + 1) * DH)
                sp.dma_start(wres[rows, rows], w_cat[0:DH, :]).then_inc(s_in, 16)
            sp.dma_start(slots_sb[:, :], slots[:, :]).then_inc(s_in, 16)
            sp.dma_start(scale_sb[:, :], scale.rearrange("(s a) -> s a", a=1)).then_inc(s_in, 16)
            sp.dma_start(wn[:, :], norm_w.partition_broadcast(P)).then_inc(s_in, 16)
            sp.wait_ge(s_edge_in, 64)
            sp.dma_start(dst_padded[:, :], e_dst[:, :]).then_inc(s_dstp, 16)

            def load_x(st):
                if st.after(6):
                    sp.wait_ge(a_hh, st.t - 5)
                sp.dma_start(xa[0:st.rows, st.slot, :], x[tile_rows(st), :]).then_inc(xa_in[st.slot], 16)

            def store_row(st):
                sp.wait_ge(a_row, st.t + 1)
                sp.dma_start(node_rows[tile_rows(st), :], frow[0:st.rows, st.slot, :]).then_inc(a_st[st.slot], 16)

            def stats_io(st):
                load_x(st)
                if st.after(NU):
                    store_row(st.shift(-NU))
            walk(sp, FULL, NU, TAIL, stats_io)
            for t in range(NT - NU, NT):
                store_row(Step(t, t // NU, t % NU, P if t < FULL else TAIL))

            sp.wait_ge(s_dstp, 16)
            sp.wait_ge(a_tab, NT)
            for i in range(NU):
                sp.wait_ge(a_st[i], 16 * ring_uses(NT, NU, i))

            def row_in(lap, gb):
                sp.dma_start(dst_row[:, gb, :],
                             dst_padded[bass.ds(lap * 2 * EG + gb * EG, EG), :]
                             .rearrange("k p -> (k p)").partition_broadcast(P)).then_inc(e_row[gb], 16)

            def rows_out(lap, k):
                t = lap * XR + k
                sp.wait_ge(e_z, t + 1)
                sp.wait_ge(e_lcp, t + 1)
                sp.wait_ge(e_mcp, t + 1)
                sp.dma_start(seg_rows[bass.ds(t * P, P), :], zo[:, k % 4, :]).then_inc(e_out[k % 4], 16)

            row_in(0, 0)
            row_in(0, 1)
            for k in range(XR):
                rows_out(0, k)
            with sp.Fori(1, LAPS_E) as lap:
                for k in range(XR):
                    if k % EG == 0:
                        sp.wait_ge(e_same, (lap - 1) * XR + k + EG)
                        row_in(lap, k // EG)
                    rows_out(lap, k)
            for j in range(4):
                sp.wait_ge(e_out[j], 16 * (ET // 4))
            sp.dma_start(rr[:, :], seg_rows.rearrange("(k p) r -> k p r", p=P)[:, P - 1, :]).then_inc(b_in, 16)

            sp.wait_ge(b_fix, 16)

            def store_x1(st):
                sp.wait_ge(n_x1, st.t + 1)
                sp.dma_start(x1_dram[tile_rows(st), :], x1[0:st.rows, st.ring(3), :]).then_inc(n_st[st.ring(3)], 16)

            def nodes_io(st):
                if st.after(3):
                    store_x1(st.shift(-3))
                sp.dma_start(xn[0:st.rows, st.ring(3), :], x[tile_rows(st), :]).then_inc(n_x[st.ring(3)], 16)
                if isinstance(st.t, int) and 2 <= st.t < 6:
                    (load_w1 if st.t % 2 else load_w2)(0, st.t // 2 - 1)

            def load_w1(lap, k):
                sp.dma_start(w1b[:, k, :, :], w1[bass.ds(lap * 2 * G + k * G, G)]
                             .rearrange("s (p c) f -> p s (c f)", p=P)).then_inc(f_w1[k], 16)

            def load_w2(lap, k):
                sp.dma_start(w2b[:, k, :, :], w2[bass.ds(lap * 2 * G + k * G, G)]
                             .rearrange("s f d -> f s d")).then_inc(f_w2[k], 16)

            walk(sp, FULL, NU, TAIL, nodes_io)
            for t in range(NT - 3, NT):
                store_x1(Step(t, t // NU, t % NU, P if t < FULL else TAIL))
                if t == NT - 3:
                    sp.dma_start(xn[:, NT % 3, :], x[N - P:N, :]).then_inc(n_x[NT % 3], 16)
            with sp.Fori(1, QUADS // 2) as lap:
                for k in range(2):
                    sp.wait_ge(f_h, lap * 2 + k - 1)
                    load_w1(lap, k)
            sp.wait_ge(f_zero, 5)
            for j in range(G):
                for buf, vec in ((b1_sb, b1), (b2_sb, b2)):
                    sp.dma_start(buf[j * GR:j * GR + QUADS, :], vec.rearrange("(i j) f -> j i f", j=G)[j]).then_inc(f_in, 16)
            with sp.Fori(1, QUADS // 2) as lap:
                for k in range(2):
                    sp.wait_ge(f_y, lap * 2 + k - 1)
                    load_w2(lap, k)
            sp.wait_ge(f_d, F_OUT)
            for half in range(2):
                for j in range(G):
                    sp.dma_start(yf[half * S + j:half * S + S:G, :], y2[j * GR:j * GR + QUADS, :]).then_inc(f_yf, 16)

            def store_out(st):
                sp.wait_ge(o_o, st.t + 1)
                sp.dma_start(out[tile_rows(st), :], oo[0:st.rows, st.ring(3), :]).then_inc(o_out[st.ring(3)], 16)
            walk(sp, FULL, NU, TAIL, store_out)
            for i in range(3):
                sp.wait_ge(o_out[i], 16 * ring_uses(NT, 3, i))

        @block.gpsimd
        def _(g):
            g.memset(e_src[:, :], 0).then_inc(s_edge_pad, 1)
            g.memset(e_dst[:, :], PAD_NODE).then_inc(s_edge_pad, 1)
            g.memset(wres[:, :], 0.0).then_inc(s_edge_pad, 1)
            g.memset(ident[:, :], 0.0).then_inc(s_ident, 1)
            for i, v in enumerate((-0.5, EPS, 1.0 + EPS, EPS * EPS)):
                g.memset(kc[:, i:i + 1], v).then_inc(s_pool, 1)
            g.memset(ones[:, :], 1.0).then_inc(s_pool, 1)
            g.iota(iota_i[:, :], pattern=[[1, P]], base=0, channel_multiplier=0).then_inc(s_pool, 1)
            g.iota(e_base[:, :], pattern=[[0, 1]], base=-1, channel_multiplier=P).then_inc(s_pool, 1)
            g.memset(tri[:, :], 1.0).then_inc(s_pool, 1)
            g.memset(table[:, :, :], 0.0).then_inc(s_pool, 1)
            g.wait_ge(s_ident, 1)
            g.affine_select(out=ident[:, :], in_=ident[:, :], compare_op=ALU.not_equal, fill=1.0, base=0,
                            pattern=[[-1, P]], channel_multiplier=1).then_inc(s_ident, 1)
            g.wait_ge(s_pool, POOL_SET - 1)
            g.affine_select(out=tri[:, :], in_=tri[:, :], compare_op=ALU.is_gt, fill=0.0, base=0,
                            pattern=[[1, ET]], channel_multiplier=-1).then_inc(s_pool, 1)
            g.wait_ge(s_sq, 1)
            g.tensor_scalar(s_norm[:, 1:2], s_norm[:, 0:1], EPS * EPS, None, ALU.max).then_inc(s_gp, 1)
            g.wait_ge(s_gp, 1)
            g.tensor_tensor(s_norm[:, 2:3], s_norm[:, 1:2], kc[0:S, 0:1], ALU.pow).then_inc(s_gp, 1)

            def rstd(st):
                b = st.ring(2)
                g.wait_ge(a_mv, st.t + 1)
                g.tensor_tensor(mva[:, b, 2:3], mva[:, b, 1:2], kc[:, 1:2], ALU.add).then_inc(a_ve, 1)
                g.wait_ge(a_ve, st.t + 1)
                g.tensor_tensor(mva[:, b, 3:4], mva[:, b, 2:3], kc[:, 0:1], ALU.pow).then_inc(a_rstd, 1)
            walk(g, FULL, NU, TAIL, rstd)

            g.wait_ge(a_tab, NT)
            g.wait_ge(a_out, 16 * (FULL // NU + 1))

            for i in range(NU):
                g.wait_ge(a_st[i], 16 * ring_uses(NT, NU, i))

            def group_rows(lap, gb, first):
                if not first:
                    for j in range(EG):
                        g.wait_ge(e_x[gb * EG + j], lap * 16)
                    g.wait_ge(e_tab[gb], lap * 16 * EG)
                    g.sem_inc(e_go, 1)
                base = lap * XR + gb * EG
                g.tensor_copy(ix_s[:, gb, :], src_i[:, bass.ds(base, EG)]).then_inc(e_ix, 1)
                g.tensor_copy(ix_d[:, gb, :], dst_i[:, bass.ds(base, EG)]).then_inc(e_ix, 1)
                g.wait_ge(e_ix, (lap * 2 + gb) * 2 + 2)
                if not first:
                    g.wait_ge(e_sc, lap * 2 + gb - 1)
                g.sem_inc(e_go, 1)
                for j in range(EG):
                    g.indirect_dma_start(
                        out=tg_d[:, gb, j, :], out_offset=None, in_=node_table[:, :],
                        in_offset=bass.IndirectOffsetOnAxis(ap=ix_d[:, gb, j:j + 1], axis=0))\
                        .then_inc(e_tab[gb], 16)
                for j in range(EG):
                    slot = gb * EG + j
                    if not first:
                        g.wait_ge(e_vv, (lap - 1) * XR + slot + 1)
                        g.sem_inc(e_go, 1)
                    g.indirect_dma_start(
                        out=xg[:, slot, :], out_offset=None, in_=node_rows[:, :],
                        in_offset=bass.IndirectOffsetOnAxis(ap=ix_s[:, gb, j:j + 1], axis=0))\
                        .then_inc(e_x[slot], 16)

            g.wait_ge(s_dve, 16)
            for gb in range(2):
                group_rows(0, gb, True)
            with g.Fori(1, LAPS_E) as lap:
                for gb in range(2):
                    group_rows(lap, gb, False)

            for j in range(4):
                g.wait_ge(e_out[j], 16 * (ET // 4))
            g.indirect_dma_start(out=ff[:, :], out_offset=None, in_=seg_rows[:, :],
                                 in_offset=bass.IndirectOffsetOnAxis(ap=first_end[:, 0:1], axis=0)).then_inc(b_ff, 16)
            g.wait_ge(b_dve, 22)
            g.wait_ge(b_in, 16)
            g.indirect_dma_start(out=seg_rows[:, :], in_=ff[:, :], in_offset=None,
                                 out_offset=bass.IndirectOffsetOnAxis(ap=first_end[:, 0:1], axis=0)).then_inc(b_fix, 16)

            g.wait_ge(b_fix, 16)

            def gather(st, first):
                r, u = st.ring(3), st.t
                if not first:
                    g.wait_ge(n_sum, u - 2)
                    g.wait_ge(n_hh, u - 2)
                    g.wait_ge(n_ag[r], 16 * st.div(3))
                    g.sem_inc(n_go, 1)
                g.tensor_copy(ixn[:, r, :], pos_i[:, bass.ds(u, 1)]).then_inc(n_ix, 1)
                g.tensor_copy(mr[:, r, :], table[:, bass.ds(u, 1), SHIFT:RSTD + 1]).then_inc(n_mr, 1)
                g.memset(agg[:, r, :], 0.0).then_inc(n_ix, 1)
                g.wait_ge(n_ix, u * 2 + 2)
                g.sem_inc(n_go, 1)
                g.indirect_dma_start(out=agg[:, r, :], out_offset=None, in_=seg_rows[:, :],
                                     in_offset=bass.IndirectOffsetOnAxis(ap=ixn[:, r, :], axis=0),
                                     bounds_check=ET * P - 1, oob_is_err=False).then_inc(n_ag[r], 16)

            def norms(st):
                u, r, s6 = st.t, st.ring(3), st.slot
                base = u * 6
                g.wait_ge(n_mv, u + 1)
                g.tensor_tensor(pw[:, 0:1], mvn[:, r, 1:2], kc[:, 2:3], ALU.mult).then_inc(n_pw, 1)
                g.wait_ge(n_pw, base + 1)
                g.tensor_tensor(pw[:, 1:2], pw[:, 0:1], kc[:, 3:4], ALU.add).then_inc(n_pw, 1)
                g.wait_ge(n_pw, base + 2)
                if st.after(6):
                    g.wait_ge(g_pg, st.div(3) - 1)
                g.tensor_tensor(gam[:, s6, :], pw[:, 1:2], kc[:, 0:1], ALU.pow).then_inc(n_gam, 1)
                g.wait_ge(n_gam, u + 1)
                g.tensor_tensor(pw[:, 2:3], gam[:, s6, :], gam[:, s6, :], ALU.mult).then_inc(n_pw, 1)
                g.wait_ge(n_pw, base + 3)
                g.wait_ge(n_sq, u + 1)
                g.tensor_tensor(pw[:, 3:4], pw[:, 2:3], usum[:, r, :], ALU.mult).then_inc(n_pw, 1)
                g.wait_ge(n_pw, base + 4)
                g.sem_inc(n_go, 1)
                g.tensor_scalar(pw[:, 4:5], pw[:, 3:4], EPS * EPS, None, ALU.max).then_inc(n_pw, 1)
                g.wait_ge(n_pw, base + 5)
                g.tensor_tensor(pw[:, 5:6], pw[:, 4:5], kc[:, 0:1], ALU.pow).then_inc(n_pw, 1)
                g.wait_ge(n_pw, base + 6)
                if st.after(3):
                    g.wait_ge(n_L, u - 2)
                g.tensor_tensor(tok[:, r, :], gam[:, s6, :], pw[:, 5:6], ALU.mult).then_inc(n_tok, 1)

            def node_step(st):
                if not (isinstance(st.t, int) and st.t == FULL):
                    gather(st.shift(2), isinstance(st.t, int) and st.t == 0)
                if st.after(1):
                    norms(st.shift(-1))
            g.wait_ge(b_dve, 6)
            gather(Step(0, 0, 0, P), True)
            gather(Step(1, 0, 1, P), True)
            walk(g, FULL, NU, TAIL, node_step)
            norms(Step(FULL, FULL // NU, 0, P))

            for i in range(3):
                g.wait_ge(n_st[i], 16 * ring_uses(NT, 3, i))

            g.wait_ge(f_p, 1)
            for i in range(3):
                g.wait_ge(n_ag[i], 16 * ring_uses(NT + 1, 3, i))
            g.wait_ge(n_x[NT % 3], 16 * ring_uses(NT + 1, 3, NT % 3))
            g.wait_ge(n_hh, NT + 1)
            g.wait_ge(n_keep, NT)

            def load_x1(st):
                if st.after(6):
                    g.wait_ge(o_o, st.t - 5)
                    g.sem_inc(n_go, 1)
                g.dma_start(xo[0:st.rows, st.slot, :], x1_dram[tile_rows(st), :]).then_inc(o_x[st.slot], 16)
            walk(g, FULL, NU, TAIL, load_x1)

        @block.tensor
        def _(pe):
            mm, tr = nc.tensor.matmul, nc.tensor.transpose

            pe.wait_ge(s_in, IN_DMAS)
            mm(bank(6, 2 * H), wfc2[:, :], attn_sb[:, :], start=True, stop=True).then_inc(s_pe, 1)
            pe.wait_ge(s_ident, 2)
            pe.wait_ge(s_dve, 4)
            for i, m in enumerate((e_srcf, e_dstf, e_flag)):
                last = tr(bank(7, ET, i * ET), m[:, :], ident[0:ET, 0:ET])
            last.then_inc(s_pe, 1)
            pe.wait_ge(s_dve, 6)
            mm(ps[0:ET, 7 * 512 + 256:7 * 512 + 256 + ET], sel_last[:, :], dst_f[:, :], start=True, stop=True)\
                .then_inc(s_pe, 1)
            pe.wait_ge(s_slots, 1)
            pe.wait_ge(s_dve, 16)
            for c in range(C):
                last = tr(bank(7, S, c * S), slots_sq[:, c * P:(c + 1) * P], ident[0:S, 0:S])
            last.then_inc(s_pe, 1)

            pe.wait_ge(s_dve, 23)

            def attention(st):
                b = st.ring(2)
                pe.wait_ge(a_ev, st.t + 1)
                if st.after(2):
                    pe.wait_ge(a_row, st.t - 1)
                    pe.wait_ge(a_tab, st.t - 1)
                for c in range(C):
                    last = mm(bank(4 + 2 * b + c // 3, FC, c % 3 * FC), haT[:, b, c * P:(c + 1) * P], wfc[:, c, :],
                              start=True, stop=True)
                last.then_inc(a_att, 1)

            def stats_step(st):
                b = st.ring(2)
                pe.wait_ge(a_hh, st.t + 1)
                if st.after(2):
                    pe.wait_ge(a_ev, st.t - 1)
                for c in range(C):
                    last = tr(bank(2 * b, P, c * P), ha[:, b, c * P:(c + 1) * P], ident[:, :])
                last.then_inc(a_tr, 1)
                if st.after(1):
                    attention(st.shift(-1))
            walk(pe, FULL, NU, TAIL, stats_step)
            attention(Step(FULL, FULL // NU, 0, P))

            pe.wait_ge(a_tab, NT)

            def group(lap, gb, first):
                n = lap * 2 + gb
                pe.wait_ge(e_lk, n + 1)
                pe.wait_ge(e_fb, n + 1)
                if not first:
                    pe.wait_ge(e_dif, n)
                    pe.wait_ge(e_flag_ev, n)
                pe.sem_inc(e_go, 1)
                tr(ps[0:EG * H, 4 * 512:4 * 512 + P], lk[:, :, :].rearrange("p k h -> p (k h)"), ident[:, :])
                tr(ps[0:EG * H, 4 * 512 + P:4 * 512 + 2 * P], fb[:, :, :].rearrange("p k h -> p (k h)"), ident[:, :])\
                    .then_inc(e_tr, 1)
                pe.wait_ge(e_hot, n + 1)
                if not first:
                    pe.wait_ge(e_deg, n)
                for j in range(EG):
                    last = mm(ps[0:ET, 6 * 512:6 * 512 + P], hot_hi[:, gb, j, :], hot_lo[:, gb, j, :],
                              start=(j == 0), stop=(j == EG - 1))
                last.then_inc(e_hist, 1)
                pe.wait_ge(e_exp, n + 1)
                pe.wait_ge(e_sm, n + 1)
                if not first:
                    pe.wait_ge(e_em, n)
                pe.sem_inc(e_go, 1)
                tr(bank(5, EG * H), eeT[:, :], ident[0:EG * H, 0:EG * H])
                tr(bank(5, EG * H, EG * H), smax[:, :], ident[0:EG * H, 0:EG * H]).then_inc(e_back, 1)
                for j in range(EG):
                    t = lap * XR + gb * EG + j
                    b = j % 2
                    pe.wait_ge(e_em, n + 1)
                    pe.wait_ge(e_same, t + 1)
                    pe.wait_ge(e_vv, t + 1)
                    if not first or j >= 2:
                        pe.wait_ge(e_z, t - 1)
                        pe.wait_ge(e_lcp, t - 1)
                    mm(bank(2 * b), same[:, b, :], vv[:, b, 0:512], start=True, stop=True)
                    mm(bank(2 * b + 1, D - 512), same[:, b, :], vv[:, b, 512:D], start=True, stop=True)
                    mm(bank(2 * b + 1, H, D - 512), same[:, b, :], eem[:, gb, 0, j, :], start=True, stop=True)\
                        .then_inc(e_mm, 1)
            group(0, 0, True)
            group(0, 1, False)
            with pe.Fori(1, LAPS_E) as lap:
                for gb in range(2):
                    group(lap, gb, False)

            pe.wait_ge(b_dve, 1)
            mm(ps[0:ET, 7 * 512:7 * 512 + 1], tri[:, :], cum[:, P - 1:P], start=True, stop=True).then_inc(b_pe, 1)
            pe.wait_ge(b_dve, 5)
            tr(bank(7, ET, 256), pos_f[:, :], ident[0:ET, 0:ET]).then_inc(b_pe, 1)
            pe.wait_ge(b_dve, 7)
            HH = H // 2
            for i in range(2):
                last = mm(ps[0:ET, i * 512:i * 512 + HH * ET], ones[0:ET, 0:ET],
                          bd[:, i * HH:(i + 1) * HH, :].rearrange("j h k -> j (h k)"), start=True, stop=True)
            last.then_inc(b_pe, 1)
            pe.wait_ge(b_act, 1)
            for h in range(H):
                at = (2 + h // HH) * 512 + (h % HH) * ET
                last = tr(ps[0:ET, at:at + ET], be[:, h, :], ident[0:ET, 0:ET])
            last.then_inc(b_pe, 1)
            pe.wait_ge(b_dve, 15)
            for h in range(H):
                mm(ps[0:ET, 4 * 512 + h * DH:4 * 512 + (h + 1) * DH], bwT[:, h, :], rr[:, h * DH:(h + 1) * DH],
                   start=True, stop=True)
                last = mm(ps[0:ET, 6 * 512 + h:6 * 512 + h + 1], bwT[:, h, :], ones[0:ET, 0:1], start=True, stop=True)
            last.then_inc(b_pe, 1)

            def x_transposes(st):
                pe.wait_ge(n_hh, st.t + 1)
                for c in range(C):
                    last = tr(bank(0, P, c * P), hn[:, st.ring(3), c * P:(c + 1) * P], ident[:, :])
                last.then_inc(n_t1, 1)

            def slot_logits(st):
                pe.wait_ge(n_ev3, st.t + 1)
                if st.after(1):
                    pe.wait_ge(n_L, st.t)
                for c in range(C):
                    last = mm(bank(5, S), uT[:, c * P:(c + 1) * P], slT[:, c, :], start=(c == 0), stop=(c == C - 1))
                last.then_inc(n_lg, 1)

            def group_transpose(q, tiles, rows, first):
                pe.wait_ge(n_L, q * NG + tiles)
                if not first:
                    pe.wait_ge(g_pg, q)
                pe.sem_inc(n_go, 1)
                for j in range(tiles):
                    last = tr(ps[0:S, 6 * 512 + j * P:6 * 512 + j * P + rows], lg[0:rows, j, :],
                              ident[0:rows, 0:rows])
                last.then_inc(g_lt, 1)

            def group_back(q, tiles, rows):
                pe.wait_ge(g_exp, q + 1)
                pe.sem_inc(n_go, 1)
                for j in range(tiles):
                    last = tr(ps[0:rows, 6 * 512 + j * S:6 * 512 + (j + 1) * S], dT[:, j * P:j * P + rows],
                       ident[0:S, 0:S])
                last.then_inc(g_back, 1)

            def group_inputs(q, tiles, rows, s0, first):
                pe.wait_ge(g_pg, q + 1)
                if not first:
                    pe.wait_ge(g_ya, q)
                for j in range(tiles):
                    for half in range(2):
                        last = mm(ps[half * S:(half + 1) * S, 7 * 512:7 * 512 + HD],
                                  pg[0:rows, j, :], uu[0:rows, s0 + j, half * HD:(half + 1) * HD],
                                  start=(j == 0), stop=(j == tiles - 1))
                last.then_inc(g_y, 1)

            def x_products(st):
                pe.wait_ge(n_ev1, st.t + 1)
                if st.after(1):
                    pe.wait_ge(n_sum, st.t)
                for c in range(C):
                    last = mm(bank(3, P, c * P), hnT[:, c * P:(c + 1) * P], wres[:, :], start=True, stop=True)
                last.then_inc(n_mm, 1)

            def u_transposes(st):
                pe.wait_ge(n_u, st.t + 1)
                for c in range(C):
                    last = tr(bank(0, P, c * P), uu[:, st.slot, c * P:(c + 1) * P], ident[:, :])
                last.then_inc(n_t3, 1)

            def node_step(st):
                k = st.slot % NG
                tail = isinstance(st.t, int) and st.t == FULL
                if not tail:
                    if st.after(2):
                        pe.wait_ge(n_ev3, st.t - 1)
                    x_transposes(st.shift(1))
                if st.after(2):
                    slot_logits(st.shift(-2))
                if k == 2 and st.after(5):
                    group_back(st.div(3) - 1, NG, P)
                if st.after(1):
                    pe.wait_ge(n_ev1, st.t + (1 if tail else 2))
                    u_transposes(st.shift(-1))
                if not tail:
                    x_products(st.shift(1))
                if k == 1 and st.after(4):
                    group_transpose(st.div(3) - 1, NG, P, isinstance(st.t, int) and st.t < 6)
                if k == 2 and st.after(5):
                    group_inputs(st.div(3) - 1, NG, P, (st.slot + 1) % NU, isinstance(st.t, int) and st.t < 6)

            pe.wait_ge(b_fix, 16)
            x_transposes(Step(0, 0, 0, P))
            x_products(Step(0, 0, 0, P))
            walk(pe, FULL, NU, TAIL, node_step)
            QL = FULL // NG
            last_step = Step(FULL, FULL // NU, 0, P)
            slot_logits(last_step.shift(-1))
            pe.wait_ge(n_ev3, FULL)
            u_transposes(last_step)
            group_transpose(QL - 1, NG, P, False)
            slot_logits(last_step)
            group_back(QL - 1, NG, P)
            group_inputs(QL - 1, NG, P, NG, False)
            group_transpose(QL, 1, TAIL, False)
            group_back(QL, 1, TAIL)
            group_inputs(QL, 1, TAIL, 0, False)

            pe.wait_ge(f_d, 3)
            for c in range(C):
                last = tr(ps[0:S, c * P:(c + 1) * P], ysum[:, c:HD:C], ident[:, :])
            last.then_inc(f_p, 1)
            pe.wait_ge(f_d, 5)

            def first_products(lap, first, last_lap):
                for k in range(2):
                    n = lap * 2 + k
                    pe.wait_ge(f_w1[k], 16 * (lap + 1))
                    pe.wait_ge(f_win, n + 1)
                    for c in range(C):
                        for j in range(G):
                            last = mm(ps[j * GR:(j + 1) * GR, j * 512:j * 512 + F], yw[:, k, j, c, :],
                                      w1b[:, k, j, c * F:(c + 1) * F],
                                      start=(first and k == 0 and c == 0), stop=(last_lap and k == 1 and c == C - 1))
                    last.then_inc(f_h, 1)

            def second_products(lap, first, last_lap):
                for k in range(2):
                    n = lap * 2 + k
                    pe.wait_ge(f_w2[k], 16 * (lap + 1))
                    pe.wait_ge(f_hwin, n + 1)
                    for at, width in ((0, 512), (512, D - 512)):
                        for j in range(G):
                            last = mm(ps[j * GR:(j + 1) * GR, 2 * j * 512 + at:2 * j * 512 + at + width],
                                      hw[:, k, j, :], w2b[:, k, j, at:at + width],
                                      start=(first and k == 0), stop=(last_lap and k == 1))
                    last.then_inc(f_y, 1)

            LAPS_F = QUADS // 2
            first_products(0, True, False)
            with pe.Fori(1, LAPS_F - 1) as lap:
                first_products(lap, False, False)
            first_products(LAPS_F - 1, False, True)
            pe.wait_ge(f_a, 1)
            tr(ps[0:F, 4 * 512:4 * 512 + P], hact[:, :], ident[:, :]).then_inc(f_p, 1)
            second_products(0, True, False)
            with pe.Fori(1, LAPS_F - 1) as lap:
                second_products(lap, False, False)
            second_products(LAPS_F - 1, False, True)

            def mix(st):
                b = st.ring(2)
                pe.wait_ge(o_ev, st.t + 1)
                if st.after(2):
                    pe.wait_ge(o_o, st.t - 1)
                parts = ((0, y_a), (0, y_b), (P, y_c))
                for at, width in ((0, 512), (512, D - 512)):
                    for i, (e, y) in enumerate(parts):
                        last = mm(bank(2 * b, width, at), exT[:, b, e:e + P], y[:, at:at + width],
                                  start=(i == 0), stop=(i == len(parts) - 1))
                last.then_inc(o_mm, 1)

            def out_step(st):
                b = st.ring(2)
                if st.after(2):
                    pe.wait_ge(o_ev, st.t - 1)
                mm(bank(4 + b, P), e12[:, bass.ds(st.t, 1), :].rearrange("p t e -> p (t e)"), ident_b[:, :],
                   start=True, stop=True)
                mm(bank(4 + b, P, P), e13[:, bass.ds(st.t, 1), :].rearrange("p t e -> p (t e)"), ident_b[:, :],
                   start=True, stop=True).then_inc(o_t, 1)
                if st.after(1):
                    mix(st.shift(-1))
            pe.wait_ge(o_cw, CW)
            pe.wait_ge(f_d, F_OUT + 5)
            walk(pe, FULL, NU, TAIL, out_step)
            mix(Step(FULL, FULL // NU, 0, P))

        @block.scalar
        def _(act):
            def copy(o, i):
                return nc.scalar.activation(o, i, ACT.Copy)

            act.wait_ge(s_in, IN_DMAS)
            nc.scalar.activation(slots_sq[:, :], slots_sb[:, :], ACT.Square, accum_out=s_norm[:, 0:1]).then_inc(s_sq, 1)

            def table_out(t0, k, rows):
                act.dma_start(node_table[bass.ds(t0 * P, (k - 1) * P + rows), :]
                              .rearrange("(k p) c -> p k c", k=k),
                              table[0:rows, bass.ds(t0, k), :]).then_inc(a_out, 16)

            def rows_of(st):
                b, f = st.ring(2), st.slot
                out2 = ps[:, (4 + 2 * b) * 512:(6 + 2 * b) * 512].rearrange("p (k n) -> p k n", n=512)[:, :, 0:3 * FC]
                if st.after(NU):
                    act.wait_ge(a_st[f], 16 * st.lap)
                copy(frow[:, f, :].rearrange("p (k n) -> p k n", k=2), out2).then_inc(a_row, 1)
                copy(table[:, bass.ds(st.t, 1), 0:H].rearrange("p t (k c i) -> p (t k) c i", k=2, i=2),
                     out2.rearrange("p k (c f) -> p k c f", f=FC)[:, :, :, A2C:FC]).then_inc(a_tab, 1)

            def stats_step(st):
                b = st.ring(2)
                act.wait_ge(a_tr, st.t + 1)
                if st.after(2):
                    act.wait_ge(a_att, st.t - 1)
                copy(haT[:, b, :], bank(2 * b, D)).then_inc(a_ev, 1)
                if st.after(2):
                    rows_of(st.shift(-2))
                if st.slot == 1 and st.after(NU):
                    act.wait_ge(a_tab, st.t - 1)
                    act.wait_ge(a_mr, st.t - 1)
                    table_out(st.t - 1 - NU, NU, P)
            act.wait_ge(s_pool, POOL_SET)
            walk(act, FULL, NU, TAIL, stats_step)
            for t in (FULL - 1, FULL):
                act.wait_ge(a_att, t + 1)
                rows_of(Step(t, t // NU, t % NU, P))
            act.wait_ge(a_tab, NT)
            act.wait_ge(a_mr, NT)
            table_out(FULL - NU, NU, P)
            table_out(FULL, 1, TAIL)

            def group(lap, gb, first):
                n = lap * 2 + gb
                act.wait_ge(e_tr, n + 1)
                if not first:
                    act.wait_ge(e_sm, n)
                copy(flagT[:, 0:P], ps[0:EG * H, 4 * 512 + P:4 * 512 + 2 * P]).then_inc(e_flag_ev, 1)
                act.wait_ge(e_dif, n + 1)
                if not first:
                    act.wait_ge(e_back, n)
                nc.scalar.activation(eeT[:, :], dif[:, :], ACT.Exp).then_inc(e_exp, 1)
                act.wait_ge(e_em, n + 1)
                for j in range(EG):
                    t = lap * XR + gb * EG + j
                    if not first:
                        act.wait_ge(e_out[j], 16 * n)
                    copy(zo[:, j, D + H:ROW], eem[:, gb, 1, j, :]).then_inc(e_mcp, 1)
            group(0, 0, True)
            group(0, 1, False)
            with act.Fori(1, LAPS_E) as lap:
                for gb in range(2):
                    group(lap, gb, False)

            act.wait_ge(b_dve, 12)
            nc.scalar.activation(be[:, :, :], bm[:, :, :], ACT.Exp).then_inc(b_act, 1)
            act.wait_ge(b_dve, 13)
            nc.scalar.activation(bcf[:, :], bdf[:, :], ACT.Exp).then_inc(b_act, 1)

            def hh(st):
                r = st.ring(3)
                act.wait_ge(n_x[r], 16 * st.div(3) + 16)
                act.wait_ge(n_mr, st.t + 1)
                if st.after(3):
                    act.wait_ge(n_t1, st.t - 2)
                nc.scalar.activation(hn[:, r, :], xn[:, r, :], ACT.Identity, bias=mr[:, r, 0:1], scale=mr[:, r, 1:2])\
                    .then_inc(n_hh, 1)

            def ev1(st):
                act.wait_ge(n_t1, st.t + 1)
                if st.after(1):
                    act.wait_ge(n_mm, st.t)
                copy(hnT[:, :], bank(0, D)).then_inc(n_ev1, 1)

            def keep(st):
                act.wait_ge(n_L, st.t + 1)
                copy(logits[:, bass.ds(st.t, 1), :], lg[:, st.ring(3), :]).then_inc(n_keep, 1)

            def group_exp(q, par, cols, first):
                act.wait_ge(g_neg, q + 1)
                if not first:
                    act.wait_ge(g_back, q)
                    act.wait_ge(g_l, q)
                    act.wait_ge(g_cd, q)
                    act.wait_ge(g_ya, q)
                nc.scalar.activation(dT[:, 0:cols], ps[0:S, 6 * 512:6 * 512 + cols], ACT.Exp, bias=nneg[:, :],
                                     accum_out=dsum[:, :]).then_inc(g_exp, 1)
                nc.scalar.activation(cc[0:S, :], mrun[:, 1 - par, :], ACT.Exp, bias=nneg[:, :]).then_inc(g_c, 1)

            def square(st):
                act.wait_ge(n_u, st.t + 1)
                if st.after(1):
                    act.wait_ge(n_sq, st.t)
                if st.after(3):
                    act.wait_ge(n_tok, st.t - 2)
                nc.scalar.activation(usq[:, :], uu[:, st.slot, :], ACT.Square, accum_out=usum[:, st.ring(3), :])\
                    .then_inc(n_sq, 1)

            def ev3(st):
                act.wait_ge(n_t3, st.t + 1)
                if st.after(1):
                    act.wait_ge(n_lg, st.t)
                copy(uT[:, :], bank(0, D)).then_inc(n_ev3, 1)

            def node_step(st):
                if not (isinstance(st.t, int) and st.t == FULL):
                    ev1(st.shift(1))
                if st.after(1):
                    square(st.shift(-1))
                    ev3(st.shift(-1))
                if not (isinstance(st.t, int) and st.t == FULL):
                    hh(st.shift(2))
                if st.after(2):
                    keep(st.shift(-2))
                if st.slot % NG == 1 and st.after(4):
                    group_exp(st.div(3) - 1, (st.slot // NG + 1) % 2, NG * P, isinstance(st.t, int) and st.t < 6)
            act.wait_ge(b_fix, 16)
            hh(Step(0, 0, 0, P))
            hh(Step(1, 0, 1, P))
            ev1(Step(0, 0, 0, P))
            walk(act, FULL, NU, TAIL, node_step)
            last_step = Step(FULL, FULL // NU, 0, P)
            square(last_step)
            ev3(last_step)
            keep(last_step.shift(-1))
            keep(last_step)
            QL = FULL // NG
            group_exp(QL - 1, (QL - 1) % 2, NG * P, False)
            group_exp(QL, QL % 2, TAIL, False)

            act.wait_ge(o_cw, 2)
            nc.scalar.activation(logits[:, :, :], logits[:, :, :], ACT.Exp).then_inc(o_cexp, 1)
            act.wait_ge(f_d, 5 + G)
            nc.scalar.activation(hact[:, :], hpre[:, :], ACT.Gelu).then_inc(f_a, 1)

            def weights_T(st):
                b = st.ring(2)
                act.wait_ge(o_t, st.t + 1)
                if st.after(2):
                    act.wait_ge(o_mm, st.t - 1)
                copy(exT[:, b, :], bank(4 + b, 2 * P)).then_inc(o_ev, 1)
            walk(act, FULL, NU, TAIL, weights_T)

        @block.vector
        def _(dve):
            v = nc.vector
            link = chain_of(dve, s_dve)
            dve.wait_ge(s_edge_in, 64)
            v.memset(e_flag[:, 0:1], 0.0).then_inc(s_copies, 1)
            v.memset(yw[:, :, :, :, :], 0.0).then_inc(f_zero, 1)
            v.memset(hw[:, :, :, :], 0.0).then_inc(f_zero, 1)
            v.memset(zeros[:, :, :], 0.0).then_inc(f_zero, 1)
            v.memset(wfc[:, :, :], 0.0).then_inc(s_copies, 1)
            link(v.tensor_copy(e_srcf[:, :], e_src[:, :]))
            link(v.tensor_copy(e_dstf[:, :], e_dst[:, :]))
            link(v.tensor_tensor(e_eq[:, 1:P], e_dstf[:, 1:P], e_dstf[:, 0:P - 1], ALU.not_equal))
            dve.wait_ge(s_copies, 2)
            link(v.tensor_scalar(e_flag[:, 1:P], e_eq[:, 1:P], -BIG, None, ALU.mult))
            dve.wait_ge(s_ident, 2)
            dve.wait_ge(s_pe, 2)
            v.tensor_copy(src_i[:, :], bank(7, ET)).then_inc(s_copies, 1)
            v.tensor_copy(flag_t[:, :], bank(7, ET, 2 * ET)).then_inc(s_copies, 1)
            v.tensor_scalar(dst_i[:, :], bank(7, ET, ET), float(N - 1), None, ALU.min).then_inc(s_copies, 1)
            v.tensor_copy(dst_ti[:, :], bank(7, ET, ET)).then_inc(s_copies, 1)
            link(v.tensor_copy(sel_last[:, :], ident[:, P - 1:P].broadcast_to([P, ET])))
            link(v.tensor_copy(dst_f[:, :], bank(7, ET, ET)))
            dve.wait_ge(s_copies, 6)
            link(v.tensor_scalar(hi_i[:, :], dst_ti[:, :], P.bit_length() - 1, None, ALU.arith_shift_right))
            link(v.tensor_scalar(lo_i[:, :], dst_ti[:, :], P - 1, None, ALU.bitwise_and))
            v.tensor_copy(hi_f[:, :], hi_i[:, :]).then_inc(s_copies, 1)
            v.tensor_copy(lo_f[:, :], lo_i[:, :]).then_inc(s_copies, 1)
            dve.wait_ge(s_pool, POOL_SET)
            v.tensor_copy(iota_f[:, :], iota_i[:, :]).then_inc(s_copies, 1)
            v.tensor_copy(e_basef[:, :], e_base[:, :]).then_inc(s_copies, 1)
            link(v.tensor_scalar(e_eq[:, :], e_dstf[:, :], e_dstf[:, 0:1], None, ALU.is_equal))
            link(v.tensor_reduce(e_cnt[:, :], e_eq[:, :], AX.X, ALU.add))
            dve.wait_ge(s_copies, 10)
            link(v.tensor_tensor(first_end[:, :], e_cnt[:, :], e_basef[:, :], ALU.add))
            dve.wait_ge(s_pe, 3)
            link(v.tensor_scalar(chain[:, :], ps[0:ET, 7 * 512 + 256:7 * 512 + 256 + ET], e_dstf[:, 0:1], None,
                                 ALU.is_equal))
            link(v.tensor_tensor(e_eq[:, 0:ET], tri[:, :], ident[0:ET, 0:ET], ALU.add))
            link(v.tensor_scalar(e_eq[:, 0:ET], e_eq[:, 0:ET], -1.0, 1.0, ALU.mult, ALU.add))
            link(v.tensor_tensor(chain[:, :], chain[:, :], e_eq[:, 0:ET], ALU.mult))
            link(v.tensor_scalar(chain[:, :], chain[:, :], -1.0, BIG, ALU.add, ALU.mult))
            for half in range(2):
                for part in range(2):
                    at = half + part * H
                    link(v.tensor_copy(
                        wfc[half * DH:(half + 1) * DH, :, A1C + 2 * part + half:A1C + 2 * part + half + 1],
                        ps[half * DH:(half + 1) * DH, 6 * 512 + at:6 * 512 + part * H + H:2].unsqueeze(2)))
            dve.wait_ge(s_in, IN_DMAS)
            for half in range(2):
                rows = slice(half * DH, (half + 1) * DH)
                link(v.tensor_copy(wfc[rows, :, rows], wfcT[rows, :].unsqueeze(1).broadcast_to([DH, C, DH])))
            v.tensor_copy(ident_b[:, :], ident[:, :])
            dve.wait_ge(s_gp, 2)
            v.tensor_scalar(slots_sq[:, :], slots_sb[:, :], s_norm[:, 2:3], scale_sb[:, :], ALU.mult, ALU.mult)\
                .then_inc(s_slots, 1)
            dve.wait_ge(s_pe, 4)
            link(v.tensor_copy(slT[:, :, :].rearrange("p c s -> p (c s)"), bank(7, C * S)))

            def normalise(st):
                b = st.ring(2)
                dve.wait_ge(a_rstd, st.t + 1)
                if st.after(2):
                    dve.wait_ge(a_tr, st.t - 1)
                v.tensor_scalar(ha[:, b, :], xa[:, st.slot, :], mva[:, b, 0:1], mva[:, b, 3:4], ALU.subtract, ALU.mult)\
                    .then_inc(a_hh, 1)
                v.scalar_tensor_tensor(table[:, bass.ds(st.t, 1), SHIFT:SHIFT + 1], mva[:, b, 0:1].unsqueeze(1), -1.0,
                                       mva[:, b, 3:4].unsqueeze(1), ALU.mult, ALU.mult)
                v.tensor_copy(table[:, bass.ds(st.t, 1), RSTD:RSTD + 1], mva[:, b, 3:4].unsqueeze(1)).then_inc(a_mr, 1)

            def stats_step(st):
                b = st.ring(2)
                dve.wait_ge(xa_in[st.slot], 16 * (st.lap + 1))
                v.bn_stats(bna[:, b, 0:6], xa[:, st.slot, 0:512])
                v.bn_stats(bna[:, b, 6:12], xa[:, st.slot, 512:D]).then_inc(a_bn, 1)
                dve.wait_ge(a_bn, st.t + 1)
                if st.after(2):
                    dve.wait_ge(a_mr, st.t - 1)
                if st.after(1):
                    normalise(st.shift(-1))
                v.bn_aggr(mva[:, b, 0:2], bna[:, b, :]).then_inc(a_mv, 1)
            walk(dve, FULL, NU, TAIL, stats_step)
            normalise(Step(FULL, FULL // NU, 0, P))

            dve.wait_ge(a_tab, NT)
            for i in range(NU):
                dve.wait_ge(a_st[i], 16 * ring_uses(NT, NU, i))
            v.memset(flagT[:, P:P + 1], 0.0).then_inc(e_init, 1)
            v.memset(deg[:, :], 0.0).then_inc(e_init, 1)
            dve.wait_ge(e_init, 2)

            def group(lap, gb, first, early):
                n = lap * 2 + gb
                t0 = lap * XR + gb * EG
                dve.wait_ge(e_tab[gb], 16 * EG * (lap + 1))
                for j in range(EG):
                    dve.wait_ge(e_x[gb * EG + j], 16 * (lap + 1))
                v.tensor_tensor(sc[:, :, :].rearrange("p k (c i) -> p k c i", i=2),
                                xg[:, gb * EG:(gb + 1) * EG, :]
                                .rearrange("p k (c f) -> p k c f", f=FC)[:, :, :, A1C:A1C + 2],
                                tg_d[:, gb, :, 0:H].rearrange("p k (c i) -> p k c i", i=2), ALU.add).then_inc(e_sc, 1)
                if not early:
                    dve.wait_ge(e_hist, n - 1)
                v.tensor_tensor(hot_lo[:, gb, :, :], lo_f[:, bass.ds(t0, EG)].unsqueeze(2).broadcast_to([P, EG, P]),
                                iota_f[:, :].unsqueeze(1).broadcast_to([P, EG, P]), ALU.is_equal)
                v.tensor_tensor(hot_hi[:, gb, :, :], hi_f[:, bass.ds(t0, EG)].unsqueeze(2).broadcast_to([P, EG, ET]),
                                iota_f[:, 0:ET].unsqueeze(1).broadcast_to([P, EG, ET]), ALU.is_equal).then_inc(e_hot, 1)
                dve.wait_ge(e_sc, n + 1)
                v.scalar_tensor_tensor(lk[:, :, :], sc[:, :, :], SLOPE, sc[:, :, :], ALU.mult, ALU.max).then_inc(e_lk, 1)
                v.tensor_copy(fb[:, :, :], flag_t[:, bass.ds(t0, EG)].unsqueeze(2).broadcast_to([P, EG, H]))\
                    .then_inc(e_fb, 1)
                v.tensor_copy(dsc[:, gb, :], dst_f[:, bass.ds(t0, EG)]).then_inc(e_dsc, 1)
                dve.wait_ge(e_tr, n + 1)
                dve.wait_ge(e_flag_ev, n + 1)
                v.tensor_tensor_scan(pmax[:, :], flagT[:, 0:P], ps[0:EG * H, 4 * 512:4 * 512 + P], -BIG,
                                     ALU.add, ALU.max).then_inc(e_pm, 1)
                dve.wait_ge(e_pm, n + 1)
                v.tensor_tensor_scan(smax[:, ::-1], flagT[:, P:0:-1], pmax[:, ::-1], -BIG,
                                     ALU.add, ALU.max).then_inc(e_sm, 1)
                dve.wait_ge(e_hist, n + 1)
                v.tensor_tensor(deg[:, :], deg[:, :], ps[0:ET, 6 * 512:6 * 512 + P], ALU.add).then_inc(e_deg, 1)
                dve.wait_ge(e_sm, n + 1)
                v.tensor_tensor(dif[:, :], ps[0:EG * H, 4 * 512:4 * 512 + P], smax[:, :], ALU.subtract).then_inc(e_dif, 1)
                if not early:
                    dve.wait_ge(e_mcp, (n - 1) * EG)
                dve.wait_ge(e_back, n + 1)
                v.tensor_copy(eem[:, gb, :, :, :].rearrange("p a k h -> p (a k h)"), bank(5, 2 * EG * H)).then_inc(e_em, 1)
                dve.wait_ge(e_row[gb], 16 * (lap + 1))
                dve.wait_ge(e_dsc, n + 1)
                dve.wait_ge(e_em, n + 1)

                def rows(j):
                    t, b = t0 + j, j % 2
                    if not first or j >= 2:
                        dve.wait_ge(e_mm, t - 1)
                    v.tensor_scalar(same[:, b, :], dst_row[:, gb, j * P:(j + 1) * P], dsc[:, gb, j:j + 1], None,
                                    ALU.is_equal).then_inc(e_same, 1)
                    v.tensor_tensor(
                        vv[:, b, :].rearrange("p (c i d) -> p c i d", c=C, d=DH),
                        xg[:, gb * EG + j, :].rearrange("p (c f) -> p c f", f=FC)[:, :, 0:2 * DH]
                        .rearrange("p c (i d) -> p c i d", i=2),
                        eem[:, gb, 0, j, :].rearrange("p (c i) -> p c i", i=2).unsqueeze(3)
                        .broadcast_to([P, C, 2, DH]), ALU.mult).then_inc(e_vv, 1)

                def sums(j):
                    t, b = t0 + j, j % 2
                    dve.wait_ge(e_mm, t + 1)
                    v.reciprocal(rl[:, b, :], bank(2 * b + 1, H, D - 512)).then_inc(e_rl, 1)
                    if not first:
                        dve.wait_ge(e_out[j], 16 * n)
                    v.tensor_copy(zo[:, j, D:D + H], bank(2 * b + 1, H, D - 512)).then_inc(e_lcp, 1)
                    dve.wait_ge(e_rl, t + 1)
                    v.tensor_tensor(zo[:, j, 0:D].rearrange("p (h d) -> p h d", h=H),
                                    bank(2 * b, D).rearrange("p (h d) -> p h d", d=DH),
                                    rl[:, b, :].unsqueeze(2).broadcast_to([P, H, DH]), ALU.mult).then_inc(e_z, 1)
                rows(0)
                rows(1)
                sums(0)
                rows(2)
                sums(1)
                rows(3)
                sums(2)
                sums(3)
            group(0, 0, True, True)
            group(0, 1, False, True)
            with dve.Fori(1, LAPS_E) as lap:
                for gb in range(2):
                    group(lap, gb, False, False)

            link = chain_of(dve, b_dve)
            dve.wait_ge(e_deg, GROUPS)
            link(v.tensor_tensor_scan(cum[:, :], ones[0:ET, :], deg[:, :], 0.0, ALU.mult, ALU.add))
            dve.wait_ge(b_pe, 1)
            link(v.tensor_copy(off_sb[:, :], ps[0:ET, 7 * 512:7 * 512 + 1]))
            link(v.tensor_scalar(none[:, :], deg[:, :], 0.0, float(1 << 20), ALU.is_equal, ALU.mult))
            link(v.scalar_tensor_tensor(pos_f[:, :], cum[:, :], off_sb[:, :], none[:, :], ALU.add, ALU.add))
            link(v.tensor_scalar(pos_f[:, :], pos_f[:, :], -1.0, None, ALU.add))
            dve.wait_ge(b_pe, 2)
            link(v.tensor_copy(pos_i[:, :], bank(7, ET, 256)))
            dve.wait_ge(b_in, 16)
            LC, MC = D, D + H
            link(v.tensor_tensor(bd[:, :, :], rr[:, MC:MC + H].unsqueeze(2).broadcast_to([ET, H, ET]),
                                 ident[0:ET, 0:ET].unsqueeze(1).broadcast_to([ET, H, ET]), ALU.mult))
            dve.wait_ge(b_pe, 3)
            HH = H // 2
            for i in range(2):
                link(v.tensor_tensor(bm[:, i * HH:(i + 1) * HH, :],
                                     ps[0:ET, i * 512:i * 512 + HH * ET].rearrange("k (h j) -> k h j", j=ET),
                                     chain[:, :].unsqueeze(1).broadcast_to([ET, HH, ET]), ALU.add))
            link(v.tensor_reduce(bmax[:, :], bm[:, :, :], AX.X, ALU.max))
            dve.wait_ge(b_ff, 16)
            link(v.tensor_tensor(bmax[:, :], bmax[:, :], ff[:, MC:MC + H], ALU.max))
            link(v.tensor_tensor(bm[:, :, :], bm[:, :, :], bmax[:, :].unsqueeze(2).broadcast_to([ET, H, ET]),
                                 ALU.subtract))
            link(v.tensor_tensor(bdf[:, :], ff[:, MC:MC + H], bmax[:, :], ALU.subtract))
            dve.wait_ge(b_pe, 4)
            for i in range(2):
                link(v.tensor_tensor(bwT[:, i * HH:(i + 1) * HH, :],
                                     ps[0:ET, (2 + i) * 512:(2 + i) * 512 + HH * ET]
                                     .rearrange("j (h k) -> j h k", k=ET),
                                     rr[:, LC + i * HH:LC + (i + 1) * HH].unsqueeze(2).broadcast_to([ET, HH, ET]),
                                     ALU.mult))
            dve.wait_ge(b_act, 2)
            link(v.tensor_tensor(bcf[:, :], bcf[:, :], ff[:, LC:LC + H], ALU.mult))
            dve.wait_ge(b_pe, 5)
            link(v.tensor_tensor(btot[:, :], bcf[:, :], ps[0:ET, 6 * 512:6 * 512 + H], ALU.add))
            link(v.reciprocal(btot[:, :], btot[:, :]))
            link(v.tensor_tensor(bcf[:, :], bcf[:, :], btot[:, :], ALU.mult))
            fz = ff[:, 0:D].rearrange("k (h d) -> k h d", h=H)
            bzv = bz[:, :].rearrange("k (h d) -> k h d", d=DH)
            link(v.tensor_tensor(fz, fz, bcf[:, :].unsqueeze(2).broadcast_to([ET, H, DH]), ALU.mult))
            link(v.tensor_tensor(bzv, ps[0:ET, 4 * 512:4 * 512 + D].rearrange("k (h d) -> k h d", d=DH),
                                 btot[:, :].unsqueeze(2).broadcast_to([ET, H, DH]), ALU.mult))
            link(v.tensor_tensor(fz, fz, bzv, ALU.add))

            dve.wait_ge(b_fix, 16)
            v.memset(ysum[:, :], 0.0).then_inc(g_init, 1)
            v.memset(mrun[:, 1, :], -BIG).then_inc(g_init, 1)
            v.memset(lrun[:, :], 0.0).then_inc(g_init, 1)
            dve.wait_ge(g_init, 3)

            def logits_of(st):
                r = st.ring(3)
                dve.wait_ge(n_lg, st.t + 1)
                dve.wait_ge(n_tok, st.t + 1)
                if st.after(3):
                    dve.wait_ge(g_lt, st.div(3))
                    dve.wait_ge(n_keep, st.t - 2)
                v.tensor_scalar(lg[:, r, :], bank(5, S), tok[:, r, :], None, ALU.mult).then_inc(n_L, 1)

            def group_max(q, par, cols):
                dve.wait_ge(g_lt, q + 1)
                v.tensor_reduce(gmax[:, :], ps[0:S, 6 * 512:6 * 512 + cols], AX.X, ALU.max).then_inc(g_max, 1)
                dve.wait_ge(g_max, q + 1)
                v.tensor_tensor(mrun[:, par, :], mrun[:, 1 - par, :], gmax[:, :], ALU.max).then_inc(g_new, 1)
                dve.wait_ge(g_new, q + 1)
                v.tensor_scalar(nneg[:, :], mrun[:, par, :], -1.0, None, ALU.mult).then_inc(g_neg, 1)

            def group_scale(q, first):
                dve.wait_ge(g_exp, q + 1)
                dve.wait_ge(g_c, q + 1)
                if not first:
                    dve.wait_ge(g_l, q)
                v.scalar_tensor_tensor(lrun[:, :], lrun[:, :], cc[0:S, :], dsum[:, :], ALU.mult, ALU.add).then_inc(g_l, 1)
                v.tensor_copy(cc[S:2 * S, :], cc[0:S, :]).then_inc(g_cd, 1)

            def group_weights(q, tiles, rows, s0):
                dve.wait_ge(g_back, q + 1)
                dve.wait_ge(n_gam, q * NG + tiles)
                v.tensor_tensor(pg[0:rows, 0:tiles, :],
                                ps[0:rows, 6 * 512:6 * 512 + tiles * S].rearrange("p (k s) -> p k s", s=S),
                                gam[0:rows, s0:s0 + tiles, :].broadcast_to([rows, tiles, S]), ALU.mult).then_inc(g_pg, 1)

            def group_sum(q):
                dve.wait_ge(g_y, q + 1)
                dve.wait_ge(g_cd, q + 1)
                v.scalar_tensor_tensor(ysum[:, :], ysum[:, :], cc[:, :], bank(7, HD), ALU.mult, ALU.add).then_inc(g_ya, 1)

            def node_step(st):
                r, k = st.ring(3), st.slot % NG
                dve.wait_ge(n_mm, st.t + 1)
                if st.after(3):
                    dve.wait_ge(n_st[r], 16 * st.div(3))
                dve.wait_ge(n_ag[r], 16 * st.div(3) + 16)
                v.tensor_tensor(gat[:, :], bank(3, D), agg[:, r, 0:D], ALU.add).then_inc(n_sum, 1)
                dve.wait_ge(n_sum, st.t + 1)
                v.scalar_tensor_tensor(x1[:, r, :], gat[:, :], 0.0, xn[:, r, :], ALU.max, ALU.add).then_inc(n_x1, 1)
                dve.wait_ge(n_x1, st.t + 1)
                v.bn_stats(bnn[:, 0:6], x1[:, r, 0:512])
                v.bn_stats(bnn[:, 6:12], x1[:, r, 512:D]).then_inc(n_bn, 1)
                dve.wait_ge(n_bn, st.t + 1)
                dve.sem_inc(n_go, 1)
                v.bn_aggr(mvn[:, r, :], bnn[:, :]).then_inc(n_mv, 1)
                if k == 2 and st.after(5):
                    group_scale(st.div(3) - 1, isinstance(st.t, int) and st.t < 6)
                if st.after(6):
                    dve.wait_ge(g_y, st.div(3) - 1)
                dve.wait_ge(n_mv, st.t + 1)
                v.scalar_tensor_tensor(uu[:, st.slot, :], x1[:, r, :], mvn[:, r, 0:1], wn[:, :],
                                       ALU.subtract, ALU.mult).then_inc(n_u, 1)
                if k == 0 and st.after(6):
                    group_sum(st.div(3) - 2)
                if st.after(2):
                    logits_of(st.shift(-2))
                if k == 1 and st.after(4):
                    group_max(st.div(3) - 1, (st.slot // NG + 1) % 2, NG * P)
                if k == 2 and st.after(5):
                    group_weights(st.div(3) - 1, NG, P, (st.slot + 1) % NU)

            walk(dve, FULL, NU, TAIL, node_step)
            last_step = Step(FULL, FULL // NU, 0, P)
            logits_of(last_step.shift(-1))
            logits_of(last_step)
            QL = FULL // NG
            group_max(QL - 1, (QL - 1) % 2, NG * P)
            group_scale(QL - 1, False)
            group_weights(QL - 1, NG, P, NG)
            group_sum(QL - 1)
            group_max(QL, QL % 2, TAIL)
            group_scale(QL, False)
            group_weights(QL, 1, TAIL, 0)
            group_sum(QL)

            link = chain_of(dve, f_d)
            dve.wait_ge(g_l, QL + 1)
            dve.wait_ge(g_ya, QL + 1)
            link(v.reciprocal(rlr[0:S, :], lrun[:, :]))
            link(v.tensor_copy(rlr[S:2 * S, :], rlr[0:S, :]))
            link(v.tensor_scalar(ysum[:, :], ysum[:, :], rlr[:, :], None, ALU.mult))
            dve.wait_ge(f_p, 1)
            for half in range(2):
                link(v.tensor_copy(yT[half * S:(half + 1) * S, :, :],
                                   ps[0:S, 0:C * P].rearrange("p (c q) -> p c q", q=P)[:, :, half * S:(half + 1) * S]))
            def first_windows(lap, first):
                for k in range(2):
                    n = lap * 2 + k
                    if not first:
                        dve.wait_ge(f_h, n - 1)
                        v.tensor_copy(yw[:, k, :, :, bass.ds(n - 2, 1)].rearrange("p j c a -> p j (c a)"),
                                      zeros[:, :, :])
                    v.tensor_copy(yw[:, k, :, :, bass.ds(n, 1)].rearrange("p j c a -> p j (c a)"),
                                  yT[:, :, bass.ds(n * G, G)].rearrange("p c j -> p j c")).then_inc(f_win, 1)
            dve.wait_ge(f_zero, 3)
            first_windows(0, True)
            with dve.Fori(1, QUADS // 2) as lap:
                first_windows(lap, False)

            cw = chain_of(dve, o_cw)
            dve.wait_ge(n_keep, NT)
            for i in range(3):
                dve.wait_ge(n_st[i], 16 * ring_uses(NT, 3, i))
                dve.wait_ge(n_ag[i], 16 * ring_uses(NT + 1, 3, i))
            dve.wait_ge(n_x[NT % 3], 16 * ring_uses(NT + 1, 3, NT % 3))
            dve.wait_ge(n_hh, NT + 1)
            v.memset(b1_sb[:, :], 0.0).then_inc(f_zero, 1)
            v.memset(b2_sb[:, :], 0.0).then_inc(f_zero, 1)
            cw(v.tensor_reduce(tmax[:, :], logits[:, :, :], AX.X, ALU.max))
            cw(v.tensor_tensor(logits[:, :, :], logits[:, :, :], tmax[:, :].unsqueeze(2).broadcast_to([P, NT, S]),
                               ALU.subtract))
            dve.wait_ge(o_cexp, 1)
            cw(v.tensor_reduce(tsum[:, :], logits[:, :, :], AX.X, ALU.add))
            cw(v.reciprocal(tsum[:, :], tsum[:, :]))
            cw(v.tensor_tensor(logits[:, :, :], logits[:, :, :], tsum[:, :].unsqueeze(2).broadcast_to([P, NT, S]),
                               ALU.mult))
            cw(v.tensor_copy(e12[:, :, 0:S], logits[:, :, :]))
            cw(v.tensor_copy(e13[:, :, 0:S], e12[:, :, 0:S]))
            cw(v.tensor_tensor(logits[:, :, :], logits[:, :, :], e12[:, :, 0:S], ALU.subtract))
            cw(v.tensor_copy(e12[:, :, S:2 * S], logits[:, :, :]))
            cw(v.tensor_tensor(e13[:, :, S:2 * S], logits[:, :, :], e12[:, :, S:2 * S], ALU.subtract))

            dve.wait_ge(f_in, 16 * 2 * G)
            dve.wait_ge(f_h, QUADS)
            for j in range(G):
                rows = slice(j * GR, (j + 1) * GR)
                link(v.tensor_tensor(hpre[rows, :], ps[rows, j * 512:j * 512 + F], b1_sb[rows, :], ALU.add))
            dve.wait_ge(f_p, 2)
            link(v.tensor_copy(hT[:, :], ps[0:F, 4 * 512:4 * 512 + P]))

            def second_windows(lap, first):
                for k in range(2):
                    n = lap * 2 + k
                    if not first:
                        dve.wait_ge(f_y, n - 1)
                        v.tensor_copy(hw[:, k, :, bass.ds(n - 2, 1)], zeros[0:F, :, 0:1])
                    v.tensor_copy(hw[:, k, :, bass.ds(n, 1)],
                                  hT[:, :].rearrange("f (j i) -> f j i", j=G)[:, :, bass.ds(n, 1)]).then_inc(f_hwin, 1)
            second_windows(0, True)
            with dve.Fori(1, QUADS // 2) as lap:
                second_windows(lap, False)
            dve.wait_ge(f_y, QUADS)
            for j in range(G):
                rows = slice(j * GR, (j + 1) * GR)
                link(v.tensor_tensor(y2[rows, :], ps[rows, 2 * j * 512:2 * j * 512 + D], b2_sb[rows, :], ALU.add))
            dve.wait_ge(f_yf, 16 * 2 * G)
            link(v.tensor_copy(y_a[:, :], yf[:, :]))
            link(v.tensor_tensor(yf[:, :], yf[:, :], y_a[:, :], ALU.subtract))
            link(v.tensor_copy(y_b[:, :], yf[:, :]))
            link(v.tensor_tensor(y_c[0:S, :], yf[0:S, :], y_b[0:S, :], ALU.subtract))
            link(v.tensor_copy(y_c[S:2 * S, :], y_a[S:2 * S, :]))

            def out_step(st):
                b = st.ring(2)
                dve.wait_ge(o_x[st.slot], 16 * (st.lap + 1))
                if st.after(3):
                    dve.wait_ge(o_out[st.ring(3)], 16 * st.div(3))
                dve.wait_ge(o_mm, st.t + 1)
                v.tensor_tensor(oo[:, st.ring(3), :], bank(2 * b, D), xo[:, st.slot, :], ALU.add).then_inc(o_o, 1)
            walk(dve, FULL, NU, TAIL, out_step)


def kernel(**inputs):
    import numpy as _np
    import concourse.bacc as _bacc
    from concourse import mybir as _mybir
    from concourse.bass_utils import run_bass_kernel_spmd as _run

    a = {k: _np.asarray(v) for k, v in inputs.items()}
    arrays = {
        "x": a["x"], "src": a["src"], "dst": a["dst"],
        "w_cat": _np.concatenate([a["L0_gnn_W_res"].T, a["L0_gnn_W_fc"].T], axis=0),
        "w_fc": a["L0_gnn_W_fc"],
        "attn": _np.concatenate([a["L0_gnn_attn_l"].T, a["L0_gnn_attn_r"].T], axis=1),
        "slots": a["L0_ffn_slots"], "scale": a["L0_ffn_scale"],
        "w1": a["L0_ffn_fc1_weight"], "b1": a["L0_ffn_fc1_bias"],
        "w2": a["L0_ffn_fc2_weight"], "b2": a["L0_ffn_fc2_bias"], "norm_w": a["L0_ffn_norm_weight"],
    }
    arrays = {k: _np.ascontiguousarray(v) for k, v in arrays.items()}
    nc = _bacc.Bacc("TRN2", target_bir_lowering=False, num_devices=1)
    args = [nc.dram_tensor(k, v.shape, _mybir.dt.from_np(v.dtype), kind="ExternalInput").ap()
            for k, v in arrays.items()]
    out = nc.dram_tensor("out", a["x"].shape, F32, kind="ExternalOutput").ap()
    build(nc, *args, out)
    r = _run(nc, [arrays], core_ids=[0])
    return r.results[0]["out"]
```

```python
import concourse.bass as bass
from concourse import mybir
from concourse.alu_op_type import AluOpType as ALU
from contextlib import ExitStack

F32 = mybir.dt.float32
BF16 = mybir.dt.bfloat16
I32 = mybir.dt.int32
ACT = mybir.ActivationFunctionType
AX = mybir.AxisListType

P = 128
LAP = 6
BIG = 1.0e38
EPS = 1e-5
SLOPE = 0.2
TAB = 16
SHIFT, RSTD = 12, 13


class Step:

    def __init__(self, t, lap, slot, rows):
        self.t, self.lap, self.slot, self.rows = t, lap, slot, rows

    def ring(self, depth):
        return self.slot % depth

    def div(self, depth):
        return self.lap * (LAP // depth) + self.slot // depth

    def after(self, depth):
        return not isinstance(self.t, int) or self.t >= depth

    def shift(self, by):
        over = (self.slot + by) // LAP
        return Step(self.t + by, self.lap + over, (self.slot + by) % LAP, P)


def ring_uses(tiles, depth, slot):
    return (tiles - slot + depth - 1) // depth


def walk(eng, full, unroll, tail_rows, body, first_lap=True):
    for t in range(unroll if first_lap else 0):
        body(Step(t, 0, t, P))
    with eng.Fori(1, full // unroll) as lap:
        for k in range(unroll):
            body(Step(lap * unroll + k, lap, k, P))
    if tail_rows:
        body(Step(full, full // unroll, 0, tail_rows))


def build(nc, x, src, dst, w_cat, w_fc, attn, slots, scale, w1, b1, w2, b2, norm_w, out):
    N, D = x.shape
    H, DH = attn.shape[1] // 2, w_fc.shape[0]
    S, _, F = w1.shape
    FULL, TAIL = N // P, N % P
    NT = FULL + 1
    C = D // P
    ET = 80
    EG = 4
    GROUPS = ET // EG
    HV = 512 // DH
    PAD_NODE = ET * P - 1
    ROW = D + 2 * H
    NU = LAP
    HD = D // 2
    G = 4
    GR = P // G
    QUADS = S // G
    WR = 4
    FC = 2 * DH + 4
    A1C, A2C = 2 * DH, 2 * DH + 2
    WIDE = C * FC
    POOL_SET = 10
    NG = 3
    LAPS_E = ET // (2 * EG)
    E_FULL, E_TAIL = src.shape[0] // P, src.shape[0] % P

    node_rows = nc.dram_tensor("node_rows", (N, WIDE), F32).ap()
    node_table = nc.dram_tensor("node_table", (N, TAB), F32).ap()
    seg_rows = nc.dram_tensor("seg_rows", (ET * P, ROW), F32).ap()
    dst_padded = nc.dram_tensor("dst_padded", (ET, P), I32).ap()
    x1_dram = nc.dram_tensor("x1_dram", (N, D), F32).ap()

    ctx = ExitStack()
    with ctx:
        def sb(name, shape, dt=F32):
            return ctx.enter_context(nc.sbuf_tensor(name, shape, dt))

        def sem(name):
            return ctx.enter_context(nc.semaphore(name))

        ident = sb("ident", [P, P])
        wres = sb("wres", [P, P])
        wfc = sb("wfc", [P, C, FC])
        slT = sb("slT", [P, C, S])
        wn = sb("wn", [P, D])
        table = sb("table", [P, NT + 1, TAB])
        logits = sb("logits", [P, NT, S])
        src_i = sb("src_i", [P, ET], I32)
        dst_i = sb("dst_i", [P, ET], I32)
        dst_f = sb("dst_f", [P, ET])
        hi_f = sb("hi_f", [P, ET])
        lo_f = sb("lo_f", [P, ET])
        iota_f = sb("iota_f", [P, P])
        flag_t = sb("flag_t", [P, ET])
        pos_i = sb("pos_i", [P, ET], I32)
        first_end = sb("first_end", [ET, 1], I32)
        chain = sb("chain", [ET, ET])
        tri = sb("tri", [ET, ET])
        kc = sb("kc", [P, 4])
        ones = sb("ones", [P, P])
        ident_b = sb("ident_b", [P, P], BF16)
        yT = sb("yT", [P, C, S])
        rlr = sb("rlr", [P, 1])
        zeros = sb("zeros", [P, G, C])
        w1b = sb("w1b", [P, 2, G, C * F])
        w2b = sb("w2b", [F, 2, G, D])
        yw = sb("yw", [P, 2, G, C, GR])
        hw = sb("hw", [F, 2, G, GR])
        tmax = sb("tmax", [P, NT])
        tsum = sb("tsum", [P, NT])

        ph = ExitStack()

        def scratch(name, shape, dt=F32):
            return ph.enter_context(nc.sbuf_tensor(name, shape, dt))

        e_src = scratch("e_src", [ET, P], I32)
        e_dst = scratch("e_dst", [ET, P], I32)
        e_srcf = scratch("e_srcf", [ET, P])
        e_dstf = scratch("e_dstf", [ET, P])
        e_flag = scratch("e_flag", [ET, P])
        e_eq = scratch("e_eq", [ET, P])
        e_cnt = scratch("e_cnt", [ET, 1])
        e_base = scratch("e_base", [ET, 1], I32)
        e_basef = scratch("e_basef", [ET, 1])
        sel_last = scratch("sel_last", [P, ET])
        dst_ti = scratch("dst_ti", [P, ET], I32)
        hi_i = scratch("hi_i", [P, ET], I32)
        lo_i = scratch("lo_i", [P, ET], I32)
        iota_i = scratch("iota_i", [P, P], I32)
        wfc2 = scratch("wfc2", [DH, 2 * DH])
        wfcT = scratch("wfcT", [P, DH])
        frow = scratch("frow", [P, NU, WIDE])
        attn_sb = scratch("attn_sb", [DH, 2 * H])
        slots_sb = scratch("slots_sb", [S, D])
        slots_sq = scratch("slots_sq", [S, D])
        scale_sb = scratch("scale_sb", [S, 1])
        s_norm = scratch("s_norm", [S, 4])
        xa = scratch("xa", [P, 6, D])
        ha = scratch("ha", [P, 2, D])
        haT = scratch("haT", [P, 2, D])
        bna = scratch("bna", [P, 2, 12])
        mva = scratch("mva", [P, 2, 4])
        ph.close()

        ph = ExitStack()
        XR = 2 * EG
        dst_row = scratch("dst_row", [P, 2, EG * P], I32)
        ix_s = scratch("ix_s", [P, 2, EG], I32)
        ix_d = scratch("ix_d", [P, 2, EG], I32)
        tg_d = scratch("tg_d", [P, 2, EG, TAB])
        dsc = scratch("dsc", [P, 2, EG])
        sc = scratch("sc", [P, EG, H])
        lk = scratch("lk", [P, EG, H])
        fb = scratch("fb", [P, EG, H])
        flagT = scratch("flagT", [EG * H, P + 1])
        pmax = scratch("pmax", [EG * H, P])
        smax = scratch("smax", [EG * H, P])
        dif = scratch("dif", [EG * H, P])
        eeT = scratch("eeT", [EG * H, P])
        eem = scratch("eem", [P, 2, 2, EG, H])
        hot_hi = scratch("hot_hi", [P, 2, EG, ET], BF16)
        hot_lo = scratch("hot_lo", [P, 2, EG, P], BF16)
        deg = scratch("deg", [ET, P])
        xg = scratch("xg", [P, XR, WIDE])
        vv = scratch("vv", [P, EG, D])
        same = scratch("same", [P, EG, P])
        rl = scratch("rl", [P, 2, H])
        zo = scratch("zo", [P, 4, ROW])
        cum = scratch("cum", [ET, P])
        none = scratch("none", [ET, P])
        off_sb = scratch("off_sb", [ET, 1])
        pos_f = scratch("pos_f", [ET, P])
        rr = scratch("rr", [ET, ROW])
        ff = scratch("ff", [ET, ROW])
        bd = scratch("bd", [ET, H, ET])
        bm = scratch("bm", [ET, H, ET])
        be = scratch("be", [ET, H, ET])
        bwT = scratch("bwT", [ET, H, ET])
        bmax = scratch("bmax", [ET, H])
        bdf = scratch("bdf", [ET, H])
        bcf = scratch("bcf", [ET, H])
        btot = scratch("btot", [ET, H])
        bz = scratch("bz", [ET, D])
        ph.close()

        ph = ExitStack()
        xn = scratch("xn", [P, NU, D])
        ixn = scratch("ixn", [P, 3, 1], I32)
        mr = scratch("mr", [P, 3, 2])
        hn = scratch("hn", [P, 3, D])
        hnT = scratch("hnT", [P, D])
        agg = scratch("agg", [P, 3, ROW])
        gat = scratch("gat", [P, D])
        x1 = scratch("x1", [P, 3, D])
        uu = scratch("uu", [P, NU, D])
        usq = scratch("usq", [P, D])
        uT = scratch("uT", [P, D])
        bnn = scratch("bnn", [P, 12])
        mvn = scratch("mvn", [P, 3, 2])
        usum = scratch("usum", [P, 3, 1])
        gam = scratch("gam", [P, NU, 1])
        pw = scratch("pw", [P, 6])
        tok = scratch("tok", [P, 3, 1])
        lg = scratch("lg", [P, 3, S])
        mrun = scratch("mrun", [S, 2, 1])
        nneg = scratch("nneg", [S, 1])
        gmax = scratch("gmax", [S, 1])
        cc = scratch("cc", [P, 1])
        dT = scratch("dT", [S, NG * P])
        dsum = scratch("dsum", [S, 1])
        lrun = scratch("lrun", [S, 1])
        pg = scratch("pg", [P, NG, S])
        ysum = scratch("ysum", [P, HD])
        ph.close()

        ph = ExitStack()
        w1x = scratch("w1x", [P, 2, G, C * F])
        w2x = scratch("w2x", [F, 2, G, D])
        e12 = scratch("e12", [P, NT, P], BF16)
        e13 = scratch("e13", [P, NT, P], BF16)
        b1_sb = scratch("b1_sb", [P, F])
        hpre = scratch("hpre", [P, F])
        hact = scratch("hact", [P, F])
        hT = scratch("hT", [F, P])
        b2_sb = scratch("b2_sb", [P, D])
        y2 = scratch("y2", [P, D])
        yf = scratch("yf", [P, D])
        y_a = scratch("y_a", [P, D], BF16)
        y_b = scratch("y_b", [P, D], BF16)
        y_c = scratch("y_c", [P, D], BF16)
        xo = scratch("xo", [P, 6, D])
        exT = scratch("exT", [P, 2, 2 * P], BF16)
        ph.close()

        ps = ctx.enter_context(nc.psum_tensor("ps", [P, 8 * 512], F32))

        def bank(b, n=512, at=0):
            return ps[:, b * 512 + at:b * 512 + at + n]

        def sems(names):
            return [sem(n) for n in names.split()]

        s_in, s_edge_in, s_edge_pad, s_dstp, s_ident, s_pool = sems("s_in s_edge_in s_edge_pad s_dstp s_ident s_pool")
        s_dve, s_pe = sems("s_dve s_pe")
        s_copies, s_sq = sems("s_copies s_sq")

        xa_in = [sem(f"xa_in_{i}") for i in range(6)]
        a_bn, a_mv, a_ve, a_rstd, a_hh, a_mr, a_tr, a_ev, a_att, a_row, a_tab, a_out = sems(
            "a_bn a_mv a_ve a_rstd a_hh a_mr a_tr a_ev a_att a_row a_tab a_out")
        a_st = [sem(f"a_st_{i}") for i in range(NU)]

        e_row = [sem(f"e_row_{i}") for i in range(2)]
        e_tab = [sem(f"e_tab_{i}") for i in range(2)]
        e_x = [sem(f"e_x_{i}") for i in range(XR)]
        e_out = [sem(f"e_out_{i}") for i in range(4)]
        e_ix, e_sc, e_fb, e_tr, e_flag_ev, e_pm, e_sm, e_dif = sems(
            "e_ix e_sc e_fb e_tr e_flag_ev e_pm e_sm e_dif")
        e_exp, e_back, e_em, e_hist, e_deg, e_init = sems(
            "e_exp e_back e_em e_hist e_deg e_init")
        e_vv, e_same, e_mm, e_z, e_za, e_lcp, e_va, go = sems("e_vv e_same e_mm e_z e_za e_lcp e_va go")
        b_in, b_ff, b_fix, b_dve, b_pe, b_act = sems("b_in b_ff b_fix b_dve b_pe b_act")

        n_x = [sem(f"n_x_{i}") for i in range(NU)]
        n_ag = [sem(f"n_ag_{i}") for i in range(3)]
        n_st = [sem(f"n_st_{i}") for i in range(3)]
        n_ix, n_mr, n_hh, n_t1, n_ev1, n_mm, n_sum, n_x1, n_bn, n_mv, n_u, n_sq = sems(
            "n_ix n_mr n_hh n_t1 n_ev1 n_mm n_sum n_x1 n_bn n_mv n_u n_sq")
        n_t3, n_ev3, n_lg, n_pw, n_gam, n_tok, n_L, n_keep = sems(
            "n_t3 n_ev3 n_lg n_pw n_gam n_tok n_L n_keep")
        g_init, g_lt, g_max, g_new, g_neg, g_exp, g_back, g_pg, g_y, g_l, g_ya = sems(
            "g_init g_lt g_max g_new g_neg g_exp g_back g_pg g_y g_l g_ya")
        f_in, f_d, f_p, f_a, f_h, f_y, f_win, f_zero = sems("f_in f_d f_p f_a f_h f_y f_win f_zero")
        f_w1 = [sem(f"f_w1_{i}") for i in range(WR)]
        f_w2 = [sem(f"f_w2_{i}") for i in range(WR)]
        o_x = [sem(f"o_x_{i}") for i in range(6)]
        o_out = [sem(f"o_out_{i}") for i in range(NU)]
        o_cw, o_cexp, o_t, o_ev, o_mm, o_o = sems("o_cw o_cexp o_t o_ev o_mm o_o")

        IN_DMAS = 16 * 10

        def tile_rows(st):
            return bass.ds(st.t * P, st.rows)

        CW = 8
        F_OUT = 14

        def chain_of(eng, s, start=0):
            n = [start]

            def link(ins):
                n[0] += 1
                ins.then_inc(s, 1)
                eng.wait_ge(s, n[0])
            return link

        def edge_groups(eng, main):
            def lap_of(lap, last):
                main(lap, 0, lap * 2, (lap, 1, lap * 2 + 1))
                main(lap, 1, lap * 2 + 1, None if last else (lap + 1, 0, lap * 2 + 2))
            lap_of(0, False)
            with eng.Fori(1, LAPS_E - 1) as lap:
                lap_of(lap, False)
            lap_of(LAPS_E - 1, True)

        def starts(n):
            return isinstance(n, int) and n < 2

        LOGITS = (5, 2)

        def w1_slot(k):
            return w1b[:, k, :, :] if k < 2 else w1x[:, k - 2, :, :]

        def w2_slot(k):
            return w2b[:, k, :, :] if k < 2 else w2x[:, k - 2, :, :]

        def nodes_left(eng):
            eng.wait_ge(f_p, 1)
            eng.wait_ge(n_keep, NT)
            eng.wait_ge(n_hh, NT + 1)
            eng.wait_ge(n_x[NT % NU], 16 * ring_uses(NT + 1, NU, NT % NU))
            for i in range(3):
                eng.wait_ge(n_ag[i], 16 * ring_uses(NT + 1, 3, i))
                eng.wait_ge(n_st[i], 16 * ring_uses(NT, 3, i))

        block = ctx.enter_context(nc.Block())


        @block.sync
        def _(sp):
            sp.wait_ge(s_edge_pad, 2)
            for buf, lst in ((e_src, src), (e_dst, dst)):
                sp.dma_start(buf[0:E_FULL, :], lst[0:E_FULL * P].rearrange("(k p) -> k p", p=P)).then_inc(s_edge_in, 16)
                sp.dma_start(buf[E_FULL:E_FULL + 1, 0:E_TAIL],
                             lst[E_FULL * P:].rearrange("(a p) -> a p", a=1)).then_inc(s_edge_in, 16)
            sp.dma_start(wfc2[:, 0:DH], w_fc[:, :]).then_inc(s_in, 16)
            sp.dma_start(wfc2[:, DH:2 * DH], w_fc[:, :]).then_inc(s_in, 16)
            sp.dma_start(attn_sb[:, :], attn[:, :]).then_inc(s_in, 16)
            for half in range(2):
                rows = slice(half * DH, (half + 1) * DH)
                sp.dma_start(wfcT[rows, :], w_cat[DH:2 * DH, :]).then_inc(s_in, 16)
            sp.wait_ge(s_edge_pad, 3)
            for half in range(2):
                rows = slice(half * DH, (half + 1) * DH)
                sp.dma_start(wres[rows, rows], w_cat[0:DH, :]).then_inc(s_in, 16)
            sp.dma_start(slots_sb[:, :], slots[:, :]).then_inc(s_in, 16)
            sp.dma_start(scale_sb[:, :], scale.rearrange("(s a) -> s a", a=1)).then_inc(s_in, 16)
            sp.dma_start(wn[:, :], norm_w.partition_broadcast(P)).then_inc(s_in, 16)
            sp.wait_ge(s_edge_in, 64)
            sp.dma_start(dst_padded[:, :], e_dst[:, :]).then_inc(s_dstp, 16)

            def load_x(st):
                if st.after(6):
                    sp.wait_ge(a_hh, st.t - 5)
                sp.dma_start(xa[0:st.rows, st.slot, :], x[tile_rows(st), :]).then_inc(xa_in[st.slot], 16)

            def store_row(st):
                sp.wait_ge(a_row, st.t + 1)
                sp.dma_start(node_rows[tile_rows(st), :], frow[0:st.rows, st.slot, :]).then_inc(a_st[st.slot], 16)

            def stats_io(st):
                load_x(st)
                if st.after(NU):
                    store_row(st.shift(-NU))
            walk(sp, FULL, NU, TAIL, stats_io)
            for t in range(NT - NU, NT):
                store_row(Step(t, t // NU, t % NU, P if t < FULL else TAIL))

            sp.wait_ge(s_dstp, 16)
            sp.wait_ge(a_tab, NT)
            for i in range(NU):
                sp.wait_ge(a_st[i], 16 * ring_uses(NT, NU, i))

            def row_in(lap, gb):
                sp.dma_start(dst_row[:, gb, :],
                             dst_padded[bass.ds(lap * 2 * EG + gb * EG, EG), :]
                             .rearrange("k p -> (k p)").partition_broadcast(P)).then_inc(e_row[gb], 16)

            def rows_out(lap, k):
                t = lap * XR + k
                sp.wait_ge(e_z, t + 1)
                sp.wait_ge(e_za, t + 1)
                sp.wait_ge(e_lcp, t + 1)
                sp.dma_start(seg_rows[bass.ds(t * P, P), :], zo[:, k % 4, :]).then_inc(e_out[k % 4], 16)

            def rows_io(lap, gb, n, ahead):
                if ahead:
                    if not (isinstance(n, int) and n == 0):
                        sp.wait_ge(e_same, n * EG)
                    row_in(*ahead[:2])
                for j in range(EG):
                    rows_out(lap, gb * EG + j)
            row_in(0, 0)
            edge_groups(sp, rows_io)
            for j in range(4):
                sp.wait_ge(e_out[j], 16 * (ET // 4))
            sp.dma_start(rr[:, :], seg_rows.rearrange("(k p) r -> k p r", p=P)[:, P - 1, :]).then_inc(b_in, 16)

            def load_w1(lap, k):
                sp.dma_start(w1_slot(k), w1[bass.ds((lap * WR + k) * G, G)]
                             .rearrange("s (p c) f -> p s (c f)", p=P)).then_inc(f_w1[k], 16)

            def load_w2(lap, k):
                sp.dma_start(w2_slot(k), w2[bass.ds((lap * WR + k) * G, G)]
                             .rearrange("s f d -> f s d")).then_inc(f_w2[k], 16)

            sp.wait_ge(b_ff, 16)
            for k in range(2):
                load_w1(0, k)
                load_w2(0, k)

            sp.wait_ge(b_fix, 16)

            def store_x1(st):
                sp.wait_ge(n_x1, st.t + 1)
                sp.dma_start(x1_dram[tile_rows(st), :], x1[0:st.rows, st.ring(3), :]).then_inc(n_st[st.ring(3)], 16)

            def nodes_io(st):
                if st.after(NU):
                    sp.wait_ge(n_x1, st.t - 5)
                sp.dma_start(xn[0:st.rows, st.slot, :], x[tile_rows(st), :]).then_inc(n_x[st.slot], 16)
                if st.after(3):
                    store_x1(st.shift(-3))

            walk(sp, FULL, NU, TAIL, nodes_io)
            for t in range(NT - 3, NT):
                store_x1(Step(t, t // NU, t % NU, P if t < FULL else TAIL))
                if t == NT - 3:
                    sp.dma_start(xn[:, NT % NU, :], x[N - P:N, :]).then_inc(n_x[NT % NU], 16)
            nodes_left(sp)
            for k in range(2, WR):
                load_w1(0, k)
            for k in range(2, WR):
                load_w2(0, k)
            with sp.Fori(1, QUADS // WR) as lap:
                for k in range(WR):
                    sp.wait_ge(f_h, (lap - 1) * WR + k + 1)
                    load_w1(lap, k)
            sp.wait_ge(f_zero, 5)
            for j in range(G):
                for buf, vec in ((b1_sb, b1), (b2_sb, b2)):
                    sp.dma_start(buf[j * GR:j * GR + QUADS, :], vec.rearrange("(i j) f -> j i f", j=G)[j]).then_inc(f_in, 16)
            with sp.Fori(1, QUADS // WR) as lap:
                for k in range(WR):
                    sp.wait_ge(f_y, (lap - 1) * WR + k + 1)
                    load_w2(lap, k)
            for j in range(G):
                sp.wait_ge(f_d, F_OUT - G + 1 + j)
                for half in range(2):
                    sp.dma_start(yf[half * S + j:half * S + S:G, :], y2[j * GR:j * GR + QUADS, :]).then_inc(f_in, 16)

            def store_out(st):
                sp.wait_ge(o_o, st.t + 1)
                sp.dma_start(out[tile_rows(st), :], xo[0:st.rows, st.slot, :]).then_inc(o_out[st.slot], 16)
            walk(sp, FULL, NU, TAIL, store_out)
            for i in range(NU):
                sp.wait_ge(o_out[i], 16 * ring_uses(NT, NU, i))

        @block.gpsimd
        def _(g):
            g.memset(e_src[:, :], 0).then_inc(s_edge_pad, 1)
            g.memset(e_dst[:, :], PAD_NODE).then_inc(s_edge_pad, 1)
            g.memset(wres[:, :], 0.0).then_inc(s_edge_pad, 1)
            g.memset(ident[:, :], 0.0).then_inc(s_ident, 1)
            for i, v in enumerate((-0.5, EPS, 1.0 + EPS, EPS * EPS)):
                g.memset(kc[:, i:i + 1], v).then_inc(s_pool, 1)
            g.memset(ones[:, :], 1.0).then_inc(s_pool, 1)
            g.iota(iota_i[:, :], pattern=[[1, P]], base=0, channel_multiplier=0).then_inc(s_pool, 1)
            g.iota(e_base[:, :], pattern=[[0, 1]], base=-1, channel_multiplier=P).then_inc(s_pool, 1)
            g.memset(tri[:, :], 1.0).then_inc(s_pool, 1)
            g.memset(table[:, :, :], 0.0).then_inc(s_pool, 1)
            g.wait_ge(s_ident, 1)
            g.affine_select(out=ident[:, :], in_=ident[:, :], compare_op=ALU.not_equal, fill=1.0, base=0,
                            pattern=[[-1, P]], channel_multiplier=1).then_inc(s_ident, 1)
            g.wait_ge(s_pool, POOL_SET - 1)
            g.affine_select(out=tri[:, :], in_=tri[:, :], compare_op=ALU.is_gt, fill=0.0, base=0,
                            pattern=[[1, ET]], channel_multiplier=-1).then_inc(s_pool, 1)
            g.wait_ge(s_sq, 1)
            g.tensor_scalar(s_norm[:, 1:2], s_norm[:, 0:1], EPS * EPS, None, ALU.max).then_inc(s_pool, 1)
            g.wait_ge(s_pool, POOL_SET + 1)
            g.tensor_tensor(s_norm[:, 2:3], s_norm[:, 1:2], kc[0:S, 0:1], ALU.pow).then_inc(s_pool, 1)

            def rstd(st):
                b = st.ring(2)
                g.wait_ge(a_mv, st.t + 1)
                g.tensor_tensor(mva[:, b, 2:3], mva[:, b, 1:2], kc[:, 1:2], ALU.add).then_inc(a_ve, 1)
                g.wait_ge(a_ve, st.t + 1)
                g.tensor_tensor(mva[:, b, 3:4], mva[:, b, 2:3], kc[:, 0:1], ALU.pow).then_inc(a_rstd, 1)
            walk(g, FULL, NU, TAIL, rstd)

            g.wait_ge(a_tab, NT)
            g.wait_ge(a_out, 16 * (FULL // NU + 1))

            for i in range(NU):
                g.wait_ge(a_st[i], 16 * ring_uses(NT, NU, i))

            def group_rows(lap, gb, first):
                if not first:
                    for j in range(EG):
                        g.wait_ge(e_x[gb * EG + j], lap * 16)
                    g.wait_ge(e_tab[gb], lap * 16 * EG)
                    g.sem_inc(go, 1)
                base = lap * XR + gb * EG
                g.tensor_copy(ix_s[:, gb, :], src_i[:, bass.ds(base, EG)]).then_inc(e_ix, 1)
                g.tensor_copy(ix_d[:, gb, :], dst_i[:, bass.ds(base, EG)]).then_inc(e_ix, 1)
                g.wait_ge(e_ix, (lap * 2 + gb) * 2 + 2)
                if not first:
                    g.wait_ge(e_sc, lap * 2 + gb - 1)
                g.sem_inc(go, 1)
                for j in range(EG):
                    g.indirect_dma_start(
                        out=tg_d[:, gb, j, :], out_offset=None, in_=node_table[:, :],
                        in_offset=bass.IndirectOffsetOnAxis(ap=ix_d[:, gb, j:j + 1], axis=0))\
                        .then_inc(e_tab[gb], 16)
                for j in range(EG):
                    slot = gb * EG + j
                    if not first:
                        g.wait_ge(e_vv, (lap - 1) * XR + slot + 1)
                        g.wait_ge(e_va, (lap - 1) * XR + slot + 1)
                        g.sem_inc(go, 1)
                    g.indirect_dma_start(
                        out=xg[:, slot, :], out_offset=None, in_=node_rows[:, :],
                        in_offset=bass.IndirectOffsetOnAxis(ap=ix_s[:, gb, j:j + 1], axis=0))\
                        .then_inc(e_x[slot], 16)

            g.wait_ge(s_dve, 16)
            for gb in range(2):
                group_rows(0, gb, True)
            with g.Fori(1, LAPS_E) as lap:
                for gb in range(2):
                    group_rows(lap, gb, False)

            for j in range(4):
                g.wait_ge(e_out[j], 16 * (ET // 4))
            g.indirect_dma_start(out=ff[:, :], out_offset=None, in_=seg_rows[:, :],
                                 in_offset=bass.IndirectOffsetOnAxis(ap=first_end[:, 0:1], axis=0)).then_inc(b_ff, 16)
            g.wait_ge(b_dve, 22)
            g.wait_ge(b_in, 16)
            g.indirect_dma_start(out=seg_rows[:, :], in_=ff[:, :], in_offset=None,
                                 out_offset=bass.IndirectOffsetOnAxis(ap=first_end[:, 0:1], axis=0)).then_inc(b_fix, 16)

            g.wait_ge(b_fix, 16)

            def gather(st, first):
                r, u = st.ring(3), st.t
                if not first:
                    g.wait_ge(n_sum, u - 2)
                    g.wait_ge(n_hh, u - 2)
                    g.wait_ge(n_ag[r], 16 * st.div(3))
                    g.sem_inc(go, 1)
                g.tensor_copy(ixn[:, r, :], pos_i[:, bass.ds(u, 1)]).then_inc(n_ix, 1)
                g.tensor_copy(mr[:, r, :], table[:, bass.ds(u, 1), SHIFT:RSTD + 1]).then_inc(n_mr, 1)
                g.memset(agg[:, r, :], 0.0).then_inc(n_ix, 1)
                g.wait_ge(n_ix, u * 2 + 2)
                g.sem_inc(go, 1)
                g.indirect_dma_start(out=agg[:, r, :], out_offset=None, in_=seg_rows[:, :],
                                     in_offset=bass.IndirectOffsetOnAxis(ap=ixn[:, r, :], axis=0),
                                     bounds_check=ET * P - 1, oob_is_err=False).then_inc(n_ag[r], 16)

            def norms(st):
                u, r, s6 = st.t, st.ring(3), st.slot
                base = u * 6
                g.wait_ge(n_mv, u + 1)
                g.tensor_tensor(pw[:, 0:1], mvn[:, r, 1:2], kc[:, 2:3], ALU.mult).then_inc(n_pw, 1)
                g.wait_ge(n_pw, base + 1)
                g.tensor_tensor(pw[:, 1:2], pw[:, 0:1], kc[:, 3:4], ALU.add).then_inc(n_pw, 1)
                g.wait_ge(n_pw, base + 2)
                if st.after(6):
                    g.wait_ge(g_pg, st.div(3) - 1)
                g.tensor_tensor(gam[:, s6, :], pw[:, 1:2], kc[:, 0:1], ALU.pow).then_inc(n_gam, 1)
                g.wait_ge(n_gam, u + 1)
                g.tensor_tensor(pw[:, 2:3], gam[:, s6, :], gam[:, s6, :], ALU.mult).then_inc(n_pw, 1)
                g.wait_ge(n_pw, base + 3)
                g.wait_ge(n_sq, u + 1)
                g.tensor_tensor(pw[:, 3:4], pw[:, 2:3], usum[:, r, :], ALU.mult).then_inc(n_pw, 1)
                g.wait_ge(n_pw, base + 4)
                g.sem_inc(go, 1)
                g.tensor_scalar(pw[:, 4:5], pw[:, 3:4], EPS * EPS, None, ALU.max).then_inc(n_pw, 1)
                g.wait_ge(n_pw, base + 5)
                g.tensor_tensor(pw[:, 5:6], pw[:, 4:5], kc[:, 0:1], ALU.pow).then_inc(n_pw, 1)
                g.wait_ge(n_pw, base + 6)
                if st.after(3):
                    g.wait_ge(n_L, u - 2)
                g.tensor_tensor(tok[:, r, :], gam[:, s6, :], pw[:, 5:6], ALU.mult).then_inc(n_tok, 1)

            def node_step(st):
                if not (isinstance(st.t, int) and st.t == FULL):
                    gather(st.shift(2), isinstance(st.t, int) and st.t == 0)
                if st.after(1):
                    norms(st.shift(-1))
            g.wait_ge(b_dve, 6)
            gather(Step(0, 0, 0, P), True)
            gather(Step(1, 0, 1, P), True)
            walk(g, FULL, NU, TAIL, node_step)
            norms(Step(FULL, FULL // NU, 0, P))

            nodes_left(g)

            def load_x1(st):
                if st.after(6):
                    g.wait_ge(o_out[st.slot], 16 * st.lap)
                    g.sem_inc(go, 1)
                g.dma_start(xo[0:st.rows, st.slot, :], x1_dram[tile_rows(st), :]).then_inc(o_x[st.slot], 16)
            for t in range(NU):
                load_x1(Step(t, 0, t, P))

            def windows(lap, first, win, used, ready, write):
                for k in range(2):
                    n = lap * 2 + k
                    if not first:
                        g.wait_ge(used, n - 1)
                        g.sem_inc(go, 1)
                        write(win[:, k], n - 2, True)
                    write(win[:, k], n, False).then_inc(ready, 1)

            def put_y(win, n, clear):
                return g.tensor_copy(win[:, :, :, bass.ds(n, 1)].rearrange("p j c a -> p j (c a)"),
                                     zeros[:, :, :] if clear else yT[:, :, bass.ds(n * G, G)].rearrange("p c j -> p j c"))

            def put_h(win, n, clear):
                return g.tensor_copy(win[:, :, bass.ds(n, 1)], zeros[0:F, :, 0:1] if clear else
                                     hT[:, :].rearrange("f (j i) -> f j i", j=G)[:, :, bass.ds(n, 1)])

            g.wait_ge(f_zero, 3)
            g.wait_ge(f_d, 5)
            windows(0, True, yw, f_h, f_win, put_y)
            with g.Fori(1, QUADS // 2) as lap:
                windows(lap, False, yw, f_h, f_win, put_y)
            g.wait_ge(f_d, 6 + G)
            windows(0, True, hw, f_y, f_win, put_h)
            with g.Fori(1, QUADS // 2) as lap:
                windows(lap, False, hw, f_y, f_win, put_h)

            walk(g, FULL, NU, TAIL, load_x1, first_lap=False)

        @block.tensor
        def _(pe):
            mm, tr = nc.tensor.matmul, nc.tensor.transpose

            pe.wait_ge(s_in, IN_DMAS)
            mm(bank(6, 2 * H), wfc2[:, :], attn_sb[:, :], start=True, stop=True).then_inc(s_pe, 1)
            pe.wait_ge(s_ident, 2)
            pe.wait_ge(s_dve, 4)
            for i, m in enumerate((e_srcf, e_dstf, e_flag)):
                last = tr(bank(7, ET, i * ET), m[:, :], ident[0:ET, 0:ET])
            last.then_inc(s_pe, 1)
            pe.wait_ge(s_dve, 6)
            mm(ps[0:ET, 7 * 512 + 256:7 * 512 + 256 + ET], sel_last[:, :], dst_f[:, :], start=True, stop=True)\
                .then_inc(s_pe, 1)
            pe.wait_ge(s_copies, 11)
            pe.wait_ge(s_dve, 16)
            for c in range(C):
                last = tr(bank(7, S, c * S), slots_sq[:, c * P:(c + 1) * P], ident[0:S, 0:S])
            last.then_inc(s_pe, 1)

            pe.wait_ge(s_dve, 23)

            def attention(st):
                b = st.ring(2)
                pe.wait_ge(a_ev, st.t + 1)
                if st.after(2):
                    pe.wait_ge(a_row, st.t - 1)
                    pe.wait_ge(a_tab, st.t - 1)
                for c in range(C):
                    last = mm(bank(4 + 2 * b + c // 3, FC, c % 3 * FC), haT[:, b, c * P:(c + 1) * P], wfc[:, c, :],
                              start=True, stop=True)
                last.then_inc(a_att, 1)

            def stats_step(st):
                b = st.ring(2)
                pe.wait_ge(a_hh, st.t + 1)
                if st.after(2):
                    pe.wait_ge(a_ev, st.t - 1)
                for c in range(C):
                    last = tr(bank(2 * b, P, c * P), ha[:, b, c * P:(c + 1) * P], ident[:, :])
                last.then_inc(a_tr, 1)
                if st.after(1):
                    attention(st.shift(-1))
            walk(pe, FULL, NU, TAIL, stats_step)
            attention(Step(FULL, FULL // NU, 0, P))

            pe.wait_ge(a_tab, NT)

            def logits_out(lap, gb, n):
                pe.wait_ge(e_fb, n + 1)
                if not (isinstance(n, int) and n == 0):
                    pe.wait_ge(e_dif, n)
                    pe.wait_ge(e_flag_ev, n)
                pe.sem_inc(go, 1)
                tr(ps[0:EG * H, 4 * 512:4 * 512 + P], lk[:, :, :].rearrange("p k h -> p (k h)"), ident[:, :])
                tr(ps[0:EG * H, 4 * 512 + P:4 * 512 + 2 * P], fb[:, :, :].rearrange("p k h -> p (k h)"), ident[:, :])\
                    .then_inc(e_tr, 1)
                if not (isinstance(n, int) and n == 0):
                    pe.wait_ge(e_deg, n)
                for j in range(EG):
                    last = mm(ps[0:ET, 6 * 512:6 * 512 + P], hot_hi[:, gb, j, :], hot_lo[:, gb, j, :],
                              start=(j == 0), stop=(j == EG - 1))
                last.then_inc(e_hist, 1)

            def weights_back(lap, gb, n):
                pe.wait_ge(e_exp, n + 1)
                pe.wait_ge(e_sm, n + 1)
                if not (isinstance(n, int) and n == 0):
                    pe.wait_ge(e_em, n)
                pe.sem_inc(go, 1)
                tr(bank(5, EG * H), eeT[:, :], ident[0:EG * H, 0:EG * H])
                tr(bank(5, EG * H, EG * H), smax[:, :], ident[0:EG * H, 0:EG * H]).then_inc(e_back, 1)

            def tile_sums(lap, gb, n, j):
                t = lap * XR + gb * EG + j
                b = j % 2
                pe.wait_ge(e_em, n + 1)
                pe.wait_ge(e_same, t + 1)
                pe.wait_ge(e_vv, t + 1)
                pe.wait_ge(e_va, t + 1)
                if not (isinstance(t, int) and t < 2):
                    pe.wait_ge(e_z, t - 1)
                    pe.wait_ge(e_za, t - 1)
                mm(bank(2 * b), same[:, j, :], vv[:, j, 0:512], start=True, stop=True)
                mm(bank(2 * b + 1, D - 512), same[:, j, :], vv[:, j, 512:D], start=True, stop=True)
                mm(bank(2 * b + 1, H, D - 512), same[:, j, :], eem[:, gb, 0, j, :], start=True, stop=True)\
                    .then_inc(e_mm, 1)

            def group(lap, gb, n, ahead):
                tile_sums(lap, gb, n, 0)
                if ahead:
                    logits_out(*ahead)
                tile_sums(lap, gb, n, 1)
                tile_sums(lap, gb, n, 2)
                if ahead:
                    weights_back(*ahead)
                tile_sums(lap, gb, n, 3)
            logits_out(0, 0, 0)
            weights_back(0, 0, 0)
            edge_groups(pe, group)

            pe.wait_ge(b_dve, 1)
            mm(ps[0:ET, 7 * 512:7 * 512 + 1], tri[:, :], cum[:, P - 1:P], start=True, stop=True).then_inc(b_pe, 1)
            pe.wait_ge(b_dve, 5)
            tr(bank(7, ET, 256), pos_f[:, :], ident[0:ET, 0:ET]).then_inc(b_pe, 1)
            pe.wait_ge(b_dve, 7)
            HH = H // 2
            for i in range(2):
                last = mm(ps[0:ET, i * 512:i * 512 + HH * ET], ones[0:ET, 0:ET],
                          bd[:, i * HH:(i + 1) * HH, :].rearrange("j h k -> j (h k)"), start=True, stop=True)
            last.then_inc(b_pe, 1)
            pe.wait_ge(b_act, 1)
            for h in range(H):
                at = (2 + h // HH) * 512 + (h % HH) * ET
                last = tr(ps[0:ET, at:at + ET], be[:, h, :], ident[0:ET, 0:ET])
            last.then_inc(b_pe, 1)
            pe.wait_ge(b_dve, 15)
            for h in range(H):
                mm(ps[0:ET, 4 * 512 + h * DH:4 * 512 + (h + 1) * DH], bwT[:, h, :], rr[:, h * DH:(h + 1) * DH],
                   start=True, stop=True)
                last = mm(ps[0:ET, 6 * 512 + h:6 * 512 + h + 1], bwT[:, h, :], ones[0:ET, 0:1], start=True, stop=True)
            last.then_inc(b_pe, 1)

            def x_transposes(st):
                pe.wait_ge(n_hh, st.t + 1)
                for c in range(C):
                    last = tr(bank(0, P, c * P), hn[:, st.ring(3), c * P:(c + 1) * P], ident[:, :])
                last.then_inc(n_t1, 1)

            def slot_logits(st):
                pe.wait_ge(n_ev3, st.t + 1)
                if st.after(2):
                    pe.wait_ge(n_L, st.t - 1)
                for c in range(C):
                    last = mm(bank(LOGITS[st.ring(2)], S), uT[:, c * P:(c + 1) * P], slT[:, c, :], start=(c == 0), stop=(c == C - 1))
                last.then_inc(n_lg, 1)

            def group_transpose(q, tiles, rows, first):
                pe.wait_ge(n_L, q * NG + tiles)
                if not first:
                    pe.wait_ge(g_pg, q)
                pe.sem_inc(go, 1)
                for j in range(tiles):
                    last = tr(ps[0:S, 6 * 512 + j * P:6 * 512 + j * P + rows], lg[0:rows, j, :],
                              ident[0:rows, 0:rows])
                last.then_inc(g_lt, 1)

            def group_back(q, tiles, rows):
                pe.wait_ge(g_exp, q + 1)
                pe.sem_inc(go, 1)
                for j in range(tiles):
                    last = tr(ps[0:rows, 6 * 512 + j * S:6 * 512 + (j + 1) * S], dT[:, j * P:j * P + rows],
                       ident[0:S, 0:S])
                last.then_inc(g_back, 1)

            def group_inputs(q, tiles, rows, s0):
                pe.wait_ge(g_pg, q + 1)
                pe.wait_ge(g_ya, q + 1)
                for j in range(tiles):
                    for half in range(2):
                        last = mm(ps[half * S:(half + 1) * S, 7 * 512:7 * 512 + HD],
                                  pg[0:rows, j, :], uu[0:rows, s0 + j, half * HD:(half + 1) * HD],
                                  start=(j == 0), stop=(j == tiles - 1))
                last.then_inc(g_y, 1)

            def x_products(st):
                pe.wait_ge(n_ev1, st.t + 1)
                if st.after(1):
                    pe.wait_ge(n_sum, st.t)
                for c in range(C):
                    last = mm(bank(3, P, c * P), hnT[:, c * P:(c + 1) * P], wres[:, :], start=True, stop=True)
                last.then_inc(n_mm, 1)

            def u_transposes(st):
                pe.wait_ge(n_u, st.t + 1)
                for c in range(C):
                    last = tr(bank(0, P, c * P), uu[:, st.slot, c * P:(c + 1) * P], ident[:, :])
                last.then_inc(n_t3, 1)

            def node_step(st):
                k = st.slot % NG
                tail = isinstance(st.t, int) and st.t == FULL
                if not tail:
                    if st.after(2):
                        pe.wait_ge(n_ev3, st.t - 1)
                    x_transposes(st.shift(1))
                if st.after(2):
                    slot_logits(st.shift(-2))
                if k == 0 and st.after(6):
                    group_inputs(st.div(3) - 2, NG, P, st.slot)
                if st.after(1):
                    pe.wait_ge(n_ev1, st.t + (1 if tail else 2))
                    u_transposes(st.shift(-1))
                if not tail:
                    x_products(st.shift(1))
                if k == 1 and st.after(4):
                    group_transpose(st.div(3) - 1, NG, P, isinstance(st.t, int) and st.t < 6)
                if k == 2 and st.after(5):
                    group_back(st.div(3) - 1, NG, P)

            pe.wait_ge(b_fix, 16)
            x_transposes(Step(0, 0, 0, P))
            x_products(Step(0, 0, 0, P))
            walk(pe, FULL, NU, TAIL, node_step)
            QL = FULL // NG
            last_step = Step(FULL, FULL // NU, 0, P)
            slot_logits(last_step.shift(-1))
            pe.wait_ge(n_ev3, FULL)
            u_transposes(last_step)
            group_transpose(QL - 1, NG, P, False)
            slot_logits(last_step)
            group_back(QL - 1, NG, P)
            group_inputs(QL - 1, NG, P, NG)
            group_transpose(QL, 1, TAIL, False)
            group_back(QL, 1, TAIL)
            group_inputs(QL, 1, TAIL, 0)

            pe.wait_ge(f_d, 3)
            for c in range(C):
                last = tr(ps[0:S, c * P:(c + 1) * P], ysum[:, c:HD:C], ident[:, :])
            last.then_inc(f_p, 1)
            pe.wait_ge(f_d, 5)

            def first_products(lap, first, last_lap):
                for k in range(WR):
                    pe.wait_ge(f_w1[k], 16 * (lap + 1))
                    pe.wait_ge(f_win, lap * WR + k + 1)
                    for c in range(C):
                        for j in range(G):
                            last = mm(ps[j * GR:(j + 1) * GR, j * 512:j * 512 + F], yw[:, k % 2, j, c, :],
                                      w1_slot(k)[:, j, c * F:(c + 1) * F],
                                      start=(first and k == 0 and c == 0), stop=(last_lap and k == WR - 1 and c == C - 1))
                    last.then_inc(f_h, 1)

            def second_products(lap, first, last_lap):
                for k in range(WR):
                    pe.wait_ge(f_w2[k], 16 * (lap + 1))
                    pe.wait_ge(f_win, QUADS + lap * WR + k + 1)
                    for at, width in ((0, 512), (512, D - 512)):
                        for j in range(G):
                            last = mm(ps[j * GR:(j + 1) * GR, 2 * j * 512 + at:2 * j * 512 + at + width],
                                      hw[:, k % 2, j, :], w2_slot(k)[:, j, at:at + width],
                                      start=(first and k == 0), stop=(last_lap and k == WR - 1))
                    last.then_inc(f_y, 1)

            LAPS_F = QUADS // WR
            first_products(0, True, False)
            with pe.Fori(1, LAPS_F - 1) as lap:
                first_products(lap, False, False)
            first_products(LAPS_F - 1, False, True)
            pe.wait_ge(f_a, 1)
            tr(ps[0:F, 4 * 512:4 * 512 + P], hact[:, :], ident[:, :]).then_inc(f_p, 1)
            second_products(0, True, False)
            with pe.Fori(1, LAPS_F - 1) as lap:
                second_products(lap, False, False)
            second_products(LAPS_F - 1, False, True)

            def mix(st):
                b = st.ring(2)
                if not st.after(1):
                    pe.wait_ge(f_d, F_OUT + 5)
                pe.wait_ge(o_ev, st.t + 1)
                if st.after(2):
                    pe.wait_ge(o_o, st.t - 1)
                parts = ((0, y_a), (0, y_b), (P, y_c))
                for at, width in ((0, 512), (512, D - 512)):
                    for i, (e, y) in enumerate(parts):
                        last = mm(bank(2 * b, width, at), exT[:, b, e:e + P], y[:, at:at + width],
                                  start=(i == 0), stop=(i == len(parts) - 1))
                last.then_inc(o_mm, 1)

            def out_step(st):
                b = st.ring(2)
                if st.after(2):
                    pe.wait_ge(o_ev, st.t - 1)
                mm(bank(4 + b, P), e12[:, bass.ds(st.t, 1), :].rearrange("p t e -> p (t e)"), ident_b[:, :],
                   start=True, stop=True)
                mm(bank(4 + b, P, P), e13[:, bass.ds(st.t, 1), :].rearrange("p t e -> p (t e)"), ident_b[:, :],
                   start=True, stop=True).then_inc(o_t, 1)
                if st.after(1):
                    mix(st.shift(-1))
            pe.wait_ge(o_cw, CW)
            pe.wait_ge(f_d, F_OUT)
            walk(pe, FULL, NU, TAIL, out_step)
            mix(Step(FULL, FULL // NU, 0, P))

        @block.scalar
        def _(act):
            def copy(o, i):
                return nc.scalar.activation(o, i, ACT.Copy)

            act.wait_ge(s_in, IN_DMAS)
            nc.scalar.activation(slots_sq[:, :], slots_sb[:, :], ACT.Square, accum_out=s_norm[:, 0:1]).then_inc(s_sq, 1)

            def table_out(t0, k, rows):
                act.dma_start(node_table[bass.ds(t0 * P, (k - 1) * P + rows), :]
                              .rearrange("(k p) c -> p k c", k=k),
                              table[0:rows, bass.ds(t0, k), :]).then_inc(a_out, 16)

            def rows_of(st):
                b, f = st.ring(2), st.slot
                out2 = ps[:, (4 + 2 * b) * 512:(6 + 2 * b) * 512].rearrange("p (k n) -> p k n", n=512)[:, :, 0:3 * FC]
                if st.after(NU):
                    act.wait_ge(a_st[f], 16 * st.lap)
                copy(frow[:, f, :].rearrange("p (k n) -> p k n", k=2), out2).then_inc(a_row, 1)
                copy(table[:, bass.ds(st.t, 1), 0:H].rearrange("p t (k c i) -> p (t k) c i", k=2, i=2),
                     out2.rearrange("p k (c f) -> p k c f", f=FC)[:, :, :, A2C:FC]).then_inc(a_tab, 1)

            def stats_step(st):
                b = st.ring(2)
                act.wait_ge(a_tr, st.t + 1)
                if st.after(2):
                    act.wait_ge(a_att, st.t - 1)
                copy(haT[:, b, :], bank(2 * b, D)).then_inc(a_ev, 1)
                if st.after(2):
                    rows_of(st.shift(-2))
                if st.slot == 1 and st.after(NU):
                    act.wait_ge(a_tab, st.t - 1)
                    act.wait_ge(a_mr, st.t - 1)
                    table_out(st.t - 1 - NU, NU, P)
            act.wait_ge(s_pool, POOL_SET)
            walk(act, FULL, NU, TAIL, stats_step)
            for t in (FULL - 1, FULL):
                act.wait_ge(a_att, t + 1)
                rows_of(Step(t, t // NU, t % NU, P))
            act.wait_ge(a_tab, NT)
            act.wait_ge(a_mr, NT)
            table_out(FULL - NU, NU, P)
            table_out(FULL, 1, TAIL)

            def flags_of(n):
                act.wait_ge(e_tr, n + 1)
                if not (isinstance(n, int) and n == 0):
                    act.wait_ge(e_sm, n)
                copy(flagT[:, 0:P], ps[0:EG * H, 4 * 512 + P:4 * 512 + 2 * P]).then_inc(e_flag_ev, 1)

            def exponentials(n):
                act.wait_ge(e_dif, n + 1)
                if not (isinstance(n, int) and n == 0):
                    act.wait_ge(e_back, n)
                nc.scalar.activation(eeT[:, :], dif[:, :], ACT.Exp).then_inc(e_exp, 1)

            def group(lap, gb, n, ahead):
                t0 = lap * XR + gb * EG

                def rows(j):
                    if not (isinstance(n, int) and n == 0):
                        act.wait_ge(e_mm, t0 + j - 3)
                    for h in range(HV, H):
                        at = h // 2 * FC + h % 2 * DH
                        last = nc.scalar.activation(vv[:, j, h * DH:(h + 1) * DH], xg[:, gb * EG + j, at:at + DH],
                                                    ACT.Copy, scale=eem[:, gb, 0, j, h:h + 1])
                    last.then_inc(e_va, 1)

                def sums(j):
                    b = j % 2
                    if not (isinstance(n, int) and n == 0):
                        act.wait_ge(e_out[j], 16 * n)
                    copy(zo[:, j, D + H:ROW], eem[:, gb, 1, j, :])
                    act.wait_ge(e_lcp, t0 + j + 1)
                    for h in range(HV, H):
                        last = nc.scalar.activation(zo[:, j, h * DH:(h + 1) * DH],
                                                    bank(2 * b + 1, DH, (h - HV) * DH), ACT.Copy, scale=rl[:, b, h:h + 1])
                    last.then_inc(e_za, 1)
                act.wait_ge(e_em, n + 1)
                rows(0)
                rows(1)
                if ahead:
                    flags_of(ahead[2])
                rows(2)
                sums(0)
                if ahead:
                    exponentials(ahead[2])
                rows(3)
                sums(1)
                sums(2)
                sums(3)
            flags_of(0)
            exponentials(0)
            edge_groups(act, group)

            act.wait_ge(b_dve, 12)
            nc.scalar.activation(be[:, :, :], bm[:, :, :], ACT.Exp).then_inc(b_act, 1)
            act.wait_ge(b_dve, 13)
            nc.scalar.activation(bcf[:, :], bdf[:, :], ACT.Exp).then_inc(b_act, 1)

            def hh(st):
                r = st.ring(3)
                act.wait_ge(n_x[st.slot], 16 * st.lap + 16)
                act.wait_ge(n_mr, st.t + 1)
                if st.after(3):
                    act.wait_ge(n_t1, st.t - 2)
                nc.scalar.activation(hn[:, r, :], xn[:, st.slot, :], ACT.Identity, bias=mr[:, r, 0:1], scale=mr[:, r, 1:2])\
                    .then_inc(n_hh, 1)

            def ev1(st):
                act.wait_ge(n_t1, st.t + 1)
                if st.after(1):
                    act.wait_ge(n_mm, st.t)
                copy(hnT[:, :], bank(0, D)).then_inc(n_ev1, 1)

            def keep(st):
                act.wait_ge(n_L, st.t + 1)
                copy(logits[:, bass.ds(st.t, 1), :], lg[:, st.ring(3), :]).then_inc(n_keep, 1)

            def group_exp(q, par, cols, first):
                act.wait_ge(g_neg, q + 1)
                if not first:
                    act.wait_ge(g_back, q)
                    act.wait_ge(g_l, q)
                    act.wait_ge(g_ya, q + 1)
                nc.scalar.activation(dT[:, 0:cols], ps[0:S, 6 * 512:6 * 512 + cols], ACT.Exp, bias=nneg[:, :],
                                     accum_out=dsum[:, :])
                nc.scalar.activation(cc[0:S, :], mrun[:, 1 - par, :], ACT.Exp, bias=nneg[:, :]).then_inc(g_exp, 1)

            def square(st):
                act.wait_ge(n_u, st.t + 1)
                if st.after(1):
                    act.wait_ge(n_sq, st.t)
                if st.after(3):
                    act.wait_ge(n_tok, st.t - 2)
                nc.scalar.activation(usq[:, :], uu[:, st.slot, :], ACT.Square, accum_out=usum[:, st.ring(3), :])\
                    .then_inc(n_sq, 1)

            def ev3(st):
                act.wait_ge(n_t3, st.t + 1)
                if st.after(1):
                    act.wait_ge(n_lg, st.t)
                copy(uT[:, :], bank(0, D)).then_inc(n_ev3, 1)

            def node_step(st):
                if not (isinstance(st.t, int) and st.t == FULL):
                    hh(st.shift(2))
                    ev1(st.shift(1))
                if st.slot % NG == 2 and st.after(5):
                    group_exp(st.div(3) - 1, (st.slot // NG + 1) % 2, NG * P, isinstance(st.t, int) and st.t < 6)
                if st.after(1):
                    square(st.shift(-1))
                    ev3(st.shift(-1))
                if st.after(2):
                    keep(st.shift(-2))
            act.wait_ge(b_fix, 16)
            hh(Step(0, 0, 0, P))
            hh(Step(1, 0, 1, P))
            ev1(Step(0, 0, 0, P))
            walk(act, FULL, NU, TAIL, node_step)
            last_step = Step(FULL, FULL // NU, 0, P)
            square(last_step)
            ev3(last_step)
            keep(last_step.shift(-1))
            keep(last_step)
            QL = FULL // NG
            group_exp(QL - 1, (QL - 1) % 2, NG * P, False)
            group_exp(QL, QL % 2, TAIL, False)

            act.wait_ge(o_cw, 2)
            nc.scalar.activation(logits[:, :, :], logits[:, :, :], ACT.Exp).then_inc(o_cexp, 1)
            act.wait_ge(f_d, 5 + G)
            nc.scalar.activation(hact[:, :], hpre[:, :], ACT.Gelu).then_inc(f_a, 1)
            act.wait_ge(o_cw, 5)
            copy(e12[:, :, 0:S], logits[:, :, :]).then_inc(o_cexp, 1)
            act.wait_ge(o_cw, 7)
            copy(e12[:, :, S:2 * S], logits[:, :, :]).then_inc(o_cexp, 1)

            def weights_T(st):
                b = st.ring(2)
                act.wait_ge(o_t, st.t + 1)
                if st.after(2):
                    act.wait_ge(o_mm, st.t - 1)
                copy(exT[:, b, :], bank(4 + b, 2 * P)).then_inc(o_ev, 1)
            walk(act, FULL, NU, TAIL, weights_T)

        @block.vector
        def _(dve):
            v = nc.vector
            link = chain_of(dve, s_dve)
            dve.wait_ge(s_edge_in, 64)
            v.memset(e_flag[:, 0:1], 0.0).then_inc(s_copies, 1)
            v.memset(yw[:, :, :, :, :], 0.0).then_inc(f_zero, 1)
            v.memset(hw[:, :, :, :], 0.0).then_inc(f_zero, 1)
            v.memset(zeros[:, :, :], 0.0).then_inc(f_zero, 1)
            v.memset(wfc[:, :, :], 0.0).then_inc(s_copies, 1)
            link(v.tensor_copy(e_srcf[:, :], e_src[:, :]))
            link(v.tensor_copy(e_dstf[:, :], e_dst[:, :]))
            link(v.tensor_tensor(e_eq[:, 1:P], e_dstf[:, 1:P], e_dstf[:, 0:P - 1], ALU.not_equal))
            dve.wait_ge(s_copies, 2)
            link(v.tensor_scalar(e_flag[:, 1:P], e_eq[:, 1:P], -BIG, None, ALU.mult))
            dve.wait_ge(s_ident, 2)
            dve.wait_ge(s_pe, 2)
            v.tensor_copy(src_i[:, :], bank(7, ET)).then_inc(s_copies, 1)
            v.tensor_copy(flag_t[:, :], bank(7, ET, 2 * ET)).then_inc(s_copies, 1)
            v.tensor_scalar(dst_i[:, :], bank(7, ET, ET), float(N - 1), None, ALU.min).then_inc(s_copies, 1)
            v.tensor_copy(dst_ti[:, :], bank(7, ET, ET)).then_inc(s_copies, 1)
            link(v.tensor_copy(sel_last[:, :], ident[:, P - 1:P].broadcast_to([P, ET])))
            link(v.tensor_copy(dst_f[:, :], bank(7, ET, ET)))
            dve.wait_ge(s_copies, 6)
            link(v.tensor_scalar(hi_i[:, :], dst_ti[:, :], P.bit_length() - 1, None, ALU.arith_shift_right))
            link(v.tensor_scalar(lo_i[:, :], dst_ti[:, :], P - 1, None, ALU.bitwise_and))
            v.tensor_copy(hi_f[:, :], hi_i[:, :]).then_inc(s_copies, 1)
            v.tensor_copy(lo_f[:, :], lo_i[:, :]).then_inc(s_copies, 1)
            dve.wait_ge(s_pool, POOL_SET)
            v.tensor_copy(iota_f[:, :], iota_i[:, :]).then_inc(s_copies, 1)
            v.tensor_copy(e_basef[:, :], e_base[:, :]).then_inc(s_copies, 1)
            link(v.tensor_scalar(e_eq[:, :], e_dstf[:, :], e_dstf[:, 0:1], None, ALU.is_equal))
            link(v.tensor_reduce(e_cnt[:, :], e_eq[:, :], AX.X, ALU.add))
            dve.wait_ge(s_copies, 10)
            link(v.tensor_tensor(first_end[:, :], e_cnt[:, :], e_basef[:, :], ALU.add))
            dve.wait_ge(s_pe, 3)
            link(v.tensor_scalar(chain[:, :], ps[0:ET, 7 * 512 + 256:7 * 512 + 256 + ET], e_dstf[:, 0:1], None,
                                 ALU.is_equal))
            link(v.tensor_tensor(e_eq[:, 0:ET], tri[:, :], ident[0:ET, 0:ET], ALU.add))
            link(v.tensor_scalar(e_eq[:, 0:ET], e_eq[:, 0:ET], -1.0, 1.0, ALU.mult, ALU.add))
            link(v.tensor_tensor(chain[:, :], chain[:, :], e_eq[:, 0:ET], ALU.mult))
            link(v.tensor_scalar(chain[:, :], chain[:, :], -1.0, BIG, ALU.add, ALU.mult))
            for half in range(2):
                for part in range(2):
                    at = half + part * H
                    link(v.tensor_copy(
                        wfc[half * DH:(half + 1) * DH, :, A1C + 2 * part + half:A1C + 2 * part + half + 1],
                        ps[half * DH:(half + 1) * DH, 6 * 512 + at:6 * 512 + part * H + H:2].unsqueeze(2)))
            dve.wait_ge(s_in, IN_DMAS)
            for half in range(2):
                rows = slice(half * DH, (half + 1) * DH)
                link(v.tensor_copy(wfc[rows, :, rows], wfcT[rows, :].unsqueeze(1).broadcast_to([DH, C, DH])))
            v.tensor_copy(ident_b[:, :], ident[:, :])
            dve.wait_ge(s_pool, POOL_SET + 2)
            v.tensor_scalar(slots_sq[:, :], slots_sb[:, :], s_norm[:, 2:3], scale_sb[:, :], ALU.mult, ALU.mult)\
                .then_inc(s_copies, 1)
            dve.wait_ge(s_pe, 4)
            link(v.tensor_copy(slT[:, :, :].rearrange("p c s -> p (c s)"), bank(7, C * S)))

            def normalise(st):
                b = st.ring(2)
                dve.wait_ge(a_rstd, st.t + 1)
                if st.after(2):
                    dve.wait_ge(a_tr, st.t - 1)
                v.tensor_scalar(ha[:, b, :], xa[:, st.slot, :], mva[:, b, 0:1], mva[:, b, 3:4], ALU.subtract, ALU.mult)\
                    .then_inc(a_hh, 1)
                v.scalar_tensor_tensor(table[:, bass.ds(st.t, 1), SHIFT:SHIFT + 1], mva[:, b, 0:1].unsqueeze(1), -1.0,
                                       mva[:, b, 3:4].unsqueeze(1), ALU.mult, ALU.mult)
                v.tensor_copy(table[:, bass.ds(st.t, 1), RSTD:RSTD + 1], mva[:, b, 3:4].unsqueeze(1)).then_inc(a_mr, 1)

            def stats_step(st):
                b = st.ring(2)
                dve.wait_ge(xa_in[st.slot], 16 * (st.lap + 1))
                v.bn_stats(bna[:, b, 0:6], xa[:, st.slot, 0:512])
                v.bn_stats(bna[:, b, 6:12], xa[:, st.slot, 512:D]).then_inc(a_bn, 1)
                dve.wait_ge(a_bn, st.t + 1)
                if st.after(2):
                    dve.wait_ge(a_mr, st.t - 1)
                if st.after(1):
                    normalise(st.shift(-1))
                v.bn_aggr(mva[:, b, 0:2], bna[:, b, :]).then_inc(a_mv, 1)
            walk(dve, FULL, NU, TAIL, stats_step)
            normalise(Step(FULL, FULL // NU, 0, P))

            dve.wait_ge(a_tab, NT)
            for i in range(NU):
                dve.wait_ge(a_st[i], 16 * ring_uses(NT, NU, i))
            v.memset(flagT[:, P:P + 1], 0.0).then_inc(e_init, 1)
            v.memset(deg[:, :], 0.0).then_inc(e_init, 1)
            dve.wait_ge(e_init, 2)

            def logits_of_group(lap, gb, n):
                t0 = lap * XR + gb * EG
                dve.wait_ge(e_tab[gb], 16 * EG * (lap + 1))
                for j in range(EG):
                    dve.wait_ge(e_x[gb * EG + j], 16 * (lap + 1))
                v.tensor_tensor(sc[:, :, :].rearrange("p k (c i) -> p k c i", i=2),
                                xg[:, gb * EG:(gb + 1) * EG, :]
                                .rearrange("p k (c f) -> p k c f", f=FC)[:, :, :, A1C:A1C + 2],
                                tg_d[:, gb, :, 0:H].rearrange("p k (c i) -> p k c i", i=2), ALU.add).then_inc(e_sc, 1)
                if not starts(n):
                    dve.wait_ge(e_hist, n - 1)
                v.tensor_tensor(hot_lo[:, gb, :, :], lo_f[:, bass.ds(t0, EG)].unsqueeze(2).broadcast_to([P, EG, P]),
                                iota_f[:, :].unsqueeze(1).broadcast_to([P, EG, P]), ALU.is_equal)
                v.tensor_tensor(hot_hi[:, gb, :, :], hi_f[:, bass.ds(t0, EG)].unsqueeze(2).broadcast_to([P, EG, ET]),
                                iota_f[:, 0:ET].unsqueeze(1).broadcast_to([P, EG, ET]), ALU.is_equal)
                dve.wait_ge(e_sc, n + 1)
                v.scalar_tensor_tensor(lk[:, :, :], sc[:, :, :], SLOPE, sc[:, :, :], ALU.mult, ALU.max)
                v.tensor_copy(dsc[:, gb, :], dst_f[:, bass.ds(t0, EG)])
                v.tensor_copy(fb[:, :, :], flag_t[:, bass.ds(t0, EG)].unsqueeze(2).broadcast_to([P, EG, H]))\
                    .then_inc(e_fb, 1)

            def maxima_of_group(lap, gb, n):
                dve.wait_ge(e_tr, n + 1)
                dve.wait_ge(e_flag_ev, n + 1)
                v.tensor_tensor_scan(pmax[:, :], flagT[:, 0:P], ps[0:EG * H, 4 * 512:4 * 512 + P], -BIG,
                                     ALU.add, ALU.max).then_inc(e_pm, 1)
                dve.wait_ge(e_pm, n + 1)
                v.tensor_tensor_scan(smax[:, ::-1], flagT[:, P:0:-1], pmax[:, ::-1], -BIG,
                                     ALU.add, ALU.max).then_inc(e_sm, 1)
                dve.wait_ge(e_hist, n + 1)
                v.tensor_tensor(deg[:, :], deg[:, :], ps[0:ET, 6 * 512:6 * 512 + P], ALU.add).then_inc(e_deg, 1)
                dve.wait_ge(e_sm, n + 1)
                v.tensor_tensor(dif[:, :], ps[0:EG * H, 4 * 512:4 * 512 + P], smax[:, :], ALU.subtract).then_inc(e_dif, 1)

            def weights_of_group(lap, gb, n):
                if not starts(n):
                    dve.wait_ge(e_za, (n - 1) * EG)
                dve.wait_ge(e_back, n + 1)
                v.tensor_copy(eem[:, gb, :, :, :].rearrange("p a k h -> p (a k h)"), bank(5, 2 * EG * H)).then_inc(e_em, 1)

            def group(lap, gb, n, ahead):
                t0 = lap * XR + gb * EG

                def rows(j):
                    if not (isinstance(n, int) and n == 0):
                        dve.wait_ge(e_mm, t0 + j - 3)
                    v.tensor_scalar(same[:, j, :], dst_row[:, gb, j * P:(j + 1) * P], dsc[:, gb, j:j + 1], None,
                                    ALU.is_equal).then_inc(e_same, 1)
                    v.tensor_tensor(
                        vv[:, j, 0:HV * DH].rearrange("p (c i d) -> p c i d", i=2, d=DH),
                        xg[:, gb * EG + j, :].rearrange("p (c f) -> p c f", f=FC)[:, 0:HV // 2, 0:2 * DH]
                        .rearrange("p c (i d) -> p c i d", i=2),
                        eem[:, gb, 0, j, 0:HV].rearrange("p (c i) -> p c i", i=2).unsqueeze(3)
                        .broadcast_to([P, HV // 2, 2, DH]), ALU.mult).then_inc(e_vv, 1)

                def sums(j):
                    t, b = t0 + j, j % 2
                    dve.wait_ge(e_mm, t + 1)
                    v.reciprocal(rl[:, b, :], bank(2 * b + 1, H, D - 512))
                    if not (isinstance(n, int) and n == 0):
                        dve.wait_ge(e_out[j], 16 * n)
                    v.tensor_copy(zo[:, j, D:D + H], bank(2 * b + 1, H, D - 512)).then_inc(e_lcp, 1)
                    dve.wait_ge(e_lcp, t + 1)
                    v.tensor_tensor(zo[:, j, 0:HV * DH].rearrange("p (h d) -> p h d", h=HV),
                                    bank(2 * b).rearrange("p (h d) -> p h d", d=DH),
                                    rl[:, b, 0:HV].unsqueeze(2).broadcast_to([P, HV, DH]), ALU.mult).then_inc(e_z, 1)
                dve.wait_ge(e_row[gb], 16 * (lap + 1))
                dve.wait_ge(e_fb, n + 1)
                dve.wait_ge(e_em, n + 1)
                rows(0)
                rows(1)
                if ahead:
                    logits_of_group(*ahead)
                rows(2)
                sums(0)
                if ahead:
                    maxima_of_group(*ahead)
                rows(3)
                sums(1)
                sums(2)
                if ahead:
                    weights_of_group(*ahead)
                sums(3)
            logits_of_group(0, 0, 0)
            maxima_of_group(0, 0, 0)
            weights_of_group(0, 0, 0)
            edge_groups(dve, group)

            link = chain_of(dve, b_dve)
            dve.wait_ge(e_deg, GROUPS)
            link(v.tensor_tensor_scan(cum[:, :], ones[0:ET, :], deg[:, :], 0.0, ALU.mult, ALU.add))
            dve.wait_ge(b_pe, 1)
            link(v.tensor_copy(off_sb[:, :], ps[0:ET, 7 * 512:7 * 512 + 1]))
            link(v.tensor_scalar(none[:, :], deg[:, :], 0.0, float(1 << 20), ALU.is_equal, ALU.mult))
            link(v.scalar_tensor_tensor(pos_f[:, :], cum[:, :], off_sb[:, :], none[:, :], ALU.add, ALU.add))
            link(v.tensor_scalar(pos_f[:, :], pos_f[:, :], -1.0, None, ALU.add))
            dve.wait_ge(b_pe, 2)
            link(v.tensor_copy(pos_i[:, :], bank(7, ET, 256)))
            dve.wait_ge(b_in, 16)
            LC, MC = D, D + H
            link(v.tensor_tensor(bd[:, :, :], rr[:, MC:MC + H].unsqueeze(2).broadcast_to([ET, H, ET]),
                                 ident[0:ET, 0:ET].unsqueeze(1).broadcast_to([ET, H, ET]), ALU.mult))
            dve.wait_ge(b_pe, 3)
            HH = H // 2
            for i in range(2):
                link(v.tensor_tensor(bm[:, i * HH:(i + 1) * HH, :],
                                     ps[0:ET, i * 512:i * 512 + HH * ET].rearrange("k (h j) -> k h j", j=ET),
                                     chain[:, :].unsqueeze(1).broadcast_to([ET, HH, ET]), ALU.add))
            link(v.tensor_reduce(bmax[:, :], bm[:, :, :], AX.X, ALU.max))
            dve.wait_ge(b_ff, 16)
            link(v.tensor_tensor(bmax[:, :], bmax[:, :], ff[:, MC:MC + H], ALU.max))
            link(v.tensor_tensor(bm[:, :, :], bm[:, :, :], bmax[:, :].unsqueeze(2).broadcast_to([ET, H, ET]),
                                 ALU.subtract))
            link(v.tensor_tensor(bdf[:, :], ff[:, MC:MC + H], bmax[:, :], ALU.subtract))
            dve.wait_ge(b_pe, 4)
            for i in range(2):
                link(v.tensor_tensor(bwT[:, i * HH:(i + 1) * HH, :],
                                     ps[0:ET, (2 + i) * 512:(2 + i) * 512 + HH * ET]
                                     .rearrange("j (h k) -> j h k", k=ET),
                                     rr[:, LC + i * HH:LC + (i + 1) * HH].unsqueeze(2).broadcast_to([ET, HH, ET]),
                                     ALU.mult))
            dve.wait_ge(b_act, 2)
            link(v.tensor_tensor(bcf[:, :], bcf[:, :], ff[:, LC:LC + H], ALU.mult))
            dve.wait_ge(b_pe, 5)
            link(v.tensor_tensor(btot[:, :], bcf[:, :], ps[0:ET, 6 * 512:6 * 512 + H], ALU.add))
            link(v.reciprocal(btot[:, :], btot[:, :]))
            link(v.tensor_tensor(bcf[:, :], bcf[:, :], btot[:, :], ALU.mult))
            fz = ff[:, 0:D].rearrange("k (h d) -> k h d", h=H)
            bzv = bz[:, :].rearrange("k (h d) -> k h d", d=DH)
            link(v.tensor_tensor(fz, fz, bcf[:, :].unsqueeze(2).broadcast_to([ET, H, DH]), ALU.mult))
            link(v.tensor_tensor(bzv, ps[0:ET, 4 * 512:4 * 512 + D].rearrange("k (h d) -> k h d", d=DH),
                                 btot[:, :].unsqueeze(2).broadcast_to([ET, H, DH]), ALU.mult))
            link(v.tensor_tensor(fz, fz, bzv, ALU.add))

            dve.wait_ge(b_fix, 16)
            v.memset(ysum[:, :], 0.0).then_inc(g_ya, 1)
            v.memset(mrun[:, 1, :], -BIG).then_inc(g_init, 1)
            v.memset(lrun[:, :], 0.0).then_inc(g_init, 1)
            dve.wait_ge(g_init, 2)
            dve.wait_ge(g_ya, 1)

            def logits_of(st):
                r = st.ring(3)
                dve.wait_ge(n_lg, st.t + 1)
                dve.wait_ge(n_tok, st.t + 1)
                if st.after(3):
                    dve.wait_ge(g_lt, st.div(3))
                    dve.wait_ge(n_keep, st.t - 2)
                v.tensor_scalar(lg[:, r, :], bank(LOGITS[st.ring(2)], S), tok[:, r, :], None, ALU.mult).then_inc(n_L, 1)

            def group_max(q, par, cols):
                dve.wait_ge(g_lt, q + 1)
                v.tensor_reduce(gmax[:, :], ps[0:S, 6 * 512:6 * 512 + cols], AX.X, ALU.max).then_inc(g_max, 1)
                dve.wait_ge(g_max, q + 1)
                v.tensor_tensor(mrun[:, par, :], mrun[:, 1 - par, :], gmax[:, :], ALU.max).then_inc(g_new, 1)
                dve.wait_ge(g_new, q + 1)
                v.tensor_scalar(nneg[:, :], mrun[:, par, :], -1.0, None, ALU.mult).then_inc(g_neg, 1)

            def group_scale(q, first):
                dve.wait_ge(g_exp, q + 1)
                if not first:
                    dve.wait_ge(g_l, q)
                v.scalar_tensor_tensor(lrun[:, :], lrun[:, :], cc[0:S, :], dsum[:, :], ALU.mult, ALU.add)
                v.tensor_copy(cc[S:2 * S, :], cc[0:S, :]).then_inc(g_l, 1)

            def group_weights(q, tiles, rows, s0):
                dve.wait_ge(g_back, q + 1)
                dve.wait_ge(n_gam, q * NG + tiles)
                v.tensor_tensor(pg[0:rows, 0:tiles, :],
                                ps[0:rows, 6 * 512:6 * 512 + tiles * S].rearrange("p (k s) -> p k s", s=S),
                                gam[0:rows, s0:s0 + tiles, :].broadcast_to([rows, tiles, S]), ALU.mult).then_inc(g_pg, 1)

            def group_sum(q):
                dve.wait_ge(g_y, q + 1)
                dve.wait_ge(g_l, q + 1)
                v.scalar_tensor_tensor(ysum[:, :], ysum[:, :], cc[:, :], bank(7, HD), ALU.mult, ALU.add).then_inc(g_ya, 1)

            def node_step(st):
                r, k = st.ring(3), st.slot % NG
                dve.wait_ge(n_mm, st.t + 1)
                if st.after(3):
                    dve.wait_ge(n_st[r], 16 * st.div(3))
                dve.wait_ge(n_ag[r], 16 * st.div(3) + 16)
                v.tensor_tensor(gat[:, :], bank(3, D), agg[:, r, 0:D], ALU.add).then_inc(n_sum, 1)
                dve.wait_ge(n_sum, st.t + 1)
                v.scalar_tensor_tensor(x1[:, r, :], gat[:, :], 0.0, xn[:, st.slot, :], ALU.max, ALU.add).then_inc(n_x1, 1)
                dve.wait_ge(n_x1, st.t + 1)
                v.bn_stats(bnn[:, 0:6], x1[:, r, 0:512])
                v.bn_stats(bnn[:, 6:12], x1[:, r, 512:D]).then_inc(n_bn, 1)
                if k == 2 and st.after(5):
                    group_scale(st.div(3) - 1, isinstance(st.t, int) and st.t < 6)
                dve.wait_ge(n_bn, st.t + 1)
                dve.sem_inc(go, 1)
                v.bn_aggr(mvn[:, r, :], bnn[:, :]).then_inc(n_mv, 1)
                if st.after(2):
                    logits_of(st.shift(-2))
                if st.after(6):
                    dve.wait_ge(g_y, st.div(3) - 1)
                dve.wait_ge(n_mv, st.t + 1)
                v.scalar_tensor_tensor(uu[:, st.slot, :], x1[:, r, :], mvn[:, r, 0:1], wn[:, :],
                                       ALU.subtract, ALU.mult).then_inc(n_u, 1)
                if k == 0 and st.after(6):
                    group_sum(st.div(3) - 2)
                if k == 2 and st.after(5):
                    group_weights(st.div(3) - 1, NG, P, (st.slot + 1) % NU)
                if k == 1 and st.after(4):
                    group_max(st.div(3) - 1, (st.slot // NG + 1) % 2, NG * P)

            walk(dve, FULL, NU, TAIL, node_step)
            last_step = Step(FULL, FULL // NU, 0, P)
            logits_of(last_step.shift(-1))
            logits_of(last_step)
            QL = FULL // NG
            group_max(QL - 1, (QL - 1) % 2, NG * P)
            group_scale(QL - 1, False)
            group_weights(QL - 1, NG, P, NG)
            group_sum(QL - 1)
            group_max(QL, QL % 2, TAIL)
            group_scale(QL, False)
            group_weights(QL, 1, TAIL, 0)
            group_sum(QL)

            link = chain_of(dve, f_d)
            dve.wait_ge(g_l, QL + 1)
            dve.wait_ge(g_ya, QL + 2)
            link(v.reciprocal(rlr[0:S, :], lrun[:, :]))
            link(v.tensor_copy(rlr[S:2 * S, :], rlr[0:S, :]))
            link(v.tensor_scalar(ysum[:, :], ysum[:, :], rlr[:, :], None, ALU.mult))
            dve.wait_ge(f_p, 1)
            for half in range(2):
                link(v.tensor_copy(yT[half * S:(half + 1) * S, :, :],
                                   ps[0:S, 0:C * P].rearrange("p (c q) -> p c q", q=P)[:, :, half * S:(half + 1) * S]))
            cw = chain_of(dve, o_cw)
            dve.wait_ge(n_keep, NT)
            nodes_left(dve)
            v.memset(b1_sb[:, :], 0.0).then_inc(f_zero, 1)
            v.memset(b2_sb[:, :], 0.0).then_inc(f_zero, 1)
            cw(v.tensor_reduce(tmax[:, :], logits[:, :, :], AX.X, ALU.max))
            cw(v.tensor_tensor(logits[:, :, :], logits[:, :, :], tmax[:, :].unsqueeze(2).broadcast_to([P, NT, S]),
                               ALU.subtract))
            dve.wait_ge(o_cexp, 1)
            cw(v.tensor_reduce(tsum[:, :], logits[:, :, :], AX.X, ALU.add))
            cw(v.reciprocal(tsum[:, :], tsum[:, :]))
            cw(v.tensor_tensor(logits[:, :, :], logits[:, :, :], tsum[:, :].unsqueeze(2).broadcast_to([P, NT, S]),
                               ALU.mult))

            dve.wait_ge(f_in, 16 * 2 * G)
            dve.wait_ge(f_h, QUADS)
            for j in range(G):
                rows = slice(j * GR, (j + 1) * GR)
                link(v.tensor_tensor(hpre[rows, :], ps[rows, j * 512:j * 512 + F], b1_sb[rows, :], ALU.add))
            dve.wait_ge(f_p, 2)
            link(v.tensor_copy(hT[:, :], ps[0:F, 4 * 512:4 * 512 + P]))

            dve.wait_ge(o_cexp, 2)
            cw(v.tensor_copy(e13[:, :, 0:S], e12[:, :, 0:S]))
            cw(v.tensor_tensor(logits[:, :, :], logits[:, :, :], e12[:, :, 0:S], ALU.subtract))
            dve.wait_ge(o_cexp, 3)
            cw(v.tensor_tensor(e13[:, :, S:2 * S], logits[:, :, :], e12[:, :, S:2 * S], ALU.subtract))
            dve.wait_ge(f_y, QUADS)
            for j in range(G):
                rows = slice(j * GR, (j + 1) * GR)
                link(v.tensor_tensor(y2[rows, :], ps[rows, 2 * j * 512:2 * j * 512 + D], b2_sb[rows, :], ALU.add))
            dve.wait_ge(f_in, 16 * 4 * G)
            link(v.tensor_copy(y_a[:, :], yf[:, :]))
            link(v.tensor_tensor(yf[:, :], yf[:, :], y_a[:, :], ALU.subtract))
            link(v.tensor_copy(y_b[:, :], yf[:, :]))
            link(v.tensor_tensor(y_c[0:S, :], yf[0:S, :], y_b[0:S, :], ALU.subtract))
            link(v.tensor_copy(y_c[S:2 * S, :], y_a[S:2 * S, :]))

            def out_step(st):
                b = st.ring(2)
                dve.wait_ge(o_x[st.slot], 16 * (st.lap + 1))
                dve.wait_ge(o_mm, st.t + 1)
                v.tensor_tensor(xo[:, st.slot, :], bank(2 * b, D), xo[:, st.slot, :], ALU.add).then_inc(o_o, 1)
            walk(dve, FULL, NU, TAIL, out_step)


def kernel(**inputs):
    import numpy as _np
    import concourse.bacc as _bacc
    from concourse import mybir as _mybir
    from concourse.bass_utils import run_bass_kernel_spmd as _run

    a = {k: _np.asarray(v) for k, v in inputs.items()}
    arrays = {
        "x": a["x"], "src": a["src"], "dst": a["dst"],
        "w_cat": _np.concatenate([a["L0_gnn_W_res"].T, a["L0_gnn_W_fc"].T], axis=0),
        "w_fc": a["L0_gnn_W_fc"],
        "attn": _np.concatenate([a["L0_gnn_attn_l"].T, a["L0_gnn_attn_r"].T], axis=1),
        "slots": a["L0_ffn_slots"], "scale": a["L0_ffn_scale"],
        "w1": a["L0_ffn_fc1_weight"], "b1": a["L0_ffn_fc1_bias"],
        "w2": a["L0_ffn_fc2_weight"], "b2": a["L0_ffn_fc2_bias"], "norm_w": a["L0_ffn_norm_weight"],
    }
    arrays = {k: _np.ascontiguousarray(v) for k, v in arrays.items()}
    nc = _bacc.Bacc("TRN2", target_bir_lowering=False, num_devices=1)
    args = [nc.dram_tensor(k, v.shape, _mybir.dt.from_np(v.dtype), kind="ExternalInput").ap()
            for k, v in arrays.items()]
    out = nc.dram_tensor("out", a["x"].shape, F32, kind="ExternalOutput").ap()
    build(nc, *args, out)
    r = _run(nc, [arrays], core_ids=[0])
    return r.results[0]["out"]
```
